# Optimizing a Trainium2 kernel written in Bass

```python
import numpy as np
import jax
import jax.numpy as jnp

def _softmax(x, axis=-1):
    return jax.nn.softmax(x, axis=axis)

def _gelu(x):
    return jax.nn.gelu(x, approximate=True)

def _silu(x):
    return jax.nn.silu(x)

def _sigmoid(x):
    return jax.nn.sigmoid(x)

def _layernorm(x, axis=-1, eps=1e-05):
    m = jnp.mean(x, axis=axis, keepdims=True)
    v = jnp.var(x, axis=axis, keepdims=True)
    return (x - m) / jnp.sqrt(v + eps)

def _scatter_add(tgt, idx, src, axis=0):
    return tgt.at[idx].add(src)

def _segment_sum(src, seg, n):
    return jax.ops.segment_sum(src, seg, n)
kernel_name = 'mk_adaln_d2_jaxref_r8_129c7a'

def setup_inputs(seed: int=0):
    np.random.seed(seed)
    _w = jnp.asarray

    def _L0_attn_setup():
        import jax, jax.numpy as jnp
        import numpy as np
        BATCH, SEQ, D_MODEL, D_STATE, TIMESCALE = (4, 256, 128, 64, 2)
        EPS = 1e-06

        def _reference_tuple_inner(x, w_in, b_in, A, Bm, Cm, Dv, w_out, b_out, g_norm):
            B, L, D = x.shape
            S = A.shape[1]
            ts = TIMESCALE
            x_sub = x[:, ::ts] if ts > 1 else x
            x_sub = x_sub * jax.lax.rsqrt(jnp.mean(jnp.square(x_sub), axis=-1, keepdims=True) + EPS) * g_norm
            xz = jnp.einsum('bld,ed->ble', x_sub, w_in) + b_in
            x_proj, gate = jnp.split(xz, 2, axis=-1)
            c_sum = Cm.sum(axis=0)
            h0 = jnp.zeros((B, D, S), dtype=x.dtype)

            def step(h, xt):
                h = jnp.tanh(h * A + xt[:, :, None] * Bm)
                y = h @ c_sum + Dv * xt
                return (h, y)
            h_last, ys = jax.lax.scan(step, h0, jnp.swapaxes(x_proj, 0, 1))
            out = jnp.swapaxes(ys, 0, 1)
            out = out * jax.nn.silu(gate)
            out = jnp.einsum('bld,ed->ble', out, w_out) + b_out
            if ts > 1:
                out = jnp.repeat(out, ts, axis=1)[:, :L]
            return (out, h_last)
        key = jax.random.key(seed)
        ks = jax.random.split(key, 6)
        D, S = (D_MODEL, D_STATE)
        return {'x': jax.random.normal(ks[0], (BATCH, SEQ, D), dtype=jnp.float32), 'w_in': jax.random.normal(ks[1], (2 * D, D), dtype=jnp.float32) * 0.02, 'b_in': jnp.zeros((2 * D,), dtype=jnp.float32), 'A': jax.random.normal(ks[2], (D, S), dtype=jnp.float32) * 0.01, 'Bm': jax.random.normal(ks[3], (D, S), dtype=jnp.float32) * 0.01, 'Cm': jax.random.normal(ks[4], (D, S), dtype=jnp.float32) * 0.01, 'Dv': jnp.ones((D,), dtype=jnp.float32), 'w_out': jax.random.normal(ks[5], (D, D), dtype=jnp.float32) * 0.02, 'b_out': jnp.zeros((D,), dtype=jnp.float32), 'g_norm': jnp.ones((D,), dtype=jnp.float32)}
    _L0_attn_in = _L0_attn_setup()

    def _L0_ffn_setup():
        import jax, jax.numpy as jnp
        import numpy as np
        NUM_TRUE = 8
        NUM_NULL = 2
        NUM_EXPERTS = NUM_TRUE + NUM_NULL
        TOP_K = 2
        key = jax.random.key(seed)
        k0, k1, k2 = jax.random.split(key, 3)
        B, S, D = (4, 256, 128)
        inputs = jax.random.normal(k0, (B, S, D), dtype=jnp.float32)
        gate_w = jax.random.normal(k1, (NUM_EXPERTS, D), dtype=jnp.float32) * 0.02
        gate_b = jnp.zeros((NUM_EXPERTS,), dtype=jnp.float32)
        expert_w = jax.random.normal(k2, (NUM_TRUE, D, D), dtype=jnp.float32) * 0.02
        expert_b = jnp.zeros((NUM_TRUE, D), dtype=jnp.float32)
        return {'inputs': inputs, 'gate_w': gate_w, 'gate_b': gate_b, 'expert_w': expert_w, 'expert_b': expert_b}
    _L0_ffn_in = _L0_ffn_setup()
    _L0_c = _w((lambda *s: np.random.randn(*s).astype(np.float32) * 0.05)(8, 128))
    _L0_wmod = _w((lambda *s: np.random.randn(*s).astype(np.float32) * 0.05)(128, 6 * 128) * 128 ** (-0.5))

    def _L1_attn_setup():
        import jax, jax.numpy as jnp
        import numpy as np
        B, S, E, H = (4, 128, 128, 16)
        HD = E // H
        MAX_SEQ = 625
        key = jax.random.key(seed)
        ks = jax.random.split(key, 10)

        def lin(kw, kb):
            w = jax.random.normal(kw, (E, E), dtype=jnp.float32) * (1.0 / np.sqrt(E))
            b = jax.random.normal(kb, (E,), dtype=jnp.float32) * 0.01
            return (w, b)
        wq, bq = lin(ks[0], ks[1])
        wk, bk = lin(ks[2], ks[3])
        wv, bv = lin(ks[4], ks[5])
        wo, bo = lin(ks[6], ks[7])
        rpe_table = jax.random.normal(ks[8], (H, 2 * MAX_SEQ - 1, HD), dtype=jnp.float32) * 0.02
        x = jax.random.normal(ks[9], (B, S, E), dtype=jnp.float32)
        return {'x': x, 'wq': wq, 'bq': bq, 'wk': wk, 'bk': bk, 'wv': wv, 'bv': bv, 'wo': wo, 'bo': bo, 'rpe_table': rpe_table}
    _L1_attn_in = _L1_attn_setup()

    def _L1_ffn_setup():
        import jax, jax.numpy as jnp
        import numpy as np
        E = 8
        TOP_K = 2
        ROUTE_SCALE = 1.0
        ALPHA = 1.702
        LIMIT = 7.0
        D = 128
        F = 128
        B, S = (2, 128)

        def swiglu(h):
            g = jnp.minimum(h[..., ::2], LIMIT)
            l = jnp.clip(h[..., 1::2], -LIMIT, LIMIT)
            return g * jax.nn.sigmoid(ALPHA * g) * (l + 1.0)
        if __name__ == '__main__':
            out = reference(**setup_inputs())
            print(out.shape, out.dtype)
        key = jax.random.key(seed)
        ks = jax.random.split(key, 16)
        sd = 1.0 / np.sqrt(D)
        sf = 1.0 / np.sqrt(F)
        return {'x': jax.random.normal(ks[0], (B, S, D), jnp.float32), 'gate_w': jax.random.normal(ks[1], (E, D), jnp.float32) * sd, 'gate_b': jax.random.normal(ks[2], (E,), jnp.float32) * 0.01, 'w1': jax.random.normal(ks[3], (E, 2 * F, D), jnp.float32) * sd, 'b1': jax.random.normal(ks[4], (E, 2 * F), jnp.float32) * 0.01, 'w3': jax.random.normal(ks[5], (E, 2 * F, D), jnp.float32) * sd, 'b3': jax.random.normal(ks[6], (E, 2 * F), jnp.float32) * 0.01, 'w2': jax.random.normal(ks[7], (E, D, F), jnp.float32) * sf, 'b2': jax.random.normal(ks[8], (E, D), jnp.float32) * 0.01, 'sw1': jax.random.normal(ks[9], (2 * F, D), jnp.float32) * sd, 'sb1': jax.random.normal(ks[10], (2 * F,), jnp.float32) * 0.01, 'sw3': jax.random.normal(ks[11], (2 * F, D), jnp.float32) * sd, 'sb3': jax.random.normal(ks[12], (2 * F,), jnp.float32) * 0.01, 'sw2': jax.random.normal(ks[13], (D, F), jnp.float32) * sf, 'sb2': jax.random.normal(ks[14], (D,), jnp.float32) * 0.01}
    _L1_ffn_in = _L1_ffn_setup()
    _L1_c = _w((lambda *s: np.random.randn(*s).astype(np.float32) * 0.05)(8, 128))
    _L1_wmod = _w((lambda *s: np.random.randn(*s).astype(np.float32) * 0.05)(128, 6 * 128) * 128 ** (-0.5))
    _d = {'L0_attn_x': _L0_attn_in['x'], 'L0_attn_w_in': _L0_attn_in['w_in'], 'L0_attn_b_in': _L0_attn_in['b_in'], 'L0_attn_A': _L0_attn_in['A'], 'L0_attn_Bm': _L0_attn_in['Bm'], 'L0_attn_Cm': _L0_attn_in['Cm'], 'L0_attn_Dv': _L0_attn_in['Dv'], 'L0_attn_w_out': _L0_attn_in['w_out'], 'L0_attn_b_out': _L0_attn_in['b_out'], 'L0_attn_g_norm': _L0_attn_in['g_norm'], 'L0_ffn_gate_w': _L0_ffn_in['gate_w'], 'L0_ffn_gate_b': _L0_ffn_in['gate_b'], 'L0_ffn_expert_w': _L0_ffn_in['expert_w'], 'L0_ffn_expert_b': _L0_ffn_in['expert_b'], 'L0_c': _L0_c, 'L0_wmod': _L0_wmod, 'L1_attn_wq': _L1_attn_in['wq'], 'L1_attn_bq': _L1_attn_in['bq'], 'L1_attn_wk': _L1_attn_in['wk'], 'L1_attn_bk': _L1_attn_in['bk'], 'L1_attn_wv': _L1_attn_in['wv'], 'L1_attn_bv': _L1_attn_in['bv'], 'L1_attn_wo': _L1_attn_in['wo'], 'L1_attn_bo': _L1_attn_in['bo'], 'L1_attn_rpe_table': _L1_attn_in['rpe_table'], 'L1_ffn_gate_w': _L1_ffn_in['gate_w'], 'L1_ffn_gate_b': _L1_ffn_in['gate_b'], 'L1_ffn_w1': _L1_ffn_in['w1'], 'L1_ffn_b1': _L1_ffn_in['b1'], 'L1_ffn_w3': _L1_ffn_in['w3'], 'L1_ffn_b3': _L1_ffn_in['b3'], 'L1_ffn_w2': _L1_ffn_in['w2'], 'L1_ffn_b2': _L1_ffn_in['b2'], 'L1_ffn_sw1': _L1_ffn_in['sw1'], 'L1_ffn_sb1': _L1_ffn_in['sb1'], 'L1_ffn_sw3': _L1_ffn_in['sw3'], 'L1_ffn_sb3': _L1_ffn_in['sb3'], 'L1_ffn_sw2': _L1_ffn_in['sw2'], 'L1_ffn_sb2': _L1_ffn_in['sb2'], 'L1_c': _L1_c, 'L1_wmod': _L1_wmod}
    _x0 = _d['L0_attn_x']
    _d['L0_attn_x'] = jax.random.normal(jax.random.fold_in(jax.random.key(seed), 1), (8, 512, 128), dtype=_x0.dtype)
    del _x0
    return _d

def reference(L0_attn_x, L0_attn_w_in, L0_attn_b_in, L0_attn_A, L0_attn_Bm, L0_attn_Cm, L0_attn_Dv, L0_attn_w_out, L0_attn_b_out, L0_attn_g_norm, L0_ffn_gate_w, L0_ffn_gate_b, L0_ffn_expert_w, L0_ffn_expert_b, L0_c, L0_wmod, L1_attn_wq, L1_attn_bq, L1_attn_wk, L1_attn_bk, L1_attn_wv, L1_attn_bv, L1_attn_wo, L1_attn_bo, L1_attn_rpe_table, L1_ffn_gate_w, L1_ffn_gate_b, L1_ffn_w1, L1_ffn_b1, L1_ffn_w3, L1_ffn_b3, L1_ffn_w2, L1_ffn_b2, L1_ffn_sw1, L1_ffn_sb1, L1_ffn_sw3, L1_ffn_sb3, L1_ffn_sw2, L1_ffn_sb2, L1_c, L1_wmod):

    def _L0_attn_ref(x, w_in, b_in, A, Bm, Cm, Dv, w_out, b_out, g_norm):
        import jax, jax.numpy as jnp
        import numpy as np
        BATCH, SEQ, D_MODEL, D_STATE, TIMESCALE = (4, 256, 128, 64, 2)
        EPS = 1e-06

        def _reference_tuple_inner(x, w_in, b_in, A, Bm, Cm, Dv, w_out, b_out, g_norm):
            B, L, D = x.shape
            S = A.shape[1]
            ts = TIMESCALE
            x_sub = x[:, ::ts] if ts > 1 else x
            x_sub = x_sub * jax.lax.rsqrt(jnp.mean(jnp.square(x_sub), axis=-1, keepdims=True) + EPS) * g_norm
            xz = jnp.einsum('bld,ed->ble', x_sub, w_in) + b_in
            x_proj, gate = jnp.split(xz, 2, axis=-1)
            c_sum = Cm.sum(axis=0)
            h0 = jnp.zeros((B, D, S), dtype=x.dtype)

            def step(h, xt):
                h = jnp.tanh(h * A + xt[:, :, None] * Bm)
                y = h @ c_sum + Dv * xt
                return (h, y)
            h_last, ys = jax.lax.scan(step, h0, jnp.swapaxes(x_proj, 0, 1))
            out = jnp.swapaxes(ys, 0, 1)
            out = out * jax.nn.silu(gate)
            out = jnp.einsum('bld,ed->ble', out, w_out) + b_out
            if ts > 1:
                out = jnp.repeat(out, ts, axis=1)[:, :L]
            return (out, h_last)
        return _reference_tuple_inner(x, w_in, b_in, A, Bm, Cm, Dv, w_out, b_out, g_norm)[0]

    def _L0_ffn_ref(inputs, gate_w, gate_b, expert_w, expert_b):
        import jax, jax.numpy as jnp
        import numpy as np
        NUM_TRUE = 8
        NUM_NULL = 2
        NUM_EXPERTS = NUM_TRUE + NUM_NULL
        TOP_K = 2
        D = inputs.shape[-1]
        x = inputs.reshape(-1, D)
        gate_logits = x @ gate_w.T + gate_b
        gate_probs = jax.nn.softmax(gate_logits, axis=-1)
        weights, selected = jax.lax.top_k(gate_probs, TOP_K)
        true_mask = selected < NUM_TRUE
        true_weights = weights * true_mask
        denom = true_weights.sum(axis=-1, keepdims=True)
        denom = jnp.where(denom > 0, denom, jnp.ones_like(denom))
        norm_w = (true_weights / denom).astype(x.dtype)
        one_hot = jax.nn.one_hot(selected, NUM_EXPERTS, dtype=norm_w.dtype)
        combine_w = jnp.einsum('tk,tke->te', norm_w, one_hot)[:, :NUM_TRUE]
        expert_out = jnp.einsum('td,edh->teh', x, expert_w) + expert_b[None, :, :]
        out = jnp.einsum('te,teh->th', combine_w, expert_out)
        return out.reshape(inputs.shape[:-1] + (out.shape[-1],))

    def _L1_attn_ref(x, wq, bq, wk, bk, wv, bv, wo, bo, rpe_table):
        import jax, jax.numpy as jnp
        import numpy as np
        B, S, E, H = (4, 128, 128, 16)
        HD = E // H
        MAX_SEQ = 625
        b, s, e = x.shape
        scale = 1.0 / np.sqrt(HD)
        q = (x @ wq.T + bq).reshape(b, s, H, HD).transpose(0, 2, 1, 3)
        k = (x @ wk.T + bk).reshape(b, s, H, HD).transpose(0, 2, 1, 3)
        v = (x @ wv.T + bv).reshape(b, s, H, HD).transpose(0, 2, 1, 3)
        scores = jnp.einsum('bhqd,bhkd->bhqk', q, k) * scale
        table = rpe_table[:, :2 * s - 1]
        rel = jnp.einsum('bhqd,hrd->bhqr', q, table)
        idx = jnp.arange(s)[:, None] - jnp.arange(s)[None, :] + (s - 1)
        rpe_scores = jnp.take_along_axis(rel, jnp.broadcast_to(idx[None, None], (b, H, s, s)), axis=-1)
        attn = jax.nn.softmax(scores + rpe_scores, axis=-1)
        ctx = jnp.einsum('bhqk,bhkd->bhqd', attn, v)
        ctx = ctx.transpose(0, 2, 1, 3).reshape(b, s, e)
        return ctx @ wo.T + bo

    def _L1_ffn_ref(x, gate_w, gate_b, w1, b1, w3, b3, w2, b2, sw1, sb1, sw3, sb3, sw2, sb2):
        import jax, jax.numpy as jnp
        import numpy as np
        E = 8
        TOP_K = 2
        ROUTE_SCALE = 1.0
        ALPHA = 1.702
        LIMIT = 7.0
        D = 128
        F = 128
        B, S = (2, 128)

        def swiglu(h):
            g = jnp.minimum(h[..., ::2], LIMIT)
            l = jnp.clip(h[..., 1::2], -LIMIT, LIMIT)
            return g * jax.nn.sigmoid(ALPHA * g) * (l + 1.0)
        if __name__ == '__main__':
            out = reference(**setup_inputs())
            print(out.shape, out.dtype)
        inp_shape = x.shape
        xt = x.reshape(-1, D)
        logits = xt @ gate_w.T
        scores = jax.nn.softmax(logits.astype(jnp.float32), axis=-1)
        biased = scores + gate_b.astype(jnp.float32)
        idx = jax.lax.top_k(biased, TOP_K)[1]
        weights = (jnp.take_along_axis(scores, idx, axis=-1) * ROUTE_SCALE).astype(x.dtype)
        cw = jnp.sum(jax.nn.one_hot(idx, E, dtype=x.dtype) * weights[..., None], axis=1)
        h1 = jnp.einsum('td,efd->etf', xt, w1) + b1[:, None, :]
        h3 = jnp.einsum('td,efd->etf', xt, w3) + b3[:, None, :]
        a = swiglu(h1 * h3)
        y = jnp.einsum('etf,edf->etd', a, w2) + b2[:, None, :]
        routed = jnp.einsum('te,etd->td', cw, y)
        sh = swiglu((xt @ sw1.T + sb1) * (xt @ sw3.T + sb3))
        shared = sh @ sw2.T + sb2
        return (routed + shared).reshape(inp_shape)
    x = L0_attn_x
    mod = (_silu(L0_c) @ L0_wmod).reshape(L0_c.shape[0], 6, 1, -1)
    sa, ca, ga, sb, cb, gb = (mod[:, 0], mod[:, 1], mod[:, 2], mod[:, 3], mod[:, 4], mod[:, 5])
    ga = (2 * (ga >= 0) - 1) * jnp.maximum(jnp.abs(ga), 0.25)
    gb = (2 * (gb >= 0) - 1) * jnp.maximum(jnp.abs(gb), 0.25)
    h = _layernorm(x, axis=-1) * (1 + ca) + sa
    x = x + ga * _L0_attn_ref(h, L0_attn_w_in, L0_attn_b_in, L0_attn_A, L0_attn_Bm, L0_attn_Cm, L0_attn_Dv, L0_attn_w_out, L0_attn_b_out, L0_attn_g_norm)
    h = _layernorm(x, axis=-1) * (1 + cb) + sb
    x = x + gb * _L0_ffn_ref(h, L0_ffn_gate_w, L0_ffn_gate_b, L0_ffn_expert_w, L0_ffn_expert_b)
    mod = (_silu(L1_c) @ L1_wmod).reshape(L1_c.shape[0], 6, 1, -1)
    sa, ca, ga, sb, cb, gb = (mod[:, 0], mod[:, 1], mod[:, 2], mod[:, 3], mod[:, 4], mod[:, 5])
    ga = (2 * (ga >= 0) - 1) * jnp.maximum(jnp.abs(ga), 0.25)
    gb = (2 * (gb >= 0) - 1) * jnp.maximum(jnp.abs(gb), 0.25)
    h = _layernorm(x, axis=-1) * (1 + ca) + sa
    x = x + ga * _L1_attn_ref(h, L1_attn_wq, L1_attn_bq, L1_attn_wk, L1_attn_bk, L1_attn_wv, L1_attn_bv, L1_attn_wo, L1_attn_bo, L1_attn_rpe_table)
    h = _layernorm(x, axis=-1) * (1 + cb) + sb
    x = x + gb * _L1_ffn_ref(h, L1_ffn_gate_w, L1_ffn_gate_b, L1_ffn_w1, L1_ffn_b1, L1_ffn_w3, L1_ffn_b3, L1_ffn_w2, L1_ffn_b2, L1_ffn_sw1, L1_ffn_sb1, L1_ffn_sw3, L1_ffn_sb3, L1_ffn_sw2, L1_ffn_sb2)
    return x

_drawn_inputs = setup_inputs


def setup_inputs(seed=0):
    import zlib

    import numpy as np

    out = dict(_drawn_inputs(seed))
    spreads = {'L0_attn_b_in': (0.0, 0.8),
     'L0_attn_Dv': (1.0, 0.6),
     'L0_attn_b_out': (0.0, 1.168),
     'L0_attn_g_norm': (1.0, 0.6),
     'L0_ffn_gate_b': (0.0, 0.452),
     'L0_ffn_expert_b': (0.0, 1.486)}
    factors = {'L0_attn_w_in': 8.0,
     'L0_attn_A': 21.345,
     'L0_attn_Bm': 8.0,
     'L0_attn_Cm': 8.0,
     'L0_attn_w_out': 8.0,
     'L1_attn_bq': 64.0,
     'L1_attn_bk': 200.0,
     'L1_attn_bv': 64.0,
     'L1_attn_bo': 64.0,
     'L1_attn_rpe_table': 64.0,
     'L1_ffn_gate_b': 39.331,
     'L1_ffn_b1': 196.099,
     'L1_ffn_b3': 190.31,
     'L1_ffn_b2': 200.0,
     'L1_ffn_sb1': 64.0,
     'L1_ffn_sb3': 64.0,
     'L1_ffn_sb2': 64.0,
     'L0_ffn_gate_w': 2.844,
     'L0_ffn_expert_w': 4.54,
     'L1_attn_wq': 4.525,
     'L1_attn_wk': 4.467,
     'L1_attn_wv': 2.995,
     'L1_attn_wo': 2.865}
    for name, (base, spread) in spreads.items():
        noise = np.random.default_rng([zlib.crc32(name.encode()), seed]).standard_normal(out[name].shape)
        drawn = base * np.exp(spread * noise) if base else spread * noise
        out[name] = jnp.asarray(drawn.astype(out[name].dtype))
    for name, factor in factors.items():
        out[name] = (out[name] * factor).astype(out[name].dtype)
    return out
```

```python
import concourse.bass as bass
from concourse import mybir
from contextlib import ExitStack

F32 = mybir.dt.float32
BF16 = mybir.dt.bfloat16
ALU = mybir.AluOpType
ACT = mybir.ActivationFunctionType
AX = mybir.AxisListType

P = 128
NB = 8
SEQ = 512
U = P // NB
NT = NB * SEQ // P
NC = NT // 2
BLK = 512
NBLK = NB * SEQ // BLK
TPB = BLK // P
NS = 64
HALF = NS // 2 * NB
HEADS = 16
HD = P // HEADS
NE0, NX0 = 8, 10
NE1 = 8
MODS = 6
LN_EPS, RMS_EPS = 1e-5, 1e-6
TLEN = 2 * SEQ - 1
LIMIT = 7.0
LOWEST = -3.4028234e38
ALPHA = 1.702


class Chain:

    def __init__(self, eng, sem):
        self.eng, self.sem, self.n = eng, sem, 0

    def add(self, ins):
        self.n += 1
        ins.then_inc(self.sem, 1)

    def wait(self):
        self.eng.wait_ge(self.sem, self.n)

    def __call__(self, ins):
        self.add(ins)
        self.wait()


class Roots:

    def __init__(self, asked, answered):
        self.asked, self.answered, self.n, self.served = asked, answered, 0, 0

    def rsqrt(self, dve, v, chain, val, root, tmp):
        self.n += 1
        v.tensor_scalar(tmp, val, 1.0, None, ALU.mult).then_inc(self.asked, 1)
        dve.wait_ge(self.answered, self.n)
        chain(v.reciprocal(root, root))
        chain(v.tensor_tensor(tmp, root, root, ALU.mult))
        chain(v.tensor_tensor(tmp, tmp, val, ALU.mult))
        chain(v.tensor_scalar(tmp, tmp, -0.5, 1.5, ALU.mult, ALU.add))
        chain(v.tensor_tensor(root, root, tmp, ALU.mult))

    def serve(self, act, nc, root, tmp):
        self.served += 1
        act.wait_ge(self.asked, self.served)
        nc.scalar.activation(root, tmp, ACT.Sqrt).then_inc(self.answered, 1)


def layer_norm(dve, v, chain, roots, src, out, n, stats, mv, rstd, tmp, scale, shift):
    for k in range(n):
        chain.add(v.bn_stats(stats[:, k, :], src[:, k, :]))
    chain.wait()
    for k in range(n):
        chain.add(v.bn_aggr(mv[:, k, :], stats[:, k, :]))
    chain.wait()
    chain(v.tensor_scalar(mv[:, 0:n, 1], mv[:, 0:n, 1], LN_EPS, None, ALU.add))
    roots.rsqrt(dve, v, chain, mv[:, 0:n, 1], rstd[:, 0:n], tmp[:, 0:n])
    for k in range(n):
        chain.add(v.tensor_scalar(out[:, k, :], src[:, k, :], mv[:, k, 0:1], rstd[:, k:k + 1],
                                  ALU.subtract, ALU.mult))
    chain.wait()
    chain(v.tensor_tensor(out[:, 0:n, :], out[:, 0:n, :], scale.unsqueeze(1).to_broadcast([P, n, P]), ALU.mult))
    chain(v.tensor_tensor(out[:, 0:n, :], out[:, 0:n, :], shift.unsqueeze(1).to_broadcast([P, n, P]), ALU.add))


def prologue(nc, d, keep, scan):
    x, mod, ident, ones = keep["x"], keep["mod"], keep["ident"], keep["ones"]
    with ExitStack() as ctx:
        sb = lambda name, shape, dt=F32: ctx.enter_context(nc.sbuf_tensor(name, shape, dt))
        sem = lambda name: ctx.enter_context(nc.semaphore(name))
        cT = sb("cT", [P, 2, NB])
        cth = sb("cth", [P, 2, NB])
        crep = sb("crep", [P, 2, U, NB])
        wmod = sb("wmod", [P, 2, MODS * P])
        guard = sb("guard", [P, 2, P])
        winT = sb("winT", [P, 2 * P])
        binc = sb("binc", [P, 2])
        binh = sb("binh", [P, 1])
        gn = sb("gn", [P, 1])
        cm = sb("cm", [P, NS])
        am = sb("am", [P, NS])
        csum = sb("csum", [P, NS])
        h = sb("h0", [P, NC, P])
        hT = sb("h0T", [P, NC * P])
        sq = sb("sq", [P, NC, P])
        stats = sb("stats0", [P, NC, 6])
        mv = sb("mv0", [P, NC, 2])
        rstd = sb("rstd0", [P, NC])
        rtmp = sb("rtmp0", [P, NC])
        ms = sb("ms", [P, NC])
        gate = sb("gate", [P, 2, BLK])
        gth = sb("gth", [P, 2, BLK])
        pm = [ctx.enter_context(nc.psum_tensor(f"pm{i}", [P, 512], F32)) for i in range(8)]
        x_in, w_in, zero, id_ready, v_chain = sem("x_in"), sem("w_in"), sem("zero"), sem("id_ready"), sem("v_chain0")
        c_tanh, c_rep, mod_ps, mod_sb = sem("c_tanh"), sem("c_rep"), sem("mod_ps"), sem("mod_sb")
        h_ready, hT_ps, hT_sb, proj_ps = sem("h_ready"), sem("hT_ps"), sem("hT_sb"), sem("proj_ps")
        proj_sb, gate_sb, gate_used, csum_ps = sem("proj_sb"), sem("gate_sb"), sem("gate_used"), sem("csum_ps")
        w_scaled = sem("w_scaled")
        roots = Roots(sem("var_ready0"), sem("root_ready0"))
        NBK = NC * P // BLK
        block = ctx.enter_context(nc.Block())

        @block.sync
        def _(sp):
            sp.dma_start(cT[:, :, :], d["cT"]).then_inc(w_in, 16)
            sp.dma_start(wmod[:, :, :], d["wmod"]).then_inc(w_in, 16)
            sp.dma_start(x[:, :, :], d["x"]).then_inc(x_in, 16)
            for dst, src in ((winT[:, :], d["w_inT"]), (binc[:, :], d["b_in"]), (gn[:, :], d["g_norm"]),
                             (cm[:, :], d["Cm"]), (am[:, :], d["A"]), (scan["Bm"][:, :], d["Bm"]),
                             (scan["Dv"][:, :], d["Dv"]), (scan["woT"][:, :], d["w_outT"]),
                             (scan["bo"][:, :], d["b_out"])):
                sp.dma_start(dst, src).then_inc(w_in, 16)

        ALL_W = 16 * 11

        @block.gpsimd
        def _(pool):
            nc.gpsimd.memset(ident[:, :], 0.0).then_inc(zero, 1)
            nc.gpsimd.memset(ones[:, :], 1.0).then_inc(id_ready, 1)
            pool.wait_ge(zero, 1)
            nc.gpsimd.affine_select(out=ident[:, :], in_=ident[:, :], compare_op=ALU.not_equal, fill=1.0,
                                    base=0, pattern=[[-1, P]], channel_multiplier=1).then_inc(id_ready, 1)

        @block.scalar
        def _(act):
            act.wait_ge(w_in, ALL_W)
            nc.scalar.activation(cth[:, :, :], cT[:, :, :], ACT.Tanh, scale=0.5).then_inc(c_tanh, 1)
            for n, (lo, hi) in enumerate(((0, 512), (512, 768)) * 2):
                act.wait_ge(mod_ps, n + 1)
                nc.scalar.copy(mod[:, n // 2, lo:hi], pm[n][:, 0:hi - lo]).then_inc(mod_sb, 1)
            roots.serve(act, nc, rstd[:, :], rtmp[:, :])
            roots.serve(act, nc, rstd[:, :], rtmp[:, :])
            for j in range(NBK):
                act.wait_ge(hT_ps, j + 1)
                nc.scalar.copy(hT[:, j * BLK:(j + 1) * BLK], pm[4 + j % 2][:, :]).then_inc(hT_sb, 1)
            for j in range(NBK):
                act.wait_ge(proj_ps, 2 * j + 1)
                nc.scalar.activation(scan["xp"][:, j * BLK:(j + 1) * BLK], pm[2 * (j % 2)][:, :], ACT.Identity,
                                     bias=binc[:, 0:1]).then_inc(proj_sb, 1)
                act.wait_ge(proj_ps, 2 * j + 2)
                if j >= 2:
                    act.wait_ge(gate_used, j - 1)
                nc.scalar.activation(gate[:, j % 2, :], pm[2 * (j % 2) + 1][:, :], ACT.Identity,
                                     bias=binc[:, 1:2]).then_inc(proj_sb, 1)
                act.wait_ge(w_scaled, 1)
                nc.scalar.activation(gth[:, j % 2, :], pm[2 * (j % 2) + 1][:, :], ACT.Tanh,
                                     bias=binh[:, 0:1], scale=0.5).then_inc(gate_sb, 1)

        @block.vector
        def _(dve):
            v = nc.vector
            chain = Chain(dve, v_chain)
            dve.wait_ge(c_tanh, 1)
            chain(v.scalar_tensor_tensor(cth[:, :, :], cth[:, :, :], 1.0, cT[:, :, :], ALU.add, ALU.mult))
            for l in range(2):
                v.tensor_scalar(crep[:, l, :, :], cth[:, l, :].unsqueeze(1).to_broadcast([P, U, NB]), 0.5, None,
                                ALU.mult).then_inc(c_rep, 1)
            chain(v.tensor_scalar(winT[:, :], winT[:, :], gn[:, 0:1], None, ALU.mult))
            chain(v.tensor_scalar(scan["woT"][:, :], scan["woT"][:, :], 0.5, None, ALU.mult))
            v.tensor_scalar(binh[:, :], binc[:, 1:2], 0.5, None, ALU.mult).then_inc(w_scaled, 1)
            chain(v.tensor_copy(scan["A"][:, :].rearrange("p (s b) -> p s b", b=NB),
                                am[:, :].unsqueeze(2).to_broadcast([P, NS, NB])))
            dve.wait_ge(csum_ps, 1)
            chain(v.tensor_copy(csum[:, :], pm[7][:, 0:NS]))
            dve.wait_ge(id_ready, 2)
            chain(v.tensor_tensor(scan["diagC"][:, :, :], ident[:, :].unsqueeze(1).to_broadcast([P, NS, P]),
                                  csum[:, :].unsqueeze(2).to_broadcast([P, NS, P]), ALU.mult))
            chain(v.memset(scan["hist"][:, 1, U - 1, :], 0.0))
            dve.wait_ge(mod_sb, 4)
            for l in range(2):
                for m in (1, 4):
                    chain(v.tensor_scalar(mod[:, l, m * P:(m + 1) * P], mod[:, l, m * P:(m + 1) * P], 1.0, None,
                                          ALU.add))
                for m in (2, 5):
                    g = mod[:, l, m * P:(m + 1) * P]
                    chain(v.tensor_scalar(guard[:, 0, :], g, 0.0, 2.0, ALU.is_ge, ALU.mult))
                    chain(v.scalar_tensor_tensor(guard[:, 1, :], g, -1.0, g, ALU.mult, ALU.max))
                    chain(v.tensor_scalar(guard[:, 1, :], guard[:, 1, :], 0.25, None, ALU.max))
                    chain(v.scalar_tensor_tensor(g, guard[:, 0, :], -1.0, guard[:, 1, :], ALU.add, ALU.mult))
            dve.wait_ge(x_in, 16)
            layer_norm(dve, v, chain, roots, x[:, :, :].rearrange("p (c o) e -> p c o e", o=2)[:, :, 0, :], h, NC,
                       stats, mv, rstd, rtmp, mod[:, 0, P:2 * P], mod[:, 0, 0:P])
            chain(v.tensor_tensor(sq[:, :, :], h[:, :, :], h[:, :, :], ALU.mult))
            chain(v.tensor_reduce(ms[:, :], sq[:, :, :], AX.X, ALU.add))
            chain(v.tensor_scalar(ms[:, :], ms[:, :], 1.0 / P, RMS_EPS, ALU.mult, ALU.add))
            roots.rsqrt(dve, v, chain, ms[:, :], rstd[:, :], rtmp[:, :])
            v.tensor_tensor(h[:, :, :], h[:, :, :], rstd[:, :].unsqueeze(2).to_broadcast([P, NC, P]),
                            ALU.mult).then_inc(h_ready, 1)
            for j in range(NBK):
                dve.wait_ge(gate_sb, j + 1)
                v.scalar_tensor_tensor(scan["gate"][:, j * BLK:(j + 1) * BLK], gth[:, j % 2, :], 1.0,
                                       gate[:, j % 2, :], ALU.add, ALU.mult).then_inc(gate_used, 1)

        @block.tensor
        def _(pe):
            mm = nc.tensor.matmul
            pe.wait_ge(w_in, ALL_W)
            pe.wait_ge(id_ready, 2)
            mm(pm[7][:, 0:NS], ones[:, :], cm[:, :], start=True, stop=True).then_inc(csum_ps, 1)
            pe.wait_ge(c_rep, 2)
            for n, (lo, hi) in enumerate(((0, 512), (512, 768)) * 2):
                mm(pm[n][:, 0:hi - lo], crep[:, n // 2, :, :].rearrange("p u b -> p (u b)"),
                   wmod[:, n // 2, lo:hi], start=True, stop=True).then_inc(mod_ps, 1)
            pe.wait_ge(h_ready, 1)
            for j in range(NBK):
                if j >= 2:
                    pe.wait_ge(hT_sb, j - 1)
                for q in range(TPB):
                    last = nc.tensor.transpose(pm[4 + j % 2][:, q * P:(q + 1) * P], h[:, j * TPB + q, :], ident[:, :])
                last.then_inc(hT_ps, 1)
            for j in range(NBK):
                pe.wait_ge(hT_sb, j + 1)
                for half in range(2):
                    if j == 0:
                        pe.wait_ge(mod_sb, 4)
                    if j >= 2:
                        pe.wait_ge(proj_sb, 2 * (j - 2) + half + 1)
                        pe.wait_ge(gate_sb, j - 1)
                    mm(pm[2 * (j % 2) + half][:, :], winT[:, half * P:(half + 1) * P], hT[:, j * BLK:(j + 1) * BLK],
                       start=True, stop=True).then_inc(proj_ps, 1)


def scan_phase(nc, d, keep, scan):
    x, mod, ones = keep["x"], keep["mod"], keep["ones"]
    A, Bm, Dv, xp, gate = scan["A"], scan["Bm"], scan["Dv"], scan["xp"], scan["gate"]
    hist, diagC, woT, bo = scan["hist"], scan["diagC"], scan["woT"], scan["bo"]
    S_ACT = 20
    with ExitStack() as ctx:
        sb = lambda name, shape, dt=F32: ctx.enter_context(nc.sbuf_tensor(name, shape, dt))
        sem = lambda name: ctx.enter_context(nc.semaphore(name))
        xb = sb("xb", [P, 2, U, NS * NB])
        xc = sb("xc", [P, 2, P])
        g = sb("g", [P, NS * NB])
        y2 = sb("y2", [P, P])
        yg = sb("yg", [P, P])
        upd = sb("upd", [P, P])
        zp = [ctx.enter_context(nc.psum_tensor(f"zp{i}", [P, 512], F32)) for i in range(2)]
        py = [ctx.enter_context(nc.psum_tensor(f"py{i}", [P, 512], F32)) for i in range(2)]
        po = ctx.enter_context(nc.psum_tensor("po", [P, 512], F32))
        decayed, z_ready, h_done = sem("decayed"), sem("z_ready"), sem("h_done")
        xb_act, xb_pool, xb_used = sem("xb_act"), sem("xb_pool"), sem("xb_used")
        xc_ready = sem("xc_ready")
        y_ready, yd_ready, yg_ready, out_ready, upd_ready, x_updated = (
            sem("y_ready"), sem("yd_ready"), sem("yg_ready"), sem("out_ready"), sem("upd_ready"), sem("x_updated"))
        block = ctx.enter_context(nc.Block())
        OUT_AT = 13
        N_POOL = NS - S_ACT

        def chunks(eng, body):
            body(0, 0, True)
            body(1, 1, False)
            with eng.Fori(1, NC // 2) as i:
                body(2 * i, 0, False)
                body(2 * i + 1, 1, False)

        def xb_slot(s, par):
            return xb[:, par, :, s * NB:(s + 1) * NB]

        def xp_chunk(c):
            return xp[:, bass.ds(c * P, P)] if not isinstance(c, int) else xp[:, c * P:(c + 1) * P]

        @block.vector
        def _(dve):
            v = nc.vector

            def output(c):
                dve.wait_ge(y_ready, c + 1)
                par = output.par
                xs = xp_chunk(c)
                v.scalar_tensor_tensor(y2[:, :], xs, Dv[:, 0:1], py[par][:, 0:P], ALU.mult, ALU.add)\
                 .then_inc(yd_ready, 1)
                dve.wait_ge(yd_ready, c + 1)
                gs = gate[:, bass.ds(c * P, P)] if not isinstance(c, int) else gate[:, c * P:(c + 1) * P]
                v.tensor_tensor(yg[:, :], y2[:, :], gs, ALU.mult).then_inc(yg_ready, 1)

            def add_output(c):
                dve.wait_ge(out_ready, c + 1)
                v.tensor_tensor(upd[:, :], po[:, 0:P], mod[:, 0, 2 * P:3 * P], ALU.mult).then_inc(upd_ready, 1)
                dve.wait_ge(upd_ready, c + 1)
                xs = x[:, bass.ds(2 * c, 2), :] if not isinstance(c, int) else x[:, 2 * c:2 * c + 2, :]
                v.tensor_tensor(xs, xs, upd[:, :].unsqueeze(1).to_broadcast([P, 2, P]), ALU.add)\
                 .then_inc(x_updated, 1)

            def body(c, par, first):
                dve.wait_ge(xb_act, S_ACT * (c + 1))
                dve.wait_ge(xb_pool, N_POOL * (c + 1))
                for u in range(U):
                    prev = hist[:, par, u - 1, :] if u else hist[:, 1 - par, U - 1, :]
                    step = c * U + u
                    for j in range(2):
                        lo, hi = j * HALF, (j + 1) * HALF
                        if not (first and u == 0):
                            dve.wait_ge(h_done, 2 * step + j - 1)
                        v.tensor_tensor(g[:, lo:hi], prev[:, lo:hi], A[:, lo:hi], ALU.mult).then_inc(decayed, 1)
                    for j in range(2):
                        lo, hi = j * HALF, (j + 1) * HALF
                        dve.wait_ge(decayed, 2 * step + j + 1)
                        ins = v.tensor_tensor(zp[j][:, 0:HALF], g[:, lo:hi], xb[:, par, u, lo:hi], ALU.add)
                        ins.then_inc(z_ready, 1)
                    if not first and u == OUT_AT:
                        output.par = 1 - par
                        output(c - 1)
                    if not first and u == U - 1:
                        add_output(c - 1)

            chunks(dve, body)
            output.par = 1
            output(NC - 1)
            add_output(NC - 1)
            dve.wait_ge(x_updated, NC)

        def make_xb(eng, op, states, c, par, ready):
            for s in states:
                op(xb_slot(s, par), xp_chunk(c).rearrange("p (u b) -> p u b", b=NB), Bm[:, s:s + 1]).then_inc(ready, 1)

        @block.scalar
        def _(act):
            def op(out, in_, scale):
                return nc.scalar.activation(out, in_, ACT.Copy, scale=scale)

            make_xb(act, op, range(S_ACT), 0, 0, xb_act)
            make_xb(act, op, range(S_ACT), 1, 1, xb_act)

            def body(c, par, first):
                made = 0
                for u in range(U):
                    step = c * U + u
                    if not first and u == 0:
                        pass
                    for j in range(2):
                        act.wait_ge(z_ready, 2 * step + j + 1)
                        if u == 0 and j == 0 and not (isinstance(c, int) and c < 2):
                            act.wait_ge(y_ready, c - 1)
                        nc.scalar.activation(hist[:, par, u, j * HALF:(j + 1) * HALF], zp[j][:, 0:HALF], ACT.Tanh)\
                          .then_inc(h_done, 1)
                    if not (isinstance(c, int) and c == 0):
                        upto = S_ACT * (u + 1) // U
                        make_next(c, par, range(made, upto), u)
                        made = upto

            def make_next(c, par, states, u):
                if u == 0:
                    act.wait_ge(z_ready, 2 * U * c)
                make_xb(act, op, states, c + 1, 1 - par, xb_act)

            body(0, 0, True)
            body(1, 1, False)
            with act.Fori(1, NC // 2 - 1) as i:
                body(2 * i, 0, False)
                body(2 * i + 1, 1, False)
            made_last = NC - 2
            body(made_last, 0, False)
            for u in range(U):
                for j in range(2):
                    step = (NC - 1) * U + u
                    act.wait_ge(z_ready, 2 * step + j + 1)
                    if u == 0 and j == 0:
                        act.wait_ge(y_ready, NC - 2)
                    nc.scalar.activation(hist[:, 1, u, j * HALF:(j + 1) * HALF], zp[j][:, 0:HALF], ACT.Tanh)\
                      .then_inc(h_done, 1)

        @block.gpsimd
        def _(pool):
            def chunk(c, par, slot_used):
                if slot_used:
                    pool.wait_ge(z_ready, 2 * U * (c - 1))
                nc.gpsimd.tensor_copy(xc[:, par, :], xp_chunk(c)).then_inc(xc_ready, 1)
                pool.wait_ge(xc_ready, c + 1)
                nc.gpsimd.tensor_tensor(xb_slot(S_ACT, par), xc[:, par, :].rearrange("p (u b) -> p u b", b=NB),
                                        Bm[:, S_ACT:S_ACT + 1].unsqueeze(1).to_broadcast([P, U, NB]), ALU.mult)\
                  .then_inc(xb_pool, 1)
                for s in range(S_ACT + 1, NS):
                    nc.gpsimd.tensor_scalar(xb_slot(s, par), xc[:, par, :].rearrange("p (u b) -> p u b", b=NB),
                                            Bm[:, s:s + 1], 1.0, ALU.mult, ALU.mult).then_inc(xb_pool, 1)

            chunk(0, 0, False)
            chunk(1, 1, False)
            with pool.Fori(1, NC // 2) as i:
                chunk(2 * i, 0, True)
                chunk(2 * i + 1, 1, True)

        @block.tensor
        def _(pe):
            mm = nc.tensor.matmul

            def body(c, par, first):
                pe.wait_ge(h_done, 2 * U * (c + 1))
                if not (isinstance(c, int) and c < 2):
                    pe.wait_ge(yd_ready, c - 1)
                for s in range(NS):
                    last = mm(py[par][:, 0:P], diagC[:, s, :], hist[:, par, :, s * NB:(s + 1) * NB],
                              start=(s == 0), stop=(s == NS - 1))
                last.then_inc(y_ready, 1)
                pe.wait_ge(yg_ready, c + 1)
                if not first:
                    pe.wait_ge(upd_ready, c)
                mm(po[:, 0:P], yg[:, :], woT[:, :], start=True, stop=False)
                mm(po[:, 0:P], ones[0:1, :], bo[:, :], start=False, stop=True).then_inc(out_ready, 1)

            chunks(pe, body)


class Normed:

    def __init__(self, nc, sb, sem, keep, layer, half, hT, banks, tag):
        self.nc, self.keep, self.hT, self.banks = nc, keep, hT, banks
        self.shift = keep["mod"][:, layer, (3 * half) * P:(3 * half + 1) * P]
        self.scale = keep["mod"][:, layer, (3 * half + 1) * P:(3 * half + 2) * P]
        self.h = sb(f"h{tag}", [P, NT, P])
        self.stats = sb(f"stats{tag}", [P, NT, 6])
        self.mv = sb(f"mv{tag}", [P, NT, 2])
        self.rstd = sb(f"rstd{tag}", [P, NT])
        self.tmp = sb(f"rtmp{tag}", [P, NT])
        self.h_ready, self.t_ready, self.hT_ready = sem(f"h_ready{tag}"), sem(f"t_ready{tag}"), sem(f"hT_ready{tag}")
        self.roots = Roots(sem(f"var_ready{tag}"), sem(f"root_ready{tag}"))

    def vector(self, dve, chain):
        v = self.nc.vector
        layer_norm(dve, v, chain, self.roots, self.keep["x"], self.h, NT, self.stats, self.mv, self.rstd, self.tmp,
                   self.scale, self.shift)
        v.sem_inc(self.h_ready, 1)

    def scalar(self, act):
        self.roots.serve(act, self.nc, self.rstd[:, :], self.tmp[:, :])
        for j in range(NBLK):
            act.wait_ge(self.t_ready, j + 1)
            self.nc.scalar.copy(self.hT[:, j * BLK:(j + 1) * BLK], self.banks[j % 2][:, :]).then_inc(self.hT_ready, 1)

    def tensor(self, pe):
        pe.wait_ge(self.h_ready, 1)
        for j in range(NBLK):
            if j >= 2:
                pe.wait_ge(self.hT_ready, j - 1)
            for q in range(TPB):
                last = self.nc.tensor.transpose(self.banks[j % 2][:, q * P:(q + 1) * P], self.h[:, j * TPB + q, :],
                                                self.keep["ident"][:, :])
            last.then_inc(self.t_ready, 1)


def softmax_probs(dve, nc, chain, probs, logits_ps, bias, top, n, asked, answered):
    v = nc.vector
    wide = lambda t: t.unsqueeze(2).to_broadcast([P, NT, n])
    if bias is None:
        chain(v.tensor_copy(probs, logits_ps))
    else:
        chain(v.tensor_tensor(probs, logits_ps, bias.unsqueeze(1).to_broadcast([P, NT, n]), ALU.add))
    chain(v.tensor_reduce(top, probs, AX.X, ALU.max))
    v.tensor_tensor(probs, probs, wide(top), ALU.subtract).then_inc(asked, 1)
    dve.wait_ge(answered, 1)
    chain(v.tensor_reduce(top, probs, AX.X, ALU.add))
    chain(v.reciprocal(top, top))
    chain(v.tensor_tensor(probs, probs, wide(top), ALU.mult))


def first_of_max(nc, chain, keys, rank, hot, top, n):
    v = nc.vector
    wide = lambda t: t.unsqueeze(2).to_broadcast([P, NT, n])
    chain(v.tensor_reduce(top, keys, AX.X, ALU.max))
    chain(v.tensor_tensor(hot, keys, wide(top), ALU.is_equal))
    chain(v.tensor_tensor(hot, hot, rank.unsqueeze(1).to_broadcast([P, NT, n]), ALU.mult))
    chain(v.tensor_reduce(top, hot, AX.X, ALU.max))
    chain(v.tensor_tensor(hot, hot, wide(top), ALU.is_equal))


def experts0(nc, d, keep):
    x, mod, ident = keep["x"], keep["mod"], keep["ident"]
    with ExitStack() as ctx:
        sb = lambda name, shape, dt=F32: ctx.enter_context(nc.sbuf_tensor(name, shape, dt))
        sem = lambda name: ctx.enter_context(nc.semaphore(name))
        pm = [ctx.enter_context(nc.psum_tensor(f"px{i}", [P, 512], F32)) for i in range(8)]
        hT = sb("hTx", [P, NT * P])
        W = sb("W0", [P, NE0 * P])
        gw = sb("gw0", [P, NX0])
        gb = sb("gb0", [P, NX0])
        eb = sb("eb0", [NE0, P])
        rank = sb("rank0", [P, NX0])
        ranki = sb("ranki0", [P, NX0], mybir.dt.int32)
        probs = sb("probs0", [P, NT, NX0])
        hot = sb("hot0", [P, 2, NT, NX0])
        top = sb("top0", [P, NT])
        den = sb("den0", [P, NT])
        cw = sb("cw0", [P, NT, NE0])
        cwT = sb("cwT0", [NE0, NT * P])
        acc = sb("acc0", [P, 2, 2, P])
        w_in, v_chain, ranks = sem("w_inx"), sem("v_chainx"), sem("ranks0")
        logits_ready, exp_asked, exp_done = sem("logits_ready0"), sem("exp_asked0"), sem("exp_done0")
        cw_ready, cwT_ps, cwT_ready = sem("cw_ready0"), sem("cwT_ps0"), sem("cwT_ready0")
        y_ready, y_used, seeded, x_added = sem("y_readyx"), sem("y_usedx"), sem("seeded0"), sem("x_added0")
        norm = Normed(nc, sb, sem, keep, 0, 1, hT, pm[0:2], "x")
        block = ctx.enter_context(nc.Block())

        @block.sync
        def _(sp):
            for dst, src in ((gw[:, :], d["gw0"]), (gb[:, :], d["gb0"].to_broadcast([P, NX0])),
                             (W[:, :], d["ew0"]), (eb[:, :], d["eb0"])):
                sp.dma_start(dst, src).then_inc(w_in, 16)

        @block.gpsimd
        def _(pool):
            nc.gpsimd.iota(ranki[:, :], pattern=[[-1, NX0]], base=NX0, channel_multiplier=0).then_inc(ranks, 1)
            pool.wait_ge(ranks, 1)
            nc.gpsimd.tensor_copy(rank[:, :], ranki[:, :]).then_inc(ranks, 1)

        @block.scalar
        def _(act):
            norm.scalar(act)
            act.wait_ge(exp_asked, 1)
            nc.scalar.activation(probs[:, :, :], probs[:, :, :], ACT.Exp).then_inc(exp_done, 1)
            for j in range(NBLK):
                act.wait_ge(cwT_ps, j + 1)
                nc.scalar.copy(cwT[:, j * BLK:(j + 1) * BLK], pm[2 + j % 2][0:NE0, :]).then_inc(cwT_ready, 1)
            for k in range(NT):
                act.wait_ge(y_ready, k + 1)
                if k >= 4:
                    act.wait_ge(x_added, k // 2 - 1)
                nc.scalar.copy(acc[:, (k // 2) % 2, k % 2, :], pm[4 + k % 2][:, 0:P]).then_inc(seeded, 1)

        @block.vector
        def _(dve):
            v = nc.vector
            chain = Chain(dve, v_chain)
            norm.vector(dve, chain)
            dve.wait_ge(w_in, 16 * 4)
            dve.wait_ge(ranks, 2)
            dve.wait_ge(logits_ready, 1)
            softmax_probs(dve, nc, chain, probs[:, :, :], pm[4][:, 0:NT * NX0].rearrange("p (k e) -> p k e", e=NX0),
                          gb[:, :], top[:, :], NX0, exp_asked, exp_done)
            wide = lambda t: t.unsqueeze(2).to_broadcast([P, NT, NX0])
            chain(v.tensor_copy(hot[:, 1, :, :], probs[:, :, :]))
            first_of_max(nc, chain, hot[:, 1, :, :], rank[:, :], hot[:, 0, :, :], top[:, :], NX0)
            chain(v.scalar_tensor_tensor(hot[:, 1, :, :], hot[:, 0, :, :], -4.0, probs[:, :, :], ALU.mult, ALU.add))
            chain(v.tensor_tensor(hot[:, 0, :, :], hot[:, 0, :, :], probs[:, :, :], ALU.mult))
            chain(v.tensor_copy(cw[:, :, :], hot[:, 0, :, 0:NE0]))
            first_of_max(nc, chain, hot[:, 1, :, :], rank[:, :], hot[:, 0, :, :], top[:, :], NX0)
            chain(v.tensor_tensor(hot[:, 0, :, :], hot[:, 0, :, :], probs[:, :, :], ALU.mult))
            chain(v.tensor_tensor(cw[:, :, :], cw[:, :, :], hot[:, 0, :, 0:NE0], ALU.add))
            chain(v.tensor_reduce(den[:, :], cw[:, :, :], AX.X, ALU.add))
            chain(v.tensor_scalar(top[:, :], den[:, :], 0.0, None, ALU.is_le))
            chain(v.tensor_tensor(den[:, :], den[:, :], top[:, :], ALU.add))
            chain(v.reciprocal(den[:, :], den[:, :]))
            chain(v.tensor_tensor(cw[:, :, :], cw[:, :, :], den[:, :].unsqueeze(2).to_broadcast([P, NT, NE0]),
                                  ALU.mult))
            v.sem_inc(cw_ready, 1)
            for k2 in range(0, NT, 2):
                for e in range(NE0):
                    for k in (k2, k2 + 1):
                        a, par = k % 2, (k // 2) % 2
                        if e == 0:
                            dve.wait_ge(seeded, k + 1)
                        src = pm[2 * a + e // 4][:, (e % 4) * P:(e % 4 + 1) * P]
                        ins = v.scalar_tensor_tensor(acc[:, par, a, :], src, cw[:, k, e:e + 1], acc[:, par, a, :],
                                                     ALU.mult, ALU.add)
                        ins.then_inc(y_used, 1)
                    if e < NE0 - 1:
                        dve.wait_ge(y_used, k2 * NE0 + 2 * (e + 1))
                par = (k2 // 2) % 2
                dve.wait_ge(y_used, (k2 + 2) * NE0)
                chain(v.tensor_tensor(acc[:, par, :, :], acc[:, par, :, :],
                                      mod[:, 0, 5 * P:6 * P].unsqueeze(1).to_broadcast([P, 2, P]), ALU.mult))
                v.tensor_tensor(x[:, k2:k2 + 2, :], x[:, k2:k2 + 2, :], acc[:, par, :, :], ALU.add)\
                 .then_inc(x_added, 1)

        @block.tensor
        def _(pe):
            mm = nc.tensor.matmul
            norm.tensor(pe)
            pe.wait_ge(w_in, 16 * 4)
            pe.wait_ge(norm.hT_ready, NBLK)
            for k in range(NT):
                last = mm(pm[4][:, k * NX0:(k + 1) * NX0], hT[:, k * P:(k + 1) * P], gw[:, :], start=True, stop=True)
            last.then_inc(logits_ready, 1)
            pe.wait_ge(cw_ready, 1)
            for j in range(NBLK):
                if j >= 2:
                    pe.wait_ge(cwT_ready, j - 1)
                for q in range(TPB):
                    last = nc.tensor.transpose(pm[2 + j % 2][0:NE0, q * P:(q + 1) * P], cw[:, j * TPB + q, :],
                                               ident[:, :])
                last.then_inc(cwT_ps, 1)
            pe.wait_ge(cwT_ready, NBLK)
            for k in range(NT):
                a = k % 2
                if k >= 2:
                    pe.wait_ge(y_used, (k - a) * NE0)
                for half in range(2):
                    mm(pm[2 * a + half][:, :], hT[:, k * P:(k + 1) * P], W[:, half * 512:(half + 1) * 512],
                       start=True, stop=True)
                mm(pm[4 + a][:, 0:P], cwT[:, k * P:(k + 1) * P], eb[:, :], start=True, stop=True).then_inc(y_ready, 1)


QK_TERMS = (((0, 0), (0, 1)), ((1, 1), (0, 1)), ((0, 2), (2, 0)))
REL_TERMS = (((0, 0, 1, 1), (0, 1, 0, 1)), ((0, 2, 1, 2), (2, 0, 2, 1)))
PARTS = 3
TOK = NB * SEQ
V4 = 4
W4 = U // V4
NG4 = NT * W4
TWIN = TLEN - 2 * (V4 - 1)
TROW = TLEN + 1
JT = SEQ // P


def attention_inputs(nc, d, keep, vals, scratch):
    with ExitStack() as ctx:
        sb = lambda name, shape, dt=F32: ctx.enter_context(nc.sbuf_tensor(name, shape, dt))
        sem = lambda name: ctx.enter_context(nc.semaphore(name))
        pm = [ctx.enter_context(nc.psum_tensor(f"pi{i}", [P, 512], F32)) for i in range(8)]
        hT = sb("hTi", [P, TOK])
        wq, wk, wv = sb("wq", [P, P]), sb("wk", [P, P]), sb("wv", [P, P])
        bq, bk, bks, bv = sb("bq", [P, 1]), sb("bk", [P, 1]), sb("bks", [P, 1]), sb("bv", [P, P])
        table = sb("table", [P, TROW])
        tparts = sb("tparts", [P, PARTS, TROW], BF16)
        rest = sb("rest", [P, 2, BLK])
        nat = sb("nat", [P, 2, PARTS, BLK], BF16)
        qparts = sb("qparts", [P, PARTS, V4, NB, NG4], BF16)
        kparts = sb("kparts", [P, PARTS, TOK], BF16)
        hTb = sb("hTb", [P, TOK])
        w_in, t_in, v_chain, bias_ready = sem("w_ini"), sem("t_in"), sem("v_chaini"), sem("bias_ready")
        proj_ready, value_ready, cut_ready = sem("proj_readyi"), sem("value_ready"), sem("cut_ready")
        q_placed, by_seq = sem("q_placed"), sem("by_seq")
        v_ready, v_done, t_cut, stored = sem("v_ready"), sem("v_done"), sem("t_cut"), sem("stored_parts")
        norm = Normed(nc, sb, sem, keep, 1, 0, hT, pm[0:2], "i")
        block = ctx.enter_context(nc.Block())
        NPROJ = 2 * NBLK

        @block.sync
        def _(sp):
            sp.dma_start(table[:, 0:TLEN], d["table"]).then_inc(t_in, 16)
            for dst, src in ((wq[:, :], d["wqT"]), (wk[:, :], d["wkT"]), (wv[:, :], d["wvT"]), (bq[:, :], d["bq"]),
                             (bk[:, :], d["bk"]), (bv[:, :], d["bv"].to_broadcast([P, P]))):
                sp.dma_start(dst, src).then_inc(w_in, 16)
            sp.wait_ge(t_cut, 1)
            for t in range(PARTS):
                sp.dma_start(scratch["t"][t, :, 0:TLEN], tparts[:, t, 0:TLEN]).then_inc(stored, 16)
            sp.wait_ge(q_placed, NBLK)
            for t in range(PARTS):
                sp.dma_start(scratch["q"][t, :, :], qparts[:, t, :, :, :].rearrange("p v b g -> p (v b g)"))\
                  .then_inc(stored, 16)
            sp.wait_ge(cut_ready, NPROJ)
            for t in range(PARTS):
                sp.dma_start(scratch["k"][t, :, :], kparts[:, t, :]).then_inc(stored, 16)
            sp.wait_ge(stored, 16 * 3 * PARTS)

        @block.scalar
        def _(act):
            norm.scalar(act)
            act.wait_ge(w_in, 16 * 6)
            act.wait_ge(bias_ready, 1)
            for n in range(NPROJ):
                par, j = n % 2, n % NBLK
                is_q = n < NBLK
                act.wait_ge(proj_ready, n + 1)
                if n >= 2:
                    act.wait_ge(cut_ready, n - 1)
                nc.scalar.activation(rest[:, par, :], pm[2 + par][:, :], ACT.Identity,
                                     bias=bq[:, 0:1] if is_q else bks[:, 0:1],
                                     scale=1.0 if is_q else HD ** -0.5).then_inc(value_ready, 1)
                if is_q:
                    act.wait_ge(cut_ready, n + 1)
                    for t in range(PARTS):
                        last = nc.scalar.copy(
                            qparts[:, t, :, :, j * (NG4 // NBLK):(j + 1) * (NG4 // NBLK)].rearrange("p v b g -> p g (v b)"),
                            nat[:, par, t, :].rearrange("p (g c) -> p g c", c=V4 * NB))
                    last.then_inc(q_placed, 1)

        @block.vector
        def _(dve):
            v = nc.vector
            chain = Chain(dve, v_chain)
            dve.wait_ge(w_in, 16 * 6)
            v.tensor_scalar(bks[:, :], bk[:, :], HD ** -0.5, None, ALU.mult).then_inc(bias_ready, 1)
            dve.wait_ge(t_in, 16)
            T = slice(0, TLEN)
            chain(v.tensor_copy(tparts[:, 0, T], table[:, T]))
            chain(v.tensor_tensor(table[:, T], table[:, T], tparts[:, 0, T], ALU.subtract))
            chain(v.tensor_copy(tparts[:, 1, T], table[:, T]))
            v.tensor_tensor(tparts[:, 2, T], table[:, T], tparts[:, 1, T], ALU.subtract).then_inc(t_cut, 1)
            norm.vector(dve, chain)
            for n in range(NPROJ):
                par = n % 2
                dve.wait_ge(value_ready, n + 1)
                j = n % NBLK
                p0, p1, p2 = (nat[:, par, t, :] if n < NBLK else kparts[:, t, j * BLK:(j + 1) * BLK]
                              for t in range(PARTS))
                if 2 <= n < NBLK:
                    dve.wait_ge(q_placed, n - 1)
                chain(v.tensor_copy(p0, rest[:, par, :]))
                chain(v.tensor_tensor(rest[:, par, :], rest[:, par, :], p0, ALU.subtract))
                chain(v.tensor_copy(p1, rest[:, par, :]))
                v.tensor_tensor(p2, rest[:, par, :], p1, ALU.subtract).then_inc(cut_ready, 1)
            for m in range(JT * NB // TPB):
                dve.wait_ge(v_ready, m + 1)
                v.tensor_tensor(vals[:, m * TPB:(m + 1) * TPB, :], pm[4 + m % 2][:, :].rearrange("p (q e) -> p q e", q=TPB),
                                bv[:, :].unsqueeze(1).to_broadcast([P, TPB, P]), ALU.add).then_inc(v_done, 1)

        @block.gpsimd
        def _(pool):
            for j in range(NBLK):
                pool.wait_ge(norm.hT_ready, j + 1)
                for c in range(2):
                    src = hT[:, (2 * j + c) * 2 * P:(2 * j + c + 1) * 2 * P].rearrange("p (o u b) -> p o u b", o=2, u=U)
                    dst = hTb[:, :].rearrange("p (b c u o) -> p c o u b", b=NB, u=U, o=2)[:, 2 * j + c, :, :, :]
                    nc.gpsimd.tensor_copy(dst, src).then_inc(by_seq, 1)

        @block.tensor
        def _(pe):
            mm = nc.tensor.matmul
            norm.tensor(pe)
            pe.wait_ge(w_in, 16 * 6)
            pe.wait_ge(norm.hT_ready, NBLK)
            for n in range(NPROJ):
                j = n % NBLK
                if n >= 2:
                    pe.wait_ge(value_ready, n - 1)
                if n == NBLK:
                    pe.wait_ge(by_seq, 2 * NBLK)
                w, src = (wq, hT) if n < NBLK else (wk, hTb)
                mm(pm[2 + n % 2][:, :], w[:, :], src[:, j * BLK:(j + 1) * BLK], start=True, stop=True)\
                  .then_inc(proj_ready, 1)
            for m in range(JT * NB // TPB):
                if m >= 2:
                    pe.wait_ge(v_done, m - 1)
                for q in range(TPB):
                    jt, b = divmod(m * TPB + q, NB)
                    last = mm(pm[4 + m % 2][:, q * P:(q + 1) * P], hTb[:, b * SEQ + jt * P:b * SEQ + (jt + 1) * P],
                              wv[:, :], start=True, stop=True)
                last.then_inc(v_ready, 1)


def attention(nc, d, keep, vals, scratch, ctxt):
    ident = keep["ident"]
    with ExitStack() as ctx:
        sb = lambda name, shape, dt=F32: ctx.enter_context(nc.sbuf_tensor(name, shape, dt))
        sem = lambda name: ctx.enter_context(nc.semaphore(name))
        qs = [[sb(f"qs{p}{m}", [P, V4, NB, NG4], BF16) for m in range(len(QK_TERMS))] for p in range(2)]
        qr = [[sb(f"qr{p}{m}", [P, V4, NB, NG4], BF16) for m in range(len(REL_TERMS))] for p in range(2)]
        ks = [[sb(f"ks{p}{m}", [P, SEQ], BF16) for m in range(2)] for p in range(2)]
        tb = [[sb(f"tb{p}{m}", [P, TWIN], BF16) for m in range(len(REL_TERMS))] for p in range(2)]
        vh = sb("vh", [P, 2, JT, NB, HD])
        mask = sb("mask", [P, NB, HD])
        own = sb("own", [P, NB])
        prob = [sb(f"prob{i}", [P, SEQ]) for i in range(2)]
        probT = [sb(f"probT{i}", [P, JT, P]) for i in range(2)]
        ntop = sb("ntop", [P, NT])
        rsum = sb("rsum", [P, 2, NT])
        picked = sb("picked", [P, 2, NB, NB, HD])
        part = sb("part", [P, 2, NB, HD])
        sp_ = [ctx.enter_context(nc.psum_tensor(f"score{i}", [P, 512], F32)) for i in range(3)]
        tp_ = [ctx.enter_context(nc.psum_tensor(f"turned{i}", [P, 512], F32)) for i in range(2)]
        vp_ = [ctx.enter_context(nc.psum_tensor(f"mixed{i}", [P, 512], F32)) for i in range(2)]
        zeroed, mask_ready, head_in, v_head = sem("zeroed"), sem("mask_ready"), [sem("head_in0"), sem("head_in1")], sem("v_head")
        scores, top_ready, prob_ready, turned, turned_sb = (sem("scores"), sem("top_ready"), sem("prob_ready"),
                                                            sem("turned"), sem("turned_sb"))
        mixed, picked_ready, rinv_ready, part_ready, ctx_ready = (
            sem("mixed"), sem("picked_ready"), sem("rinv_ready"), sem("part_ready"), sem("ctx_ready"))
        block = ctx.enter_context(nc.Block())
        GRP = 8
        NG = NT // GRP
        PS = P * TOK

        def load_head(eng, p, h):
            n = 0

            def start(dst, base, dims):
                nonlocal n
                src = bass.AP(base.tensor, base.offset + dims[0], dims[1])
                eng.dma_start(dst, src).then_inc(head_in[p], 16)
                n += 1

            for m, ((t0, t1), _) in enumerate(QK_TERMS):
                for b in range(NB):
                    start(qs[p][m][16 * b:16 * b + 16, :, b, :], scratch["q"],
                          (h * (HD * TOK) + t0 * PS + b * NG4,
                           [[(t1 - t0) * PS, 2], [TOK, HD], [NB * NG4, V4], [1, NG4]]))
            for m, (ts, tt) in enumerate(REL_TERMS):
                for w in range(V4):
                    for a in range(2):
                        start(qr[p][m][32 * w + 16 * a:32 * w + 16 * a + 16, w, :, :], scratch["q"],
                              (h * (HD * TOK) + ts[2 * a] * PS + w * NB * NG4,
                               [[(ts[2 * a + 1] - ts[2 * a]) * PS, 2], [TOK, HD], [1, NB * NG4]]))
                        for z in range(2):
                            at = 32 * w + 16 * a + 8 * z
                            start(tb[p][m][at:at + 8, :], scratch["t"],
                                  (h * (HD * TROW) + tt[2 * a + z] * P * TROW + 2 * (V4 - 1 - w), [[TROW, HD], [1, TWIN]]))
            for m, t in ((0, 0), (0, 1), (1, 2), (1, 0)):
                z = {(0, 0): 0, (0, 1): 1, (1, 2): 0, (1, 0): 1}[(m, t)]
                for b in range(NB):
                    at = 16 * b + 8 * z
                    start(ks[p][m][at:at + 8, :], scratch["k"],
                          (h * (HD * TOK) + t * PS + b * SEQ, [[TOK, HD], [1, SEQ]]))
            return n

        counted = [0]

        @block.sync
        def _(sp):
            sp.wait_ge(zeroed, 2 * (len(QK_TERMS) + len(REL_TERMS)))
            counted[0] = load_head(sp, 0, 0)
            load_head(sp, 1, 1)
            with sp.Fori(1, HEADS // 2) as i:
                for p in range(2):
                    sp.wait_ge(scores, (2 * i - 1 + p) * NT)
                    load_head(sp, p, 2 * i + p)

        ARRIVED = 16 * counted[0]

        @block.gpsimd
        def _(pool):
            for p in range(2):
                for t in (*qs[p], *qr[p]):
                    nc.gpsimd.memset(t[:, :, :, :], 0.0).then_inc(zeroed, 1)

            def head(p, h, used):
                if used:
                    pool.wait_ge(mixed, (h - 1) * NT)
                src = vals[:, :, bass.ds(h * HD, HD)] if not isinstance(h, int) else vals[:, :, h * HD:(h + 1) * HD]
                nc.gpsimd.tensor_copy(vh[:, p, :, :, :].rearrange("p j b d -> p (j b) d"), src).then_inc(v_head, 1)

            head(0, 0, False)
            head(1, 1, False)
            with pool.Fori(1, HEADS // 2) as i:
                head(0, 2 * i, True)
                head(1, 2 * i + 1, True)

        @block.tensor
        def _(pe):
            mm = nc.tensor.matmul

            def score(h, p, k):
                n = h * NT + k
                if k == 0:
                    pe.wait_ge(head_in[p], ARRIVED * (h // 2 + 1) if isinstance(h, int) else ARRIVED * (h_pair[0] + 1))
                out = sp_[k % 3]
                if k >= 3:
                    pe.wait_ge(prob_ready, n - 2)
                c, o = divmod(k, 2)
                for m in range(len(REL_TERMS)):
                    for w in range(W4):
                        s = SEQ - 1 - 2 * U * c - o - 2 * V4 * w - 2 * (V4 - 1)
                        mm(out[32 * w:32 * w + 32, :],
                           qr[p][m][:, :, :, k * W4 + w].rearrange("p v b -> p (v b)"), tb[p][m][:, s:s + SEQ],
                           start=(m == 0), stop=False)
                for m in range(len(QK_TERMS)):
                    for w in range(W4):
                        last = mm(out[32 * w:32 * w + 32, :],
                                  qs[p][m][:, :, :, k * W4 + w].rearrange("p v b -> p (v b)"), ks[p][m // 2][:, :],
                                  start=False, stop=(m == len(QK_TERMS) - 1))
                last.then_inc(scores, 1)

            def turn(h, k):
                n = h * NT + k
                pe.wait_ge(prob_ready, n + 1)
                if k >= 2:
                    pe.wait_ge(turned_sb, n - 1)
                for j in range(JT):
                    last = nc.tensor.transpose(tp_[k % 2][:, j * P:(j + 1) * P], prob[k % 2][:, j * P:(j + 1) * P],
                                               ident[:, :])
                last.then_inc(turned, 1)

            def mix(h, p, k):
                n = h * NT + k
                pe.wait_ge(turned_sb, n + 1)
                if k == 0:
                    pe.wait_ge(v_head, h + 1)
                g = k // GRP
                if k % GRP == 0 and g >= 2:
                    pe.wait_ge(picked_ready, h * NG + g - 1)
                for j in range(JT):
                    last = mm(vp_[g % 2][:, (k % GRP) * NB * HD:(k % GRP + 1) * NB * HD], probT[k % 2][:, j, :],
                              vh[:, p, j, :, :].rearrange("p b d -> p (b d)"), start=(j == 0), stop=(j == JT - 1))
                last.then_inc(mixed, 1)

            h_pair = [0]
            with pe.Fori(0, HEADS // 2) as i:
                h_pair[0] = i
                for p in range(2):
                    h = 2 * i + p
                    for k in range(NT + 3):
                        if k < NT:
                            score(h, p, k)
                        if 2 <= k < NT + 2:
                            turn(h, k - 2)
                        if k >= 3:
                            mix(h, p, k - 3)

        @block.scalar
        def _(act):
            with act.Fori(0, HEADS // 2) as i:
                for p in range(2):
                    h = 2 * i + p
                    for k in range(NT + 1):
                        n = h * NT + k
                        if k < NT:
                            act.wait_ge(top_ready, n + 1)
                            if k >= 2:
                                act.wait_ge(turned, n - 1)
                            nc.scalar.activation(prob[k % 2][:, :], sp_[k % 3][:, :], ACT.Exp, bias=ntop[:, k:k + 1],
                                                 accum_out=rsum[:, p, k:k + 1]).then_inc(prob_ready, 1)
                        if k >= 1:
                            act.wait_ge(turned, n)
                            if k >= 3:
                                act.wait_ge(mixed, n - 2)
                            nc.scalar.copy(probT[(k - 1) % 2][:, :, :].rearrange("p j t -> p (j t)"),
                                           tp_[(k - 1) % 2][:, :]).then_inc(turned_sb, 1)

        @block.vector
        def _(dve):
            v = nc.vector
            v.tensor_reduce(own[:, :], ident[:, :].rearrange("p (u b) -> p b u", b=NB), AX.X, ALU.add)\
             .then_inc(mask_ready, 1)
            dve.wait_ge(mask_ready, 1)
            v.tensor_copy(mask[:, :, :], own[:, :].unsqueeze(2).to_broadcast([P, NB, HD])).then_inc(mask_ready, 1)
            dve.wait_ge(mask_ready, 2)

            def finish(h, p, g):
                n = h * NG + g
                dve.wait_ge(mixed, h * NT + (g + 1) * GRP)
                q = g % 2
                tiles = slice(g * GRP, (g + 1) * GRP)
                v.tensor_tensor(picked[:, q, :, :, :].rearrange("p k b d -> p k (b d)"),
                                vp_[g % 2][:, :].rearrange("p (k e) -> p k e", k=GRP),
                                mask[:, :, :].rearrange("p b d -> p (b d)").unsqueeze(1).to_broadcast([P, GRP, NB * HD]),
                                ALU.mult).then_inc(picked_ready, 1)
                v.reciprocal(rsum[:, p, tiles], rsum[:, p, tiles]).then_inc(rinv_ready, 1)
                dve.wait_ge(picked_ready, n + 1)
                v.tensor_reduce(part[:, q, :, :], picked[:, q, :, :, :].rearrange("p k b d -> p k d b"), AX.X, ALU.add)\
                 .then_inc(part_ready, 1)
                dve.wait_ge(rinv_ready, n + 1)
                dve.wait_ge(part_ready, n + 1)
                v.tensor_tensor(ctxt[:, tiles, bass.ds(h * HD, HD)], part[:, q, :, :],
                                rsum[:, p, tiles].unsqueeze(2).to_broadcast([P, GRP, HD]), ALU.mult)\
                 .then_inc(ctx_ready, 1)

            with dve.Fori(0, HEADS // 2) as i:
                for p in range(2):
                    h = 2 * i + p
                    for k in range(NT):
                        n = h * NT + k
                        dve.wait_ge(scores, n + 1)
                        v.tensor_reduce(ntop[:, k:k + 1], sp_[k % 3][:, :], AX.X, ALU.max, negate=True)\
                         .then_inc(top_ready, 1)
                        if k >= 12 and (k - 12) % GRP == 0:
                            finish(h, p, (k - 12) // GRP)
                    finish(h, p, NG - 1)


def attention_output(nc, d, keep, ctxt):
    x, mod, ident, ones = keep["x"], keep["mod"], keep["ident"], keep["ones"]
    with ExitStack() as ctx:
        sb = lambda name, shape, dt=F32: ctx.enter_context(nc.sbuf_tensor(name, shape, dt))
        sem = lambda name: ctx.enter_context(nc.semaphore(name))
        pt = [ctx.enter_context(nc.psum_tensor(f"pt{i}", [P, 512], F32)) for i in range(2)]
        po = [ctx.enter_context(nc.psum_tensor(f"pp{i}", [P, 512], F32)) for i in range(2)]
        wo, bo = sb("wo1", [P, P]), sb("bo1", [1, P])
        cT = sb("ctxT", [P, 2, BLK])
        upd = sb("upd1", [P, 2, TPB, P])
        w_in, turned, cT_ready, out_ready, upd_ready, x_added = (
            sem("w_ino"), sem("turnedo"), sem("cT_ready"), sem("out_readyo"), sem("upd_readyo"), sem("x_addedo"))
        block = ctx.enter_context(nc.Block())

        @block.sync
        def _(sp):
            sp.dma_start(wo[:, :], d["woT"]).then_inc(w_in, 16)
            sp.dma_start(bo[:, :], d["bo"]).then_inc(w_in, 16)

        @block.scalar
        def _(act):
            for j in range(NBLK):
                act.wait_ge(turned, j + 1)
                if j >= 2:
                    act.wait_ge(out_ready, j - 1)
                nc.scalar.copy(cT[:, j % 2, :], pt[j % 2][:, :]).then_inc(cT_ready, 1)

        @block.tensor
        def _(pe):
            pe.wait_ge(w_in, 32)
            for j in range(NBLK + 1):
                if j < NBLK:
                    if j >= 2:
                        pe.wait_ge(cT_ready, j - 1)
                    for q in range(TPB):
                        last = nc.tensor.transpose(pt[j % 2][:, q * P:(q + 1) * P], ctxt[:, j * TPB + q, :], ident[:, :])
                    last.then_inc(turned, 1)
                if j >= 1:
                    i = j - 1
                    pe.wait_ge(cT_ready, i + 1)
                    if i >= 2:
                        pe.wait_ge(upd_ready, i - 1)
                    for q in range(TPB):
                        to = po[i % 2][:, q * P:(q + 1) * P]
                        nc.tensor.matmul(to, cT[:, i % 2, q * P:(q + 1) * P], wo[:, :], start=True, stop=False)
                        last = nc.tensor.matmul(to, ones[0:1, :], bo[:, :], start=False, stop=True)
                    last.then_inc(out_ready, 1)

        @block.vector
        def _(dve):
            v = nc.vector
            for j in range(NBLK):
                dve.wait_ge(out_ready, j + 1)
                if j >= 2:
                    dve.wait_ge(x_added, j - 1)
                v.tensor_tensor(upd[:, j % 2, :, :], po[j % 2][:, :].rearrange("p (q e) -> p q e", q=TPB),
                                mod[:, 1, 2 * P:3 * P].unsqueeze(1).to_broadcast([P, TPB, P]), ALU.mult)\
                 .then_inc(upd_ready, 1)
                dve.wait_ge(upd_ready, j + 1)
                xs = x[:, j * TPB:(j + 1) * TPB, :]
                v.tensor_tensor(xs, xs, upd[:, j % 2, :, :], ALU.add).then_inc(x_added, 1)
            dve.wait_ge(x_added, NBLK)


def experts1(nc, d, keep):
    x, mod, ident = keep["x"], keep["mod"], keep["ident"]
    NALL = NE1 + 1
    WCOLS = 5 * P
    with ExitStack() as ctx:
        sb = lambda name, shape, dt=F32: ctx.enter_context(nc.sbuf_tensor(name, shape, dt))
        sem = lambda name: ctx.enter_context(nc.semaphore(name))
        pm = [ctx.enter_context(nc.psum_tensor(f"pz{i}", [P, 512], F32)) for i in range(8)]
        hT = sb("hTz", [P, TOK])
        W = [sb(f"w1_{p}", [P, WCOLS]) for p in range(2)]
        B = [sb(f"b1_{p}", [P, 4]) for p in range(2)]
        gw = sb("gw1", [P, NE1])
        gb = sb("gb1", [P, NE1])
        b2 = sb("b2", [NALL, P])
        rank = sb("rank1", [P, NE1])
        ranki = sb("ranki1", [P, NE1], mybir.dt.int32)
        probs = sb("probs1", [P, NT, NE1])
        keys = sb("keys1", [P, NT, NE1])
        hot = sb("hot1", [P, NT, NE1])
        top = sb("top1", [P, NT])
        cw = sb("cw1", [P, NT, NALL])
        cwe = sb("cwe", [P, 2, NT])
        cwT = sb("cwT1", [NALL, TOK])
        acc = sb("acc1", [P, NT, P])
        g1, l1 = sb("g1", [P, 2, BLK]), sb("l1", [P, 2, BLK])
        gg, ll = sb("gg", [P, 2, BLK]), sb("ll", [P, 2, BLK])
        th, a = sb("th", [P, 2, BLK]), sb("a", [P, 2, BLK])
        w_in, v_chain, ranks = sem("w_inz"), sem("v_chainz"), sem("ranks1")
        logits_ready, exp_asked, exp_done = sem("logits_ready1"), sem("exp_asked1"), sem("exp_done1")
        cw_ready, cwT_ps, cwT_ready = sem("cw_ready1"), sem("cwT_ps1"), sem("cwT_ready1")
        seed_ps, seeded = sem("seed_ps"), sem("seeded1")
        we_in, w2_half = [sem("we_in0"), sem("we_in1")], sem("w2_half")
        gate_ps, lin_ps, first_g, first_l = sem("gate_ps"), sem("lin_ps"), sem("first_g"), sem("first_l")
        pool_steps = sem("pool_steps")
        gg_raw, gg_ready, th_ready = sem("gg_raw"), sem("gg_ready"), sem("th_ready")
        ll_raw, ll_ready, gl_ready, a_ready = sem("ll_raw"), sem("ll_ready"), sem("gl_ready"), sem("a_ready")
        y_ready, y_summed, cwe_ready = sem("y_ready1"), sem("y_summed"), sem("cwe_ready")
        norm = Normed(nc, sb, sem, keep, 1, 1, hT, pm[0:2], "z")
        G1, L1, G3, L3, Y = pm[0], pm[1], pm[2:4], pm[4:6], pm[6:8]
        block = ctx.enter_context(nc.Block())

        def experts(eng, body):
            body(0, 0)
            body(1, 1)
            with eng.Fori(1, NE1 // 2) as i:
                body(2 * i, 0)
                body(2 * i + 1, 1)
            body(NE1, 0)

        def back(e, p, j, steps):
            if j >= steps:
                return e * NBLK + j - steps, p, j - steps
            if isinstance(e, int) and e == 0:
                return None
            return e * NBLK + j - steps, 1 - p, j - steps + NBLK

        def weights_in(e, p):
            return 32 * (e // 2 + 1) if isinstance(e, int) else 16 * e + 32 - 16 * p

        @block.sync
        def _(sp):
            for dst, src in ((gw[:, :], d["gw1"]), (gb[:, :], d["gb1"].to_broadcast([P, NE1])),
                             (b2[:, :], d["b2"])):
                sp.dma_start(dst, src).then_inc(w_in, 16)

            def load(e, p):
                w, b = ((d["ew1"][bass.ds(e, 1), :, :], d["eb1"][bass.ds(e, 1), :, :]) if not isinstance(e, int)
                        else (d["ew1"][e:e + 1, :, :], d["eb1"][e:e + 1, :, :]))
                sp.dma_start(W[p][:, :], w.rearrange("o p n -> p (o n)")).then_inc(we_in[p], 16)
                sp.dma_start(B[p][:, :], b.rearrange("o p n -> p (o n)")).then_inc(we_in[p], 16)

            load(0, 0)
            load(1, 1)
            with sp.Fori(1, NE1 // 2) as i:
                for p in range(2):
                    sp.wait_ge(y_ready, (2 * i - 1 + p) * NBLK)
                    load(2 * i + p, p)
            sp.wait_ge(y_ready, (NE1 - 1) * NBLK)
            load(NE1, 0)

        @block.gpsimd
        def _(pool):
            nc.gpsimd.iota(ranki[:, :], pattern=[[-1, NE1]], base=NE1, channel_multiplier=0).then_inc(ranks, 1)
            pool.wait_ge(ranks, 1)
            nc.gpsimd.tensor_copy(rank[:, :], ranki[:, :]).then_inc(ranks, 1)

            def body(e, p):
                for j in range(NBLK):
                    n, q = e * NBLK + j, j % 2
                    pool.wait_ge(gg_raw, n + 1)
                    pool.sem_inc(pool_steps, 1)
                    nc.gpsimd.tensor_scalar(gg[:, q, :], gg[:, q, :], LIMIT, LOWEST, ALU.min, ALU.max)\
                      .then_inc(gg_ready, 1)
                    pool.wait_ge(ll_raw, n + 1)
                    pool.sem_inc(pool_steps, 1)
                    nc.gpsimd.tensor_scalar(ll[:, q, :], ll[:, q, :], LIMIT, -LIMIT, ALU.min, ALU.max)\
                      .then_inc(ll_ready, 1)

            experts(pool, body)

        @block.scalar
        def _(act):
            norm.scalar(act)
            act.wait_ge(exp_asked, 1)
            nc.scalar.activation(probs[:, :, :], probs[:, :, :], ACT.Exp).then_inc(exp_done, 1)
            for j in range(NBLK):
                act.wait_ge(cwT_ps, j + 1)
                nc.scalar.copy(cwT[:, j * BLK:(j + 1) * BLK], pm[2 + j % 2][0:NALL, :]).then_inc(cwT_ready, 1)
            for j in range(NBLK):
                act.wait_ge(seed_ps, j + 1)
                nc.scalar.copy(acc[:, j * TPB:(j + 1) * TPB, :].rearrange("p k e -> p (k e)"),
                               pm[4 + j % 2][:, :]).then_inc(seeded, 1)

            def tanh(n, p, j):
                act.wait_ge(gg_ready, n + 1)
                nc.scalar.activation(th[:, j % 2, :], gg[:, j % 2, :], ACT.Tanh, scale=ALPHA / 2)\
                  .then_inc(th_ready, 1)

            def body(e, p):
                act.wait_ge(we_in[p], weights_in(e, p))
                for j in range(NBLK):
                    n, q = e * NBLK + j, j % 2
                    act.wait_ge(gate_ps, n + 1)
                    nc.scalar.activation(g1[:, q, :], G1[:, :], ACT.Identity, bias=B[p][:, 0:1])\
                      .then_inc(first_g, 1)
                    if back(e, p, j, 1):
                        tanh(*back(e, p, j, 1))
                    act.wait_ge(lin_ps, n + 1)
                    nc.scalar.activation(l1[:, q, :], L1[:, :], ACT.Identity, bias=B[p][:, 1:2])\
                      .then_inc(first_l, 1)

            experts(act, body)
            tanh(*back(NE1, 0, NBLK, 1))

        @block.vector
        def _(dve):
            v = nc.vector
            chain = Chain(dve, v_chain)
            norm.vector(dve, chain)
            dve.wait_ge(w_in, 16 * 3)
            dve.wait_ge(ranks, 2)
            dve.wait_ge(logits_ready, 1)
            softmax_probs(dve, nc, chain, probs[:, :, :], pm[4][:, 0:NT * NE1].rearrange("p (k e) -> p k e", e=NE1),
                          None, top[:, :], NE1, exp_asked, exp_done)
            chain(v.tensor_tensor(keys[:, :, :], probs[:, :, :], gb[:, :].unsqueeze(1).to_broadcast([P, NT, NE1]),
                                  ALU.add))
            first_of_max(nc, chain, keys[:, :, :], rank[:, :], hot[:, :, :], top[:, :], NE1)
            chain(v.tensor_tensor(cw[:, :, 0:NE1], hot[:, :, :], probs[:, :, :], ALU.mult))
            chain(v.scalar_tensor_tensor(keys[:, :, :], hot[:, :, :], -3e38, keys[:, :, :], ALU.mult, ALU.add))
            first_of_max(nc, chain, keys[:, :, :], rank[:, :], hot[:, :, :], top[:, :], NE1)
            chain(v.tensor_tensor(hot[:, :, :], hot[:, :, :], probs[:, :, :], ALU.mult))
            chain(v.tensor_tensor(cw[:, :, 0:NE1], cw[:, :, 0:NE1], hot[:, :, :], ALU.add))
            chain(v.memset(cw[:, :, NE1:NALL], 1.0))
            v.sem_inc(cw_ready, 1)
            dve.wait_ge(seeded, NBLK)

            def add_up(n, p, j):
                dve.wait_ge(y_ready, n + 1)
                for t in range(TPB):
                    k = j * TPB + t
                    last = v.scalar_tensor_tensor(acc[:, k, :], Y[j % 2][:, t * P:(t + 1) * P],
                                                  cwe[:, p, k:k + 1], acc[:, k, :], ALU.mult, ALU.add)
                last.then_inc(y_summed, 1)

            def join(n, p, j):
                q = j % 2
                dve.wait_ge(gg_ready, n + 1)
                dve.wait_ge(ll_ready, n + 1)
                v.scalar_tensor_tensor(ll[:, q, :], ll[:, q, :], 1.0, gg[:, q, :], ALU.add, ALU.mult)\
                 .then_inc(gl_ready, 1)
                dve.wait_ge(gl_ready, n + 1)
                dve.wait_ge(th_ready, n + 1)
                v.scalar_tensor_tensor(a[:, q, :], th[:, q, :], 1.0, ll[:, q, :], ALU.add, ALU.mult)\
                 .then_inc(a_ready, 1)

            def body(e, p):
                src = cw[:, :, bass.ds(e, 1)] if not isinstance(e, int) else cw[:, :, e:e + 1]
                v.tensor_copy(cwe[:, p, :].unsqueeze(2), src).then_inc(cwe_ready, 1)
                dve.wait_ge(cwe_ready, e + 1)
                dve.wait_ge(we_in[p], weights_in(e, p))
                v.tensor_scalar(W[p][:, 4 * P:5 * P], W[p][:, 4 * P:5 * P], 0.5, None, ALU.mult).then_inc(w2_half, 1)
                dve.wait_ge(w2_half, e + 1)
                for j in range(NBLK):
                    n, q = e * NBLK + j, j % 2
                    if back(e, p, j, 2):
                        dve.wait_ge(a_ready, n - 1)
                    dve.wait_ge(first_g, n + 1)
                    v.scalar_tensor_tensor(gg[:, q, :], G3[q][:, :], B[p][:, 2:3], g1[:, q, :],
                                           ALU.add, ALU.mult).then_inc(gg_raw, 1)
                    dve.wait_ge(first_l, n + 1)
                    v.scalar_tensor_tensor(ll[:, q, :], L3[q][:, :], B[p][:, 3:4], l1[:, q, :],
                                           ALU.add, ALU.mult).then_inc(ll_raw, 1)
                    if back(e, p, j, 1):
                        join(*back(e, p, j, 1))
                    if back(e, p, j, 2):
                        add_up(*back(e, p, j, 2))

            experts(dve, body)
            join(*back(NE1, 0, NBLK, 1))
            add_up(*back(NE1, 0, NBLK, 2))
            add_up(*back(NE1, 0, NBLK, 1))
            dve.wait_ge(y_summed, NBLK * NALL)
            for j in range(NBLK):
                ts = slice(j * TPB, (j + 1) * TPB)
                chain(v.tensor_tensor(acc[:, ts, :], acc[:, ts, :],
                                      mod[:, 1, 5 * P:6 * P].unsqueeze(1).to_broadcast([P, TPB, P]), ALU.mult))
                chain(v.tensor_tensor(x[:, ts, :], x[:, ts, :], acc[:, ts, :], ALU.add))

        @block.tensor
        def _(pe):
            mm = nc.tensor.matmul
            norm.tensor(pe)
            pe.wait_ge(w_in, 16 * 3)
            pe.wait_ge(norm.hT_ready, NBLK)
            for k in range(NT):
                last = mm(pm[4][:, k * NE1:(k + 1) * NE1], hT[:, k * P:(k + 1) * P], gw[:, :], start=True, stop=True)
            last.then_inc(logits_ready, 1)
            pe.wait_ge(cw_ready, 1)
            for j in range(NBLK):
                if j >= 2:
                    pe.wait_ge(cwT_ready, j - 1)
                for t in range(TPB):
                    last = nc.tensor.transpose(pm[2 + j % 2][0:NALL, t * P:(t + 1) * P], cw[:, j * TPB + t, :],
                                               ident[:, :])
                last.then_inc(cwT_ps, 1)
            for j in range(NBLK):
                pe.wait_ge(cwT_ready, j + 1)
                if j >= 2:
                    pe.wait_ge(seeded, j - 1)
                for t in range(TPB):
                    last = mm(pm[4 + j % 2][:, t * P:(t + 1) * P], cwT[:, (j * TPB + t) * P:(j * TPB + t + 1) * P],
                              b2[:, :], start=True, stop=True)
                last.then_inc(seed_ps, 1)
            pe.wait_ge(seeded, NBLK)

            def second(n, p, j):
                pe.wait_ge(a_ready, n + 1)
                if not (isinstance(n, int) and n < 2):
                    pe.wait_ge(y_summed, n - 1)
                for t in range(TPB):
                    last = mm(Y[j % 2][:, t * P:(t + 1) * P], a[:, j % 2, t * P:(t + 1) * P],
                              W[p][:, 4 * P:5 * P], start=True, stop=True)
                last.then_inc(y_ready, 1)

            def body(e, p):
                pe.wait_ge(we_in[p], weights_in(e, p))
                for j in range(NBLK):
                    n, q = e * NBLK + j, j % 2
                    src = hT[:, j * BLK:(j + 1) * BLK]
                    first = isinstance(e, int) and e == 0
                    if not (first and j == 0):
                        pe.wait_ge(first_g, n)
                    mm(G1[:, :], W[p][:, 0:P], src, start=True, stop=True)
                    if not (first and j < 2):
                        pe.wait_ge(gg_raw, n - 1)
                    mm(G3[q][:, :], W[p][:, 2 * P:3 * P], src, start=True, stop=True).then_inc(gate_ps, 1)
                    if not (first and j == 0):
                        pe.wait_ge(first_l, n)
                    mm(L1[:, :], W[p][:, P:2 * P], src, start=True, stop=True)
                    if not (first and j < 2):
                        pe.wait_ge(ll_raw, n - 1)
                    mm(L3[q][:, :], W[p][:, 3 * P:4 * P], src, start=True, stop=True).then_inc(lin_ps, 1)
                    if back(e, p, j, 2):
                        second(*back(e, p, j, 2))

            experts(pe, body)
            second(*back(NE1, 0, NBLK, 2))
            second(*back(NE1, 0, NBLK, 1))


def store(nc, d, keep, out):
    with nc.semaphore("stored") as stored, nc.Block() as block:
        @block.sync
        def _(sp):
            sp.dma_start(out, keep["x"][:, :, :]).then_inc(stored, 16)
            sp.wait_ge(stored, 16)


def program(nc, d, out, stop):
    with ExitStack() as ctx:
        sb = lambda name, shape, dt=F32: ctx.enter_context(nc.sbuf_tensor(name, shape, dt))
        keep = {"x": sb("x", [P, NT, P]), "mod": sb("mod", [P, 2, MODS * P]),
                "ident": sb("ident", [P, P]), "ones": sb("ones", [P, P])}
        with ExitStack() as inner:
            sb1 = lambda name, shape, dt=F32: inner.enter_context(nc.sbuf_tensor(name, shape, dt))
            scan = {"A": sb1("A", [P, NS * NB]), "Bm": sb1("Bm", [P, NS]), "Dv": sb1("Dv", [P, 1]),
                    "xp": sb1("xp", [P, NC * P]), "gate": sb1("gate2", [P, NC * P]),
                    "hist": sb1("hist", [P, 2, U, NS * NB]), "diagC": sb1("diagC", [P, NS, P]),
                    "woT": sb1("woT", [P, P]), "bo": sb1("bo", [1, P])}
            prologue(nc, d, keep, scan)
            scan_phase(nc, d, keep, scan)
        experts0(nc, d, keep)
        scratch = {n: nc.dram_tensor(f"parts_{n}", shape, BF16, kind="Internal").ap()
                   for n, shape in (("q", (PARTS, P, TOK)), ("k", (PARTS, P, TOK)),
                                    ("t", (PARTS, P, TROW)))}
        with ExitStack() as inner:
            vals = inner.enter_context(nc.sbuf_tensor("vals", [P, JT * NB, P], F32))
            attention_inputs(nc, d, keep, vals, scratch)
            ctxt = inner.enter_context(nc.sbuf_tensor("ctxt", [P, NT, P], F32))
            attention(nc, d, keep, vals, scratch, ctxt)
            attention_output(nc, d, keep, ctxt)
        experts1(nc, d, keep)
        store(nc, d, keep, out)


def layouts(inputs, np):
    g = lambda n: np.asarray(inputs[n])
    a = {}
    a["x"] = g("L0_attn_x").reshape(NB, NC, U, 2, P).transpose(2, 0, 1, 3, 4).reshape(P, NT, P)
    a["cT"] = np.stack([g("L0_c").T, g("L1_c").T], 1)
    a["wmod"] = np.stack([g("L0_wmod"), g("L1_wmod")], 1)
    a["w_inT"] = g("L0_attn_w_in").T
    a["b_in"] = g("L0_attn_b_in").reshape(2, P).T
    a["g_norm"] = g("L0_attn_g_norm").reshape(P, 1)
    a["A"], a["Bm"], a["Cm"] = g("L0_attn_A"), g("L0_attn_Bm"), g("L0_attn_Cm")
    a["Dv"] = g("L0_attn_Dv").reshape(P, 1)
    a["w_outT"] = g("L0_attn_w_out").T
    a["b_out"] = g("L0_attn_b_out").reshape(1, P)
    a["gw0"] = g("L0_ffn_gate_w").T
    a["gb0"] = g("L0_ffn_gate_b").reshape(1, NX0)
    a["ew0"] = g("L0_ffn_expert_w").transpose(1, 0, 2).reshape(P, NE0 * P)
    a["eb0"] = g("L0_ffn_expert_b")
    a["table"] = g("L1_attn_rpe_table")[:, TLEN - 1::-1, :].transpose(0, 2, 1).reshape(P, TLEN)
    for n in "qkvo":
        a[f"w{n}T"] = g(f"L1_attn_w{n}").T
    a["bq"], a["bk"] = g("L1_attn_bq").reshape(P, 1), g("L1_attn_bk").reshape(P, 1)
    a["bv"], a["bo"] = g("L1_attn_bv").reshape(1, P), g("L1_attn_bo").reshape(1, P)
    a["gw1"] = g("L1_ffn_gate_w").T
    a["gb1"] = g("L1_ffn_gate_b").reshape(1, NE1)
    w = [np.concatenate([g(f"L1_ffn_{n}"), g(f"L1_ffn_s{n}")[None]]) for n in ("w1", "w3", "w2")]
    b = [np.concatenate([g(f"L1_ffn_{n}"), g(f"L1_ffn_s{n}")[None]]) for n in ("b1", "b3", "b2")]
    a["ew1"] = np.concatenate([m.transpose(0, 2, 1) for m in (w[0][:, ::2], w[0][:, 1::2], w[1][:, ::2],
                                                            w[1][:, 1::2], w[2])], axis=2)
    a["eb1"] = np.stack([b[0][:, ::2], b[0][:, 1::2], b[1][:, ::2], b[1][:, 1::2]], axis=2)
    a["b2"] = b[2]
    return {k: np.ascontiguousarray(v) for k, v in a.items()}


def kernel(**inputs):
    import numpy as np
    import concourse.bacc as bacc
    from concourse.bass_utils import run_bass_kernel_spmd

    arrays = layouts(inputs, np)
    nc = bacc.Bacc("TRN2", target_bir_lowering=False, num_devices=1)
    d = {k: nc.dram_tensor(f"in_{k}", v.shape, F32, kind="ExternalInput").ap() for k, v in arrays.items()}
    out = nc.dram_tensor("out_x", (P, NT, P), F32, kind="ExternalOutput").ap()
    program(nc, d, out, 99)
    r = run_bass_kernel_spmd(nc, [{f"in_{k}": v for k, v in arrays.items()}], core_ids=[0])
    y = r.results[0]["out_x"]
    return y.reshape(U, NB, NC, 2, P).transpose(1, 2, 0, 3, 4).reshape(NB, SEQ, P)
```

```python
import concourse.bass as bass
from concourse import mybir
from contextlib import ExitStack

F32 = mybir.dt.float32
BF16 = mybir.dt.bfloat16
ALU = mybir.AluOpType
ACT = mybir.ActivationFunctionType
AX = mybir.AxisListType

P = 128
NB = 8
SEQ = 512
U = P // NB
NT = NB * SEQ // P
NC = NT // 2
BLK = 512
NBLK = NB * SEQ // BLK
TPB = BLK // P
NS = 64
HALF = NS // 2 * NB
HEADS = 16
HD = P // HEADS
NE0, NX0 = 8, 10
NE1 = 8
MODS = 6
LN_EPS, RMS_EPS = 1e-5, 1e-6
TLEN = 2 * SEQ - 1
LIMIT = 7.0
LOWEST = -3.4028234e38
ALPHA = 1.702


class Chain:

    def __init__(self, eng, sem):
        self.eng, self.sem, self.n = eng, sem, 0

    def add(self, ins):
        self.n += 1
        ins.then_inc(self.sem, 1)

    def wait(self):
        self.eng.wait_ge(self.sem, self.n)

    def __call__(self, ins):
        self.add(ins)
        self.wait()


class Roots:

    def __init__(self, asked, answered):
        self.asked, self.answered, self.n, self.served = asked, answered, 0, 0

    def rsqrt(self, dve, v, chain, val, root, tmp):
        self.n += 1
        v.tensor_scalar(tmp, val, 1.0, None, ALU.mult).then_inc(self.asked, 1)
        dve.wait_ge(self.answered, self.n)
        chain(v.reciprocal(root, root))
        chain(v.tensor_tensor(tmp, root, root, ALU.mult))
        chain(v.tensor_tensor(tmp, tmp, val, ALU.mult))
        chain(v.tensor_scalar(tmp, tmp, -0.5, 1.5, ALU.mult, ALU.add))
        chain(v.tensor_tensor(root, root, tmp, ALU.mult))

    def serve(self, act, nc, root, tmp):
        self.served += 1
        act.wait_ge(self.asked, self.served)
        nc.scalar.activation(root, tmp, ACT.Sqrt).then_inc(self.answered, 1)


def layer_norm(dve, v, chain, roots, src, out, n, stats, mv, rstd, tmp, scale, shift):
    for k in range(n):
        chain.add(v.bn_stats(stats[:, k, :], src[:, k, :]))
    chain.wait()
    for k in range(n):
        chain.add(v.bn_aggr(mv[:, k, :], stats[:, k, :]))
    chain.wait()
    chain(v.tensor_scalar(mv[:, 0:n, 1], mv[:, 0:n, 1], LN_EPS, None, ALU.add))
    roots.rsqrt(dve, v, chain, mv[:, 0:n, 1], rstd[:, 0:n], tmp[:, 0:n])
    for k in range(n):
        chain.add(v.tensor_scalar(out[:, k, :], src[:, k, :], mv[:, k, 0:1], rstd[:, k:k + 1],
                                  ALU.subtract, ALU.mult))
    chain.wait()
    chain(v.tensor_tensor(out[:, 0:n, :], out[:, 0:n, :], scale.unsqueeze(1).to_broadcast([P, n, P]), ALU.mult))
    chain(v.tensor_tensor(out[:, 0:n, :], out[:, 0:n, :], shift.unsqueeze(1).to_broadcast([P, n, P]), ALU.add))


def prologue(nc, d, keep, scan):
    x, mod, ident, ones = keep["x"], keep["mod"], keep["ident"], keep["ones"]
    with ExitStack() as ctx:
        sb = lambda name, shape, dt=F32: ctx.enter_context(nc.sbuf_tensor(name, shape, dt))
        sem = lambda name: ctx.enter_context(nc.semaphore(name))
        cT = sb("cT", [P, 2, NB])
        cth = sb("cth", [P, 2, NB])
        crep = sb("crep", [P, 2, U, NB])
        wmod = sb("wmod", [P, 2, MODS * P])
        guard = sb("guard", [P, 2, P])
        winT = sb("winT", [P, 2 * P])
        binc = sb("binc", [P, 2])
        binh = sb("binh", [P, 1])
        gn = sb("gn", [P, 1])
        cm = sb("cm", [P, NS])
        am = sb("am", [P, NS])
        csum = sb("csum", [P, NS])
        h = sb("h0", [P, NC, P])
        hT = sb("h0T", [P, NC * P])
        sq = sb("sq", [P, NC, P])
        stats = sb("stats0", [P, NC, 6])
        mv = sb("mv0", [P, NC, 2])
        rstd = sb("rstd0", [P, NC])
        rtmp = sb("rtmp0", [P, NC])
        ms = sb("ms", [P, NC])
        gate = sb("gate", [P, 2, BLK])
        gth = sb("gth", [P, 2, BLK])
        pm = [ctx.enter_context(nc.psum_tensor(f"pm{i}", [P, 512], F32)) for i in range(8)]
        x_in, w_in, zero, id_ready, v_chain = sem("x_in"), sem("w_in"), sem("zero"), sem("id_ready"), sem("v_chain0")
        c_tanh, c_rep, mod_ps, mod_sb = sem("c_tanh"), sem("c_rep"), sem("mod_ps"), sem("mod_sb")
        h_ready, hT_ps, hT_sb, proj_ps = sem("h_ready"), sem("hT_ps"), sem("hT_sb"), sem("proj_ps")
        proj_sb, gate_sb, gate_used, csum_ps = sem("proj_sb"), sem("gate_sb"), sem("gate_used"), sem("csum_ps")
        w_scaled = sem("w_scaled")
        roots = Roots(sem("var_ready0"), sem("root_ready0"))
        NBK = NC * P // BLK
        block = ctx.enter_context(nc.Block())

        @block.sync
        def _(sp):
            sp.dma_start(cT[:, :, :], d["cT"]).then_inc(w_in, 16)
            sp.dma_start(wmod[:, :, :], d["wmod"]).then_inc(w_in, 16)
            sp.dma_start(x[:, :, :], d["x"]).then_inc(x_in, 16)
            for dst, src in ((winT[:, :], d["w_inT"]), (binc[:, :], d["b_in"]), (gn[:, :], d["g_norm"]),
                             (cm[:, :], d["Cm"]), (am[:, :], d["A"]), (scan["Bm"][:, :], d["Bm"]),
                             (scan["Dv"][:, :], d["Dv"]), (scan["woT"][:, :], d["w_outT"]),
                             (scan["bo"][:, :], d["b_out"])):
                sp.dma_start(dst, src).then_inc(w_in, 16)

        ALL_W = 16 * 11

        @block.gpsimd
        def _(pool):
            nc.gpsimd.memset(ident[:, :], 0.0).then_inc(zero, 1)
            nc.gpsimd.memset(ones[:, :], 1.0).then_inc(id_ready, 1)
            pool.wait_ge(zero, 1)
            nc.gpsimd.affine_select(out=ident[:, :], in_=ident[:, :], compare_op=ALU.not_equal, fill=1.0,
                                    base=0, pattern=[[-1, P]], channel_multiplier=1).then_inc(id_ready, 1)

        @block.scalar
        def _(act):
            act.wait_ge(w_in, ALL_W)
            nc.scalar.activation(cth[:, :, :], cT[:, :, :], ACT.Tanh, scale=0.5).then_inc(c_tanh, 1)
            for n, (lo, hi) in enumerate(((0, 512), (512, 768)) * 2):
                act.wait_ge(mod_ps, n + 1)
                nc.scalar.copy(mod[:, n // 2, lo:hi], pm[n][:, 0:hi - lo]).then_inc(mod_sb, 1)
            roots.serve(act, nc, rstd[:, :], rtmp[:, :])
            roots.serve(act, nc, rstd[:, :], rtmp[:, :])
            for j in range(NBK):
                act.wait_ge(hT_ps, j + 1)
                nc.scalar.copy(hT[:, j * BLK:(j + 1) * BLK], pm[4 + j % 2][:, :]).then_inc(hT_sb, 1)
            for j in range(NBK):
                act.wait_ge(proj_ps, 2 * j + 1)
                nc.scalar.activation(scan["xp"][:, j * BLK:(j + 1) * BLK], pm[2 * (j % 2)][:, :], ACT.Identity,
                                     bias=binc[:, 0:1]).then_inc(proj_sb, 1)
                act.wait_ge(proj_ps, 2 * j + 2)
                if j >= 2:
                    act.wait_ge(gate_used, j - 1)
                nc.scalar.activation(gate[:, j % 2, :], pm[2 * (j % 2) + 1][:, :], ACT.Identity,
                                     bias=binc[:, 1:2]).then_inc(proj_sb, 1)
                act.wait_ge(w_scaled, 1)
                nc.scalar.activation(gth[:, j % 2, :], pm[2 * (j % 2) + 1][:, :], ACT.Tanh,
                                     bias=binh[:, 0:1], scale=0.5).then_inc(gate_sb, 1)

        @block.vector
        def _(dve):
            v = nc.vector
            chain = Chain(dve, v_chain)
            dve.wait_ge(c_tanh, 1)
            chain(v.scalar_tensor_tensor(cth[:, :, :], cth[:, :, :], 1.0, cT[:, :, :], ALU.add, ALU.mult))
            for l in range(2):
                v.tensor_scalar(crep[:, l, :, :], cth[:, l, :].unsqueeze(1).to_broadcast([P, U, NB]), 0.5, None,
                                ALU.mult).then_inc(c_rep, 1)
            chain(v.tensor_scalar(winT[:, :], winT[:, :], gn[:, 0:1], None, ALU.mult))
            chain(v.tensor_scalar(scan["woT"][:, :], scan["woT"][:, :], 0.5, None, ALU.mult))
            v.tensor_scalar(binh[:, :], binc[:, 1:2], 0.5, None, ALU.mult).then_inc(w_scaled, 1)
            chain(v.tensor_copy(scan["A"][:, :].rearrange("p (s b) -> p s b", b=NB),
                                am[:, :].unsqueeze(2).to_broadcast([P, NS, NB])))
            dve.wait_ge(csum_ps, 1)
            chain(v.tensor_copy(csum[:, :], pm[7][:, 0:NS]))
            dve.wait_ge(id_ready, 2)
            chain(v.tensor_tensor(scan["diagC"][:, :, :], ident[:, :].unsqueeze(1).to_broadcast([P, NS, P]),
                                  csum[:, :].unsqueeze(2).to_broadcast([P, NS, P]), ALU.mult))
            chain(v.memset(scan["hist"][:, 1, U - 1, :], 0.0))
            dve.wait_ge(mod_sb, 4)
            for l in range(2):
                for m in (1, 4):
                    chain(v.tensor_scalar(mod[:, l, m * P:(m + 1) * P], mod[:, l, m * P:(m + 1) * P], 1.0, None,
                                          ALU.add))
                for m in (2, 5):
                    g = mod[:, l, m * P:(m + 1) * P]
                    chain(v.tensor_scalar(guard[:, 0, :], g, 0.0, 2.0, ALU.is_ge, ALU.mult))
                    chain(v.scalar_tensor_tensor(guard[:, 1, :], g, -1.0, g, ALU.mult, ALU.max))
                    chain(v.tensor_scalar(guard[:, 1, :], guard[:, 1, :], 0.25, None, ALU.max))
                    chain(v.scalar_tensor_tensor(g, guard[:, 0, :], -1.0, guard[:, 1, :], ALU.add, ALU.mult))
            dve.wait_ge(x_in, 16)
            layer_norm(dve, v, chain, roots, x[:, :, :].rearrange("p (c o) e -> p c o e", o=2)[:, :, 0, :], h, NC,
                       stats, mv, rstd, rtmp, mod[:, 0, P:2 * P], mod[:, 0, 0:P])
            chain(v.tensor_tensor(sq[:, :, :], h[:, :, :], h[:, :, :], ALU.mult))
            chain(v.tensor_reduce(ms[:, :], sq[:, :, :], AX.X, ALU.add))
            chain(v.tensor_scalar(ms[:, :], ms[:, :], 1.0 / P, RMS_EPS, ALU.mult, ALU.add))
            roots.rsqrt(dve, v, chain, ms[:, :], rstd[:, :], rtmp[:, :])
            v.tensor_tensor(h[:, :, :], h[:, :, :], rstd[:, :].unsqueeze(2).to_broadcast([P, NC, P]),
                            ALU.mult).then_inc(h_ready, 1)
            for j in range(NBK):
                dve.wait_ge(gate_sb, j + 1)
                v.scalar_tensor_tensor(scan["gate"][:, j * BLK:(j + 1) * BLK], gth[:, j % 2, :], 1.0,
                                       gate[:, j % 2, :], ALU.add, ALU.mult).then_inc(gate_used, 1)

        @block.tensor
        def _(pe):
            mm = nc.tensor.matmul
            pe.wait_ge(w_in, ALL_W)
            pe.wait_ge(id_ready, 2)
            mm(pm[7][:, 0:NS], ones[:, :], cm[:, :], start=True, stop=True).then_inc(csum_ps, 1)
            pe.wait_ge(c_rep, 2)
            for n, (lo, hi) in enumerate(((0, 512), (512, 768)) * 2):
                mm(pm[n][:, 0:hi - lo], crep[:, n // 2, :, :].rearrange("p u b -> p (u b)"),
                   wmod[:, n // 2, lo:hi], start=True, stop=True).then_inc(mod_ps, 1)
            pe.wait_ge(h_ready, 1)
            for j in range(NBK):
                if j >= 2:
                    pe.wait_ge(hT_sb, j - 1)
                for q in range(TPB):
                    last = nc.tensor.transpose(pm[4 + j % 2][:, q * P:(q + 1) * P], h[:, j * TPB + q, :], ident[:, :])
                last.then_inc(hT_ps, 1)
            for j in range(NBK):
                pe.wait_ge(hT_sb, j + 1)
                for half in range(2):
                    if j == 0:
                        pe.wait_ge(mod_sb, 4)
                    if j >= 2:
                        pe.wait_ge(proj_sb, 2 * (j - 2) + half + 1)
                        pe.wait_ge(gate_sb, j - 1)
                    mm(pm[2 * (j % 2) + half][:, :], winT[:, half * P:(half + 1) * P], hT[:, j * BLK:(j + 1) * BLK],
                       start=True, stop=True).then_inc(proj_ps, 1)


def scan_phase(nc, d, keep, scan):
    x, mod, ones = keep["x"], keep["mod"], keep["ones"]
    A, Bm, Dv, xp, gate = scan["A"], scan["Bm"], scan["Dv"], scan["xp"], scan["gate"]
    hist, diagC, woT, bo = scan["hist"], scan["diagC"], scan["woT"], scan["bo"]
    S_ACT = 20
    with ExitStack() as ctx:
        sb = lambda name, shape, dt=F32: ctx.enter_context(nc.sbuf_tensor(name, shape, dt))
        sem = lambda name: ctx.enter_context(nc.semaphore(name))
        xb = sb("xb", [P, 2, U, NS * NB])
        xc = sb("xc", [P, 2, P])
        g = sb("g", [P, NS * NB])
        y2 = sb("y2", [P, P])
        yg = sb("yg", [P, P])
        upd = sb("upd", [P, P])
        zp = [ctx.enter_context(nc.psum_tensor(f"zp{i}", [P, 512], F32)) for i in range(2)]
        py = [ctx.enter_context(nc.psum_tensor(f"py{i}", [P, 512], F32)) for i in range(2)]
        po = ctx.enter_context(nc.psum_tensor("po", [P, 512], F32))
        decayed, z_ready, h_done = sem("decayed"), sem("z_ready"), sem("h_done")
        xb_act, xb_pool, xb_used = sem("xb_act"), sem("xb_pool"), sem("xb_used")
        xc_ready = sem("xc_ready")
        y_ready, yd_ready, yg_ready, out_ready, upd_ready, x_updated = (
            sem("y_ready"), sem("yd_ready"), sem("yg_ready"), sem("out_ready"), sem("upd_ready"), sem("x_updated"))
        block = ctx.enter_context(nc.Block())
        OUT_AT = 13
        N_POOL = NS - S_ACT

        def chunks(eng, body):
            body(0, 0, True)
            body(1, 1, False)
            with eng.Fori(1, NC // 2) as i:
                body(2 * i, 0, False)
                body(2 * i + 1, 1, False)

        def xb_slot(s, par):
            return xb[:, par, :, s * NB:(s + 1) * NB]

        def xp_chunk(c):
            return xp[:, bass.ds(c * P, P)] if not isinstance(c, int) else xp[:, c * P:(c + 1) * P]

        @block.vector
        def _(dve):
            v = nc.vector

            def output(c):
                dve.wait_ge(y_ready, c + 1)
                par = output.par
                xs = xp_chunk(c)
                v.scalar_tensor_tensor(y2[:, :], xs, Dv[:, 0:1], py[par][:, 0:P], ALU.mult, ALU.add)\
                 .then_inc(yd_ready, 1)
                dve.wait_ge(yd_ready, c + 1)
                gs = gate[:, bass.ds(c * P, P)] if not isinstance(c, int) else gate[:, c * P:(c + 1) * P]
                v.tensor_tensor(yg[:, :], y2[:, :], gs, ALU.mult).then_inc(yg_ready, 1)

            def add_output(c):
                dve.wait_ge(out_ready, c + 1)
                v.tensor_tensor(upd[:, :], po[:, 0:P], mod[:, 0, 2 * P:3 * P], ALU.mult).then_inc(upd_ready, 1)
                dve.wait_ge(upd_ready, c + 1)
                xs = x[:, bass.ds(2 * c, 2), :] if not isinstance(c, int) else x[:, 2 * c:2 * c + 2, :]
                v.tensor_tensor(xs, xs, upd[:, :].unsqueeze(1).to_broadcast([P, 2, P]), ALU.add)\
                 .then_inc(x_updated, 1)

            def body(c, par, first):
                dve.wait_ge(xb_act, S_ACT * (c + 1))
                dve.wait_ge(xb_pool, N_POOL * (c + 1))
                for u in range(U):
                    prev = hist[:, par, u - 1, :] if u else hist[:, 1 - par, U - 1, :]
                    step = c * U + u
                    for j in range(2):
                        lo, hi = j * HALF, (j + 1) * HALF
                        if not (first and u == 0):
                            dve.wait_ge(h_done, 2 * step + j - 1)
                        v.tensor_tensor(g[:, lo:hi], prev[:, lo:hi], A[:, lo:hi], ALU.mult).then_inc(decayed, 1)
                    for j in range(2):
                        lo, hi = j * HALF, (j + 1) * HALF
                        dve.wait_ge(decayed, 2 * step + j + 1)
                        ins = v.tensor_tensor(zp[j][:, 0:HALF], g[:, lo:hi], xb[:, par, u, lo:hi], ALU.add)
                        ins.then_inc(z_ready, 1)
                    if not first and u == OUT_AT:
                        output.par = 1 - par
                        output(c - 1)
                    if not first and u == U - 1:
                        add_output(c - 1)

            chunks(dve, body)
            output.par = 1
            output(NC - 1)
            add_output(NC - 1)
            dve.wait_ge(x_updated, NC)

        def make_xb(eng, op, states, c, par, ready):
            for s in states:
                op(xb_slot(s, par), xp_chunk(c).rearrange("p (u b) -> p u b", b=NB), Bm[:, s:s + 1]).then_inc(ready, 1)

        @block.scalar
        def _(act):
            def op(out, in_, scale):
                return nc.scalar.activation(out, in_, ACT.Copy, scale=scale)

            make_xb(act, op, range(S_ACT), 0, 0, xb_act)
            make_xb(act, op, range(S_ACT), 1, 1, xb_act)

            def body(c, par, first):
                made = 0
                for u in range(U):
                    step = c * U + u
                    if not first and u == 0:
                        pass
                    for j in range(2):
                        act.wait_ge(z_ready, 2 * step + j + 1)
                        if u == 0 and j == 0 and not (isinstance(c, int) and c < 2):
                            act.wait_ge(y_ready, c - 1)
                        nc.scalar.activation(hist[:, par, u, j * HALF:(j + 1) * HALF], zp[j][:, 0:HALF], ACT.Tanh)\
                          .then_inc(h_done, 1)
                    if not (isinstance(c, int) and c == 0):
                        upto = S_ACT * (u + 1) // U
                        make_next(c, par, range(made, upto), u)
                        made = upto

            def make_next(c, par, states, u):
                if u == 0:
                    act.wait_ge(z_ready, 2 * U * c)
                make_xb(act, op, states, c + 1, 1 - par, xb_act)

            body(0, 0, True)
            body(1, 1, False)
            with act.Fori(1, NC // 2 - 1) as i:
                body(2 * i, 0, False)
                body(2 * i + 1, 1, False)
            made_last = NC - 2
            body(made_last, 0, False)
            for u in range(U):
                for j in range(2):
                    step = (NC - 1) * U + u
                    act.wait_ge(z_ready, 2 * step + j + 1)
                    if u == 0 and j == 0:
                        act.wait_ge(y_ready, NC - 2)
                    nc.scalar.activation(hist[:, 1, u, j * HALF:(j + 1) * HALF], zp[j][:, 0:HALF], ACT.Tanh)\
                      .then_inc(h_done, 1)

        @block.gpsimd
        def _(pool):
            def chunk(c, par, slot_used):
                if slot_used:
                    pool.wait_ge(z_ready, 2 * U * (c - 1))
                nc.gpsimd.tensor_copy(xc[:, par, :], xp_chunk(c)).then_inc(xc_ready, 1)
                pool.wait_ge(xc_ready, c + 1)
                nc.gpsimd.tensor_tensor(xb_slot(S_ACT, par), xc[:, par, :].rearrange("p (u b) -> p u b", b=NB),
                                        Bm[:, S_ACT:S_ACT + 1].unsqueeze(1).to_broadcast([P, U, NB]), ALU.mult)\
                  .then_inc(xb_pool, 1)
                for s in range(S_ACT + 1, NS):
                    nc.gpsimd.tensor_scalar(xb_slot(s, par), xc[:, par, :].rearrange("p (u b) -> p u b", b=NB),
                                            Bm[:, s:s + 1], 1.0, ALU.mult, ALU.mult).then_inc(xb_pool, 1)

            chunk(0, 0, False)
            chunk(1, 1, False)
            with pool.Fori(1, NC // 2) as i:
                chunk(2 * i, 0, True)
                chunk(2 * i + 1, 1, True)

        @block.tensor
        def _(pe):
            mm = nc.tensor.matmul

            def body(c, par, first):
                pe.wait_ge(h_done, 2 * U * (c + 1))
                if not (isinstance(c, int) and c < 2):
                    pe.wait_ge(yd_ready, c - 1)
                for s in range(NS):
                    last = mm(py[par][:, 0:P], diagC[:, s, :], hist[:, par, :, s * NB:(s + 1) * NB],
                              start=(s == 0), stop=(s == NS - 1))
                last.then_inc(y_ready, 1)
                pe.wait_ge(yg_ready, c + 1)
                if not first:
                    pe.wait_ge(upd_ready, c)
                mm(po[:, 0:P], yg[:, :], woT[:, :], start=True, stop=False)
                mm(po[:, 0:P], ones[0:1, :], bo[:, :], start=False, stop=True).then_inc(out_ready, 1)

            chunks(pe, body)


class Normed:

    def __init__(self, nc, sb, sem, keep, layer, half, hT, banks, tag):
        self.nc, self.keep, self.hT, self.banks = nc, keep, hT, banks
        self.shift = keep["mod"][:, layer, (3 * half) * P:(3 * half + 1) * P]
        self.scale = keep["mod"][:, layer, (3 * half + 1) * P:(3 * half + 2) * P]
        self.h = sb(f"h{tag}", [P, NT, P])
        self.stats = sb(f"stats{tag}", [P, NT, 6])
        self.mv = sb(f"mv{tag}", [P, NT, 2])
        self.rstd = sb(f"rstd{tag}", [P, NT])
        self.tmp = sb(f"rtmp{tag}", [P, NT])
        self.h_ready, self.t_ready, self.hT_ready = sem(f"h_ready{tag}"), sem(f"t_ready{tag}"), sem(f"hT_ready{tag}")
        self.roots = Roots(sem(f"var_ready{tag}"), sem(f"root_ready{tag}"))

    def vector(self, dve, chain):
        v = self.nc.vector
        layer_norm(dve, v, chain, self.roots, self.keep["x"], self.h, NT, self.stats, self.mv, self.rstd, self.tmp,
                   self.scale, self.shift)
        v.sem_inc(self.h_ready, 1)

    def scalar(self, act):
        self.roots.serve(act, self.nc, self.rstd[:, :], self.tmp[:, :])
        for j in range(NBLK):
            act.wait_ge(self.t_ready, j + 1)
            self.nc.scalar.copy(self.hT[:, j * BLK:(j + 1) * BLK], self.banks[j % 2][:, :]).then_inc(self.hT_ready, 1)

    def tensor(self, pe):
        pe.wait_ge(self.h_ready, 1)
        for j in range(NBLK):
            if j >= 2:
                pe.wait_ge(self.hT_ready, j - 1)
            for q in range(TPB):
                last = self.nc.tensor.transpose(self.banks[j % 2][:, q * P:(q + 1) * P], self.h[:, j * TPB + q, :],
                                                self.keep["ident"][:, :])
            last.then_inc(self.t_ready, 1)


def softmax_probs(dve, nc, chain, probs, logits_ps, bias, top, n, asked, answered):
    v = nc.vector
    wide = lambda t: t.unsqueeze(2).to_broadcast([P, NT, n])
    if bias is None:
        chain(v.tensor_copy(probs, logits_ps))
    else:
        chain(v.tensor_tensor(probs, logits_ps, bias.unsqueeze(1).to_broadcast([P, NT, n]), ALU.add))
    chain(v.tensor_reduce(top, probs, AX.X, ALU.max))
    v.tensor_tensor(probs, probs, wide(top), ALU.subtract).then_inc(asked, 1)
    dve.wait_ge(answered, 1)
    chain(v.tensor_reduce(top, probs, AX.X, ALU.add))
    chain(v.reciprocal(top, top))
    chain(v.tensor_tensor(probs, probs, wide(top), ALU.mult))


def first_of_max(nc, chain, keys, rank, hot, top, n):
    v = nc.vector
    wide = lambda t: t.unsqueeze(2).to_broadcast([P, NT, n])
    chain(v.tensor_reduce(top, keys, AX.X, ALU.max))
    chain(v.tensor_tensor(hot, keys, wide(top), ALU.is_equal))
    chain(v.tensor_tensor(hot, hot, rank.unsqueeze(1).to_broadcast([P, NT, n]), ALU.mult))
    chain(v.tensor_reduce(top, hot, AX.X, ALU.max))
    chain(v.tensor_tensor(hot, hot, wide(top), ALU.is_equal))


def experts0(nc, d, keep):
    x, mod, ident = keep["x"], keep["mod"], keep["ident"]
    with ExitStack() as ctx:
        sb = lambda name, shape, dt=F32: ctx.enter_context(nc.sbuf_tensor(name, shape, dt))
        sem = lambda name: ctx.enter_context(nc.semaphore(name))
        pm = [ctx.enter_context(nc.psum_tensor(f"px{i}", [P, 512], F32)) for i in range(8)]
        hT = sb("hTx", [P, NT * P])
        W = sb("W0", [P, NE0 * P])
        gw = sb("gw0", [P, NX0])
        gb = sb("gb0", [P, NX0])
        eb = sb("eb0", [NE0, P])
        rank = sb("rank0", [P, NX0])
        ranki = sb("ranki0", [P, NX0], mybir.dt.int32)
        probs = sb("probs0", [P, NT, NX0])
        hot = sb("hot0", [P, 2, NT, NX0])
        top = sb("top0", [P, NT])
        den = sb("den0", [P, NT])
        cw = sb("cw0", [P, NT, NE0])
        cwT = sb("cwT0", [NE0, NT * P])
        acc = sb("acc0", [P, 2, 2, P])
        w_in, v_chain, ranks = sem("w_inx"), sem("v_chainx"), sem("ranks0")
        logits_ready, exp_asked, exp_done = sem("logits_ready0"), sem("exp_asked0"), sem("exp_done0")
        cw_ready, cwT_ps, cwT_ready = sem("cw_ready0"), sem("cwT_ps0"), sem("cwT_ready0")
        y_ready, y_used, seeded, x_added = sem("y_readyx"), sem("y_usedx"), sem("seeded0"), sem("x_added0")
        norm = Normed(nc, sb, sem, keep, 0, 1, hT, pm[0:2], "x")
        block = ctx.enter_context(nc.Block())

        @block.sync
        def _(sp):
            for dst, src in ((gw[:, :], d["gw0"]), (gb[:, :], d["gb0"].to_broadcast([P, NX0])),
                             (W[:, :], d["ew0"]), (eb[:, :], d["eb0"])):
                sp.dma_start(dst, src).then_inc(w_in, 16)

        @block.gpsimd
        def _(pool):
            nc.gpsimd.iota(ranki[:, :], pattern=[[-1, NX0]], base=NX0, channel_multiplier=0).then_inc(ranks, 1)
            pool.wait_ge(ranks, 1)
            nc.gpsimd.tensor_copy(rank[:, :], ranki[:, :]).then_inc(ranks, 1)

        @block.scalar
        def _(act):
            norm.scalar(act)
            act.wait_ge(exp_asked, 1)
            nc.scalar.activation(probs[:, :, :], probs[:, :, :], ACT.Exp).then_inc(exp_done, 1)
            for j in range(NBLK):
                act.wait_ge(cwT_ps, j + 1)
                nc.scalar.copy(cwT[:, j * BLK:(j + 1) * BLK], pm[2 + j % 2][0:NE0, :]).then_inc(cwT_ready, 1)
            for k in range(NT):
                act.wait_ge(y_ready, k + 1)
                if k >= 4:
                    act.wait_ge(x_added, k // 2 - 1)
                nc.scalar.copy(acc[:, (k // 2) % 2, k % 2, :], pm[4 + k % 2][:, 0:P]).then_inc(seeded, 1)

        @block.vector
        def _(dve):
            v = nc.vector
            chain = Chain(dve, v_chain)
            norm.vector(dve, chain)
            dve.wait_ge(w_in, 16 * 4)
            dve.wait_ge(ranks, 2)
            dve.wait_ge(logits_ready, 1)
            softmax_probs(dve, nc, chain, probs[:, :, :], pm[4][:, 0:NT * NX0].rearrange("p (k e) -> p k e", e=NX0),
                          gb[:, :], top[:, :], NX0, exp_asked, exp_done)
            wide = lambda t: t.unsqueeze(2).to_broadcast([P, NT, NX0])
            chain(v.tensor_copy(hot[:, 1, :, :], probs[:, :, :]))
            first_of_max(nc, chain, hot[:, 1, :, :], rank[:, :], hot[:, 0, :, :], top[:, :], NX0)
            chain(v.scalar_tensor_tensor(hot[:, 1, :, :], hot[:, 0, :, :], -4.0, probs[:, :, :], ALU.mult, ALU.add))
            chain(v.tensor_tensor(hot[:, 0, :, :], hot[:, 0, :, :], probs[:, :, :], ALU.mult))
            chain(v.tensor_copy(cw[:, :, :], hot[:, 0, :, 0:NE0]))
            first_of_max(nc, chain, hot[:, 1, :, :], rank[:, :], hot[:, 0, :, :], top[:, :], NX0)
            chain(v.tensor_tensor(hot[:, 0, :, :], hot[:, 0, :, :], probs[:, :, :], ALU.mult))
            chain(v.tensor_tensor(cw[:, :, :], cw[:, :, :], hot[:, 0, :, 0:NE0], ALU.add))
            chain(v.tensor_reduce(den[:, :], cw[:, :, :], AX.X, ALU.add))
            chain(v.tensor_scalar(top[:, :], den[:, :], 0.0, None, ALU.is_le))
            chain(v.tensor_tensor(den[:, :], den[:, :], top[:, :], ALU.add))
            chain(v.reciprocal(den[:, :], den[:, :]))
            chain(v.tensor_tensor(cw[:, :, :], cw[:, :, :], den[:, :].unsqueeze(2).to_broadcast([P, NT, NE0]),
                                  ALU.mult))
            v.sem_inc(cw_ready, 1)
            for k2 in range(0, NT, 2):
                for e in range(NE0):
                    for k in (k2, k2 + 1):
                        a, par = k % 2, (k // 2) % 2
                        if e == 0:
                            dve.wait_ge(seeded, k + 1)
                        src = pm[2 * a + e // 4][:, (e % 4) * P:(e % 4 + 1) * P]
                        ins = v.scalar_tensor_tensor(acc[:, par, a, :], src, cw[:, k, e:e + 1], acc[:, par, a, :],
                                                     ALU.mult, ALU.add)
                        ins.then_inc(y_used, 1)
                    if e < NE0 - 1:
                        dve.wait_ge(y_used, k2 * NE0 + 2 * (e + 1))
                par = (k2 // 2) % 2
                dve.wait_ge(y_used, (k2 + 2) * NE0)
                chain(v.tensor_tensor(acc[:, par, :, :], acc[:, par, :, :],
                                      mod[:, 0, 5 * P:6 * P].unsqueeze(1).to_broadcast([P, 2, P]), ALU.mult))
                v.tensor_tensor(x[:, k2:k2 + 2, :], x[:, k2:k2 + 2, :], acc[:, par, :, :], ALU.add)\
                 .then_inc(x_added, 1)

        @block.tensor
        def _(pe):
            mm = nc.tensor.matmul
            norm.tensor(pe)
            pe.wait_ge(w_in, 16 * 4)
            pe.wait_ge(norm.hT_ready, NBLK)
            for k in range(NT):
                last = mm(pm[4][:, k * NX0:(k + 1) * NX0], hT[:, k * P:(k + 1) * P], gw[:, :], start=True, stop=True)
            last.then_inc(logits_ready, 1)
            pe.wait_ge(cw_ready, 1)
            for j in range(NBLK):
                if j >= 2:
                    pe.wait_ge(cwT_ready, j - 1)
                for q in range(TPB):
                    last = nc.tensor.transpose(pm[2 + j % 2][0:NE0, q * P:(q + 1) * P], cw[:, j * TPB + q, :],
                                               ident[:, :])
                last.then_inc(cwT_ps, 1)
            pe.wait_ge(cwT_ready, NBLK)
            for k in range(NT):
                a = k % 2
                if k >= 2:
                    pe.wait_ge(y_used, (k - a) * NE0)
                for half in range(2):
                    mm(pm[2 * a + half][:, :], hT[:, k * P:(k + 1) * P], W[:, half * 512:(half + 1) * 512],
                       start=True, stop=True)
                mm(pm[4 + a][:, 0:P], cwT[:, k * P:(k + 1) * P], eb[:, :], start=True, stop=True).then_inc(y_ready, 1)


QK_TERMS = (((0, 0), (0, 1)), ((1, 1), (0, 1)), ((0, 2), (2, 0)))
REL_TERMS = (((0, 0, 1, 1), (0, 1, 0, 1)), ((0, 1, 2, 2), (2, 2, 0, 1)))
PARTS = 3
TOK = NB * SEQ
V4 = 4
W4 = U // V4
NG4 = NT * W4
KEY_SLOTS = QK_TERMS[0][1] + QK_TERMS[2][1]
TABLE_SLOTS = REL_TERMS[0][1] + REL_TERMS[1][1]
TWIN = TLEN - 2 * (V4 - 1)
TROW = TLEN + 1
JT = SEQ // P


def attention_inputs(nc, d, keep, vals, scratch):
    with ExitStack() as ctx:
        sb = lambda name, shape, dt=F32: ctx.enter_context(nc.sbuf_tensor(name, shape, dt))
        sem = lambda name: ctx.enter_context(nc.semaphore(name))
        pm = [ctx.enter_context(nc.psum_tensor(f"pi{i}", [P, 512], F32)) for i in range(8)]
        hT = sb("hTi", [P, TOK])
        wq, wk, wv = sb("wq", [P, P]), sb("wk", [P, P]), sb("wv", [P, P])
        bq, bk, bks, bv = sb("bq", [P, 1]), sb("bk", [P, 1]), sb("bks", [P, 1]), sb("bv", [P, P])
        table = sb("table", [P, TROW])
        tparts = sb("tparts", [P, PARTS, TROW], BF16)
        rest = sb("rest", [P, 2, BLK])
        nat = sb("nat", [P, 2, PARTS, BLK], BF16)
        qparts = sb("qparts", [P, PARTS, W4, V4, NB, NT], BF16)
        kparts = sb("kparts", [P, PARTS, TOK], BF16)
        hTb = sb("hTb", [P, TOK])
        w_in, t_in, v_chain, bias_ready = sem("w_ini"), sem("t_in"), sem("v_chaini"), sem("bias_ready")
        proj_ready, value_ready, cut_ready = sem("proj_readyi"), sem("value_ready"), sem("cut_ready")
        q_placed, by_seq = sem("q_placed"), sem("by_seq")
        v_ready, v_done, t_cut, stored = sem("v_ready"), sem("v_done"), sem("t_cut"), sem("stored_parts")
        norm = Normed(nc, sb, sem, keep, 1, 0, hT, pm[0:2], "i")
        block = ctx.enter_context(nc.Block())
        NPROJ = 2 * NBLK

        @block.sync
        def _(sp):
            sp.dma_start(table[:, 0:TLEN], d["table"]).then_inc(t_in, 16)
            for dst, src in ((wq[:, :], d["wqT"]), (wk[:, :], d["wkT"]), (wv[:, :], d["wvT"]), (bq[:, :], d["bq"]),
                             (bk[:, :], d["bk"]), (bv[:, :], d["bv"].to_broadcast([P, P]))):
                sp.dma_start(dst, src).then_inc(w_in, 16)
            sp.wait_ge(t_cut, 1)
            for slot, t in enumerate(TABLE_SLOTS):
                sp.dma_start(scratch["t"][:, slot, :, 0:TLEN], tparts[:, t, 0:TLEN]).then_inc(stored, 16)
            sp.wait_ge(q_placed, NBLK)
            for t in range(PARTS):
                sp.dma_start(scratch["q"][t, :, :], qparts[:, t, :, :, :, :].rearrange("p w v b k -> p (w v b k)"))\
                  .then_inc(stored, 16)
            sp.wait_ge(cut_ready, NPROJ)
            for slot, t in enumerate(KEY_SLOTS):
                sp.dma_start(scratch["k"][:, slot, :, :], kparts[:, t, :]).then_inc(stored, 16)
            sp.wait_ge(stored, 16 * (len(TABLE_SLOTS) + PARTS + len(KEY_SLOTS)))

        @block.scalar
        def _(act):
            norm.scalar(act)
            act.wait_ge(w_in, 16 * 6)
            act.wait_ge(bias_ready, 1)
            for n in range(NPROJ):
                par, j = n % 2, n % NBLK
                is_q = n < NBLK
                act.wait_ge(proj_ready, n + 1)
                if n >= 2:
                    act.wait_ge(cut_ready, n - 1)
                nc.scalar.activation(rest[:, par, :], pm[2 + par][:, :], ACT.Identity,
                                     bias=bq[:, 0:1] if is_q else bks[:, 0:1],
                                     scale=1.0 if is_q else HD ** -0.5).then_inc(value_ready, 1)
                if is_q:
                    act.wait_ge(cut_ready, n + 1)
                    for t in range(PARTS):
                        last = nc.scalar.copy(
                            qparts[:, t, :, :, :, j * TPB:(j + 1) * TPB].rearrange("p w v b k -> p k (w v b)"),
                            nat[:, par, t, :].rearrange("p (k c) -> p k c", c=P))
                    last.then_inc(q_placed, 1)

        @block.vector
        def _(dve):
            v = nc.vector
            chain = Chain(dve, v_chain)
            dve.wait_ge(w_in, 16 * 6)
            v.tensor_scalar(bks[:, :], bk[:, :], HD ** -0.5, None, ALU.mult).then_inc(bias_ready, 1)
            dve.wait_ge(t_in, 16)
            T = slice(0, TLEN)
            chain(v.tensor_copy(tparts[:, 0, T], table[:, T]))
            chain(v.tensor_tensor(table[:, T], table[:, T], tparts[:, 0, T], ALU.subtract))
            chain(v.tensor_copy(tparts[:, 1, T], table[:, T]))
            v.tensor_tensor(tparts[:, 2, T], table[:, T], tparts[:, 1, T], ALU.subtract).then_inc(t_cut, 1)
            norm.vector(dve, chain)
            for n in range(NPROJ):
                par = n % 2
                dve.wait_ge(value_ready, n + 1)
                j = n % NBLK
                p0, p1, p2 = (nat[:, par, t, :] if n < NBLK else kparts[:, t, j * BLK:(j + 1) * BLK]
                              for t in range(PARTS))
                if 2 <= n < NBLK:
                    dve.wait_ge(q_placed, n - 1)
                chain(v.tensor_copy(p0, rest[:, par, :]))
                chain(v.tensor_tensor(rest[:, par, :], rest[:, par, :], p0, ALU.subtract))
                chain(v.tensor_copy(p1, rest[:, par, :]))
                v.tensor_tensor(p2, rest[:, par, :], p1, ALU.subtract).then_inc(cut_ready, 1)
            for m in range(JT * NB // TPB):
                dve.wait_ge(v_ready, m + 1)
                v.tensor_tensor(vals[:, m * TPB:(m + 1) * TPB, :], pm[4 + m % 2][:, :].rearrange("p (q e) -> p q e", q=TPB),
                                bv[:, :].unsqueeze(1).to_broadcast([P, TPB, P]), ALU.add).then_inc(v_done, 1)

        @block.gpsimd
        def _(pool):
            for j in range(NBLK):
                pool.wait_ge(norm.hT_ready, j + 1)
                for c in range(2):
                    src = hT[:, (2 * j + c) * 2 * P:(2 * j + c + 1) * 2 * P].rearrange("p (o u b) -> p o u b", o=2, u=U)
                    dst = hTb[:, :].rearrange("p (b c u o) -> p c o u b", b=NB, u=U, o=2)[:, 2 * j + c, :, :, :]
                    nc.gpsimd.tensor_copy(dst, src).then_inc(by_seq, 1)

        @block.tensor
        def _(pe):
            mm = nc.tensor.matmul
            norm.tensor(pe)
            pe.wait_ge(w_in, 16 * 6)
            pe.wait_ge(norm.hT_ready, NBLK)
            for n in range(NPROJ):
                j = n % NBLK
                if n >= 2:
                    pe.wait_ge(value_ready, n - 1)
                if n == NBLK:
                    pe.wait_ge(by_seq, 2 * NBLK)
                w, src = (wq, hT) if n < NBLK else (wk, hTb)
                mm(pm[2 + n % 2][:, :], w[:, :], src[:, j * BLK:(j + 1) * BLK], start=True, stop=True)\
                  .then_inc(proj_ready, 1)
            for m in range(JT * NB // TPB):
                if m >= 2:
                    pe.wait_ge(v_done, m - 1)
                for q in range(TPB):
                    jt, b = divmod(m * TPB + q, NB)
                    last = mm(pm[4 + m % 2][:, q * P:(q + 1) * P], hTb[:, b * SEQ + jt * P:b * SEQ + (jt + 1) * P],
                              wv[:, :], start=True, stop=True)
                last.then_inc(v_ready, 1)


def attention(nc, d, keep, vals, scratch, ctxt):
    ident = keep["ident"]
    GRP = 4
    BG = NB // 2
    RING = 4
    CTX = GRP * U * BG
    STEPS = 2 * NT
    with ExitStack() as ctx:
        sb = lambda name, shape, dt=F32: ctx.enter_context(nc.sbuf_tensor(name, shape, dt))
        sem = lambda name: ctx.enter_context(nc.semaphore(name))
        qs = [[sb(f"qs{p}{m}", [P, U, NB, NT], BF16) for m in range(len(QK_TERMS))] for p in range(2)]
        qr = [[sb(f"qr{p}{m}", [P, W4, V4, NB, NT], BF16) for m in range(len(REL_TERMS))] for p in range(2)]
        ks = [[sb(f"ks{p}{m}", [P, SEQ], BF16) for m in range(2)] for p in range(2)]
        tb = [[sb(f"tb{p}{m}", [P, TWIN], BF16) for m in range(len(REL_TERMS))] for p in range(2)]
        vh = sb("vh", [P, 2, JT, NB, HD])
        own2 = sb("own2", [P, 4 * BG])
        own = sb("own", [P, BG])
        same_d = sb("same_d", [P, HD])
        masked = sb("masked", [P, 2, GRP * U, NB])
        prob = [sb(f"prob{i}", [P, SEQ]) for i in range(2)]
        probT = [sb(f"probT{i}", [P, JT, GRP * P]) for i in range(2)]
        ntop = sb("ntop", [P, NT])
        rsum = sb("rsum", [P, 2, NT])
        score_ps = [ctx.enter_context(nc.psum_tensor(f"score{i}", [P, 512], F32)) for i in range(RING)]
        turned_ps = [ctx.enter_context(nc.psum_tensor(f"turned{i}", [P, 512], F32)) for i in range(2)]
        mixed_ps = [ctx.enter_context(nc.psum_tensor(f"mixed{i}", [P, 512], F32)) for i in range(2)]
        mask_zeroed = sem("mask_zeroed")
        zeroed, mask_ready, head_in, v_head = [sem("zeroed0"), sem("zeroed1")], sem("mask_ready"), [sem("head_in0"), sem("head_in1")], sem("v_head")
        scores, top_ready, prob_ready, turned, turned_sb = (sem("scores"), sem("top_ready"), sem("prob_ready"),
                                                            sem("turned"), sem("turned_sb"))
        mixed, masked_ready, untangled, rinv_ready, ctx_ready = (
            sem("mixed"), sem("masked_ready"), sem("untangled"), sem("rinv_ready"), sem("ctx_ready"))
        block = ctx.enter_context(nc.Block())
        PS = P * TOK

        def load_head(eng, p, h, first=False):
            n = 0

            def start(dst, base, dims):
                nonlocal n
                src = bass.AP(base.tensor, base.offset + dims[0], dims[1])
                eng.dma_start(dst, src).then_inc(head_in[p], 16)
                n += 1

            for m in range(len(REL_TERMS)):
                start(tb[p][m][:, :], scratch["t"],
                      (h * (len(TABLE_SLOTS) * HD * TROW) + m * 4 * HD * TROW,
                       [[2, V4], [TROW, 4 * HD], [1, TWIN]]))
            for m in range(2):
                start(ks[p][m][:, :], scratch["k"],
                      (h * (len(KEY_SLOTS) * HD * TOK) + m * 2 * HD * TOK, [[SEQ, NB], [TOK, 2 * HD], [1, SEQ]]))
            if first:
                eng.wait_ge(zeroed[p], len(QK_TERMS) + len(REL_TERMS))
            for m, ((t0, t1), _) in enumerate(QK_TERMS):
                for b in range(NB):
                    start(qs[p][m][16 * b:16 * b + 16, :, b, :], scratch["q"],
                          (h * (HD * TOK) + t0 * PS + b * NT,
                           [[(t1 - t0) * PS, 2], [TOK, HD], [NB * NT, U], [1, NT]]))
            for m, (ts, _) in enumerate(REL_TERMS):
                for v in range(V4):
                    for a in range(2):
                        at = 32 * (V4 - 1 - v) + 16 * a
                        start(qr[p][m][at:at + 16, :, v, :, :].rearrange("p w b k -> p w (b k)"), scratch["q"],
                              (h * (HD * TOK) + ts[2 * a] * PS + v * NB * NT,
                               [[(ts[2 * a + 1] - ts[2 * a]) * PS, 2], [TOK, HD], [V4 * NB * NT, W4], [1, NB * NT]]))
            return n

        counted = [0]

        @block.sync
        def _(sp):
            counted[0] = load_head(sp, 0, 0, True)
            load_head(sp, 1, 1, True)
            with sp.Fori(1, HEADS // 2) as i:
                for p in range(2):
                    sp.wait_ge(scores, (2 * i - 1 + p) * NT)
                    load_head(sp, p, 2 * i + p)

        ARRIVED = 16 * counted[0]

        def before(i, K):
            return K >= 0 or not (isinstance(i, int) and i == 0)

        @block.gpsimd
        def _(pool):
            for p in range(2):
                for t in qr[p]:
                    nc.gpsimd.memset(t[:, :, :, :, :], 0.0).then_inc(zeroed[p], 1)
            nc.gpsimd.memset(masked[:, :, :, :], 0.0).then_inc(mask_zeroed, 1)

            def head(p, h, used):
                if used:
                    pool.wait_ge(mixed, (h - 1) * (NT // GRP))
                src = vals[:, :, bass.ds(h * HD, HD)] if not isinstance(h, int) else vals[:, :, h * HD:(h + 1) * HD]
                nc.gpsimd.tensor_copy(vh[:, p, :, :, :].rearrange("p j b d -> p (j b) d"), src).then_inc(v_head, 1)

            head(0, 0, False)
            head(1, 1, False)
            with pool.Fori(1, HEADS // 2) as i:
                head(0, 2 * i, True)
                head(1, 2 * i + 1, True)

        @block.tensor
        def _(pe):
            mm = nc.tensor.matmul

            def score(i, K):
                p, k = divmod(K, NT)
                if k == 0:
                    pe.wait_ge(head_in[p], ARRIVED * (i + 1))
                out = score_ps[K % RING]
                if before(i, K - RING):
                    pe.wait_ge(prob_ready, i * STEPS + K + 1 - RING)
                c, o = divmod(k, 2)
                for m in range(len(REL_TERMS)):
                    for w in range(W4):
                        s = SEQ - 1 - 2 * U * c - o - 2 * V4 * w - 2 * (V4 - 1)
                        mm(out[32 * w:32 * w + 32, :],
                           qr[p][m][:, w, :, :, k].rearrange("p v b -> p (v b)"), tb[p][m][:, s:s + SEQ],
                           start=(m == 0), stop=False)
                for m in range(len(QK_TERMS)):
                    last = mm(out[:, :], qs[p][m][:, :, :, k].rearrange("p u b -> p (u b)"), ks[p][m // 2][:, :],
                              start=False, stop=(m == len(QK_TERMS) - 1))
                last.then_inc(scores, 1)

            def turn(i, K):
                pe.wait_ge(prob_ready, i * STEPS + K + 1)
                if before(i, K - 2):
                    pe.wait_ge(turned_sb, i * STEPS + K - 1)
                for j in range(JT):
                    last = nc.tensor.transpose(turned_ps[K % 2][:, j * P:(j + 1) * P],
                                               prob[K % 2][:, j * P:(j + 1) * P], ident[:, :])
                last.then_inc(turned, 1)

            def mix(i, g):
                n = i * (STEPS // GRP) + g
                pe.wait_ge(turned_sb, (n + 1) * GRP)
                h, p = 2 * i + g // (NT // GRP), g // (NT // GRP) % 2
                if g % (NT // GRP) == 0:
                    pe.wait_ge(v_head, h + 1)
                if before(i, g - 2):
                    pe.wait_ge(ctx_ready, n - 1)
                for jj in range(JT // 2):
                    for half in range(2):
                        for bg in range(2):
                            c, j = 2 * bg + half, JT // 2 * half + jj
                            last = mm(mixed_ps[g % 2][32 * c:32 * c + 32, 0:CTX],
                                      vh[:, p, j, BG * bg:BG * (bg + 1), :].rearrange("p b d -> p (b d)"),
                                      probT[g % 2][:, j, :].rearrange("p (u b) -> p u b", b=NB)[:, :, BG * bg:BG * (bg + 1)],
                                      start=(jj == 0), stop=(jj == JT // 2 - 1))
                last.then_inc(mixed, 1)

            def untangle(i, g):
                pe.wait_ge(masked_ready, 2 * (i * (STEPS // GRP) + g + 1))
                for t in range(GRP):
                    last = mm(mixed_ps[g % 2][:, CTX + t * HD:CTX + (t + 1) * HD],
                              masked[:, g % 2, t * U:(t + 1) * U, :].rearrange("p u b -> p (u b)"), same_d[:, :],
                              start=True, stop=True)
                last.then_inc(untangled, 1)

            def rest(i, K):
                if K % GRP == 0 and before(i, K - 2 * GRP):
                    untangle(i, K // GRP - 2)
                if before(i, K - 2):
                    turn(i, K - 2)
                if K % GRP == 2 and before(i, K - 6):
                    mix(i, (K - 6) // GRP)

            def pair(i):
                for K in range(STEPS):
                    score(i, K)
                    rest(i, K)

            pair(0)
            with pe.Fori(1, HEADS // 2) as i:
                pair(i)
            last_pair = HEADS // 2
            untangle(last_pair, -2)
            turn(last_pair, -2)
            turn(last_pair, -1)
            mix(last_pair, -1)
            untangle(last_pair, -1)

        @block.scalar
        def _(act):
            def copy_turned(i, K):
                act.wait_ge(turned, i * STEPS + K + 1)
                if K % GRP == 0 and before(i, K - 2 * GRP):
                    act.wait_ge(mixed, i * (STEPS // GRP) + K // GRP - 1)
                nc.scalar.copy(probT[K // GRP % 2][:, :, K % GRP * P:(K % GRP + 1) * P],
                               turned_ps[K % 2][:, :].rearrange("p (j t) -> p j t", j=JT)).then_inc(turned_sb, 1)

            def pair(i):
                for K in range(STEPS):
                    p, k = divmod(K, NT)
                    act.wait_ge(top_ready, i * STEPS + K + 1)
                    if before(i, K - 2):
                        act.wait_ge(turned, i * STEPS + K - 1)
                    nc.scalar.activation(prob[K % 2][:, :], score_ps[K % RING][:, :], ACT.Exp, bias=ntop[:, k:k + 1],
                                         accum_out=rsum[:, p, k:k + 1]).then_inc(prob_ready, 1)
                    if before(i, K - 1):
                        copy_turned(i, K - 1)

            pair(0)
            with act.Fori(1, HEADS // 2) as i:
                pair(i)
            copy_turned(HEADS // 2, -1)

        @block.vector
        def _(dve):
            v = nc.vector
            for p in range(2):
                for t in qs[p]:
                    v.memset(t[:, :, :, :], 0.0).then_inc(zeroed[p], 1)
            v.tensor_reduce(own2[:, :], ident[:, :].rearrange("p (e d) -> p e d", d=HD), AX.X, ALU.add)\
             .then_inc(mask_ready, 1)
            dve.wait_ge(mask_ready, 1)
            v.tensor_reduce(own[:, :], own2[:, :].rearrange("p (c b) -> p b c", b=BG), AX.X, ALU.add)\
             .then_inc(mask_ready, 1)
            v.tensor_reduce(same_d[:, :], ident[:, :].rearrange("p (e d) -> p d e", d=HD), AX.X, ALU.add)\
             .then_inc(mask_ready, 1)
            dve.wait_ge(mask_ready, 3)
            dve.wait_ge(mask_zeroed, 1)

            def pick(i, g):
                n = i * (STEPS // GRP) + g
                dve.wait_ge(mixed, n + 1)
                if before(i, g - 2):
                    dve.wait_ge(untangled, n - 1)
                for bg in range(2):
                    rows = slice(P // 2 * bg, P // 2 * (bg + 1))
                    v.tensor_tensor(masked[rows, g % 2, :, BG * bg:BG * (bg + 1)],
                                    mixed_ps[g % 2][rows, 0:GRP * U * BG].rearrange("p (u b) -> p u b", b=BG),
                                    own[rows, :].unsqueeze(1).to_broadcast([P // 2, GRP * U, BG]), ALU.mult)\
                     .then_inc(masked_ready, 1)

            def finish(i, g):
                n = i * (STEPS // GRP) + g
                p = g // (NT // GRP) % 2
                tiles = slice(g % (NT // GRP) * GRP, (g % (NT // GRP) + 1) * GRP)
                h = 2 * i + g // (NT // GRP)
                v.reciprocal(rsum[:, p, tiles], rsum[:, p, tiles]).then_inc(rinv_ready, 1)
                dve.wait_ge(untangled, n + 1)
                dve.wait_ge(rinv_ready, n + 1)
                v.tensor_tensor(ctxt[:, tiles, bass.ds(h * HD, HD)],
                                mixed_ps[g % 2][:, CTX:CTX + GRP * HD].rearrange("p (k d) -> p k d", d=HD),
                                rsum[:, p, tiles].unsqueeze(2).to_broadcast([P, GRP, HD]), ALU.mult)\
                 .then_inc(ctx_ready, 1)

            def pair(i):
                for K in range(STEPS):
                    p, k = divmod(K, NT)
                    dve.wait_ge(scores, i * STEPS + K + 1)
                    v.tensor_reduce(ntop[:, k:k + 1], score_ps[K % RING][:, :], AX.X, ALU.max, negate=True)\
                     .then_inc(top_ready, 1)
                    if K % GRP == 3 and before(i, K - 7):
                        pick(i, (K - 7) // GRP)
                    if K % GRP == 1 and before(i, K - 9):
                        finish(i, (K - 9) // GRP)

            pair(0)
            with dve.Fori(1, HEADS // 2) as i:
                pair(i)
            finish(HEADS // 2, -2)
            pick(HEADS // 2, -1)
            finish(HEADS // 2, -1)

def attention_output(nc, d, keep, ctxt):
    x, mod, ident, ones = keep["x"], keep["mod"], keep["ident"], keep["ones"]
    with ExitStack() as ctx:
        sb = lambda name, shape, dt=F32: ctx.enter_context(nc.sbuf_tensor(name, shape, dt))
        sem = lambda name: ctx.enter_context(nc.semaphore(name))
        pt = [ctx.enter_context(nc.psum_tensor(f"pt{i}", [P, 512], F32)) for i in range(2)]
        po = [ctx.enter_context(nc.psum_tensor(f"pp{i}", [P, 512], F32)) for i in range(2)]
        wo, bo = sb("wo1", [P, P]), sb("bo1", [1, P])
        cT = sb("ctxT", [P, 2, BLK])
        upd = sb("upd1", [P, 2, TPB, P])
        w_in, turned, cT_ready, out_ready, upd_ready, x_added = (
            sem("w_ino"), sem("turnedo"), sem("cT_ready"), sem("out_readyo"), sem("upd_readyo"), sem("x_addedo"))
        block = ctx.enter_context(nc.Block())

        @block.sync
        def _(sp):
            sp.dma_start(wo[:, :], d["woT"]).then_inc(w_in, 16)
            sp.dma_start(bo[:, :], d["bo"]).then_inc(w_in, 16)

        @block.scalar
        def _(act):
            for j in range(NBLK):
                act.wait_ge(turned, j + 1)
                if j >= 2:
                    act.wait_ge(out_ready, j - 1)
                nc.scalar.copy(cT[:, j % 2, :], pt[j % 2][:, :]).then_inc(cT_ready, 1)

        @block.tensor
        def _(pe):
            pe.wait_ge(w_in, 32)
            for j in range(NBLK + 1):
                if j < NBLK:
                    if j >= 2:
                        pe.wait_ge(cT_ready, j - 1)
                    for q in range(TPB):
                        last = nc.tensor.transpose(pt[j % 2][:, q * P:(q + 1) * P], ctxt[:, j * TPB + q, :], ident[:, :])
                    last.then_inc(turned, 1)
                if j >= 1:
                    i = j - 1
                    pe.wait_ge(cT_ready, i + 1)
                    if i >= 2:
                        pe.wait_ge(upd_ready, i - 1)
                    for q in range(TPB):
                        to = po[i % 2][:, q * P:(q + 1) * P]
                        nc.tensor.matmul(to, cT[:, i % 2, q * P:(q + 1) * P], wo[:, :], start=True, stop=False)
                        last = nc.tensor.matmul(to, ones[0:1, :], bo[:, :], start=False, stop=True)
                    last.then_inc(out_ready, 1)

        @block.vector
        def _(dve):
            v = nc.vector
            for j in range(NBLK):
                dve.wait_ge(out_ready, j + 1)
                if j >= 2:
                    dve.wait_ge(x_added, j - 1)
                v.tensor_tensor(upd[:, j % 2, :, :], po[j % 2][:, :].rearrange("p (q e) -> p q e", q=TPB),
                                mod[:, 1, 2 * P:3 * P].unsqueeze(1).to_broadcast([P, TPB, P]), ALU.mult)\
                 .then_inc(upd_ready, 1)
                dve.wait_ge(upd_ready, j + 1)
                xs = x[:, j * TPB:(j + 1) * TPB, :]
                v.tensor_tensor(xs, xs, upd[:, j % 2, :, :], ALU.add).then_inc(x_added, 1)
            dve.wait_ge(x_added, NBLK)


def experts1(nc, d, keep):
    x, mod, ident = keep["x"], keep["mod"], keep["ident"]
    NALL = NE1 + 1
    WCOLS = 5 * P
    with ExitStack() as ctx:
        sb = lambda name, shape, dt=F32: ctx.enter_context(nc.sbuf_tensor(name, shape, dt))
        sem = lambda name: ctx.enter_context(nc.semaphore(name))
        pm = [ctx.enter_context(nc.psum_tensor(f"pz{i}", [P, 512], F32)) for i in range(8)]
        hT = sb("hTz", [P, TOK])
        W = [sb(f"w1_{p}", [P, WCOLS]) for p in range(2)]
        B = [sb(f"b1_{p}", [P, 4]) for p in range(2)]
        gw = sb("gw1", [P, NE1])
        gb = sb("gb1", [P, NE1])
        b2 = sb("b2", [NALL, P])
        rank = sb("rank1", [P, NE1])
        ranki = sb("ranki1", [P, NE1], mybir.dt.int32)
        probs = sb("probs1", [P, NT, NE1])
        keys = sb("keys1", [P, NT, NE1])
        hot = sb("hot1", [P, NT, NE1])
        top = sb("top1", [P, NT])
        cw = sb("cw1", [P, NT, NALL])
        cwe = sb("cwe", [P, 2, NT])
        cwT = sb("cwT1", [NALL, TOK])
        acc = sb("acc1", [P, NT, P])
        g1, l1 = sb("g1", [P, 2, BLK]), sb("l1", [P, 2, BLK])
        gg, ll = sb("gg", [P, 2, BLK]), sb("ll", [P, 2, BLK])
        th, a = sb("th", [P, 2, BLK]), sb("a", [P, 2, BLK])
        w_in, v_chain, ranks = sem("w_inz"), sem("v_chainz"), sem("ranks1")
        logits_ready, exp_asked, exp_done = sem("logits_ready1"), sem("exp_asked1"), sem("exp_done1")
        cw_ready, cwT_ps, cwT_ready = sem("cw_ready1"), sem("cwT_ps1"), sem("cwT_ready1")
        seed_ps, seeded = sem("seed_ps"), sem("seeded1")
        we_in, w2_half = [sem("we_in0"), sem("we_in1")], sem("w2_half")
        gate_ps, lin_ps, first_g, first_l = sem("gate_ps"), sem("lin_ps"), sem("first_g"), sem("first_l")
        pool_steps = sem("pool_steps")
        gg_raw, gg_ready, th_ready = sem("gg_raw"), sem("gg_ready"), sem("th_ready")
        ll_raw, ll_ready, gl_ready, a_ready = sem("ll_raw"), sem("ll_ready"), sem("gl_ready"), sem("a_ready")
        y_ready, y_summed, cwe_ready = sem("y_ready1"), sem("y_summed"), sem("cwe_ready")
        norm = Normed(nc, sb, sem, keep, 1, 1, hT, pm[0:2], "z")
        G1, L1, G3, L3, Y = pm[0], pm[1], pm[2:4], pm[4:6], pm[6:8]
        block = ctx.enter_context(nc.Block())

        def experts(eng, body):
            body(0, 0)
            body(1, 1)
            with eng.Fori(1, NE1 // 2) as i:
                body(2 * i, 0)
                body(2 * i + 1, 1)
            body(NE1, 0)

        def back(e, p, j, steps):
            if j >= steps:
                return e * NBLK + j - steps, p, j - steps
            if isinstance(e, int) and e == 0:
                return None
            return e * NBLK + j - steps, 1 - p, j - steps + NBLK

        def weights_in(e, p):
            return 32 * (e // 2 + 1) if isinstance(e, int) else 16 * e + 32 - 16 * p

        @block.sync
        def _(sp):
            for dst, src in ((gw[:, :], d["gw1"]), (gb[:, :], d["gb1"].to_broadcast([P, NE1])),
                             (b2[:, :], d["b2"])):
                sp.dma_start(dst, src).then_inc(w_in, 16)

            def load(e, p):
                w, b = ((d["ew1"][bass.ds(e, 1), :, :], d["eb1"][bass.ds(e, 1), :, :]) if not isinstance(e, int)
                        else (d["ew1"][e:e + 1, :, :], d["eb1"][e:e + 1, :, :]))
                sp.dma_start(W[p][:, :], w.rearrange("o p n -> p (o n)")).then_inc(we_in[p], 16)
                sp.dma_start(B[p][:, :], b.rearrange("o p n -> p (o n)")).then_inc(we_in[p], 16)

            load(0, 0)
            load(1, 1)
            with sp.Fori(1, NE1 // 2) as i:
                for p in range(2):
                    sp.wait_ge(y_ready, (2 * i - 1 + p) * NBLK)
                    load(2 * i + p, p)
            sp.wait_ge(y_ready, (NE1 - 1) * NBLK)
            load(NE1, 0)

        @block.gpsimd
        def _(pool):
            nc.gpsimd.iota(ranki[:, :], pattern=[[-1, NE1]], base=NE1, channel_multiplier=0).then_inc(ranks, 1)
            pool.wait_ge(ranks, 1)
            nc.gpsimd.tensor_copy(rank[:, :], ranki[:, :]).then_inc(ranks, 1)

            def body(e, p):
                for j in range(NBLK):
                    n, q = e * NBLK + j, j % 2
                    pool.wait_ge(gg_raw, n + 1)
                    pool.sem_inc(pool_steps, 1)
                    nc.gpsimd.tensor_scalar(gg[:, q, :], gg[:, q, :], LIMIT, LOWEST, ALU.min, ALU.max)\
                      .then_inc(gg_ready, 1)
                    pool.wait_ge(ll_raw, n + 1)
                    pool.sem_inc(pool_steps, 1)
                    nc.gpsimd.tensor_scalar(ll[:, q, :], ll[:, q, :], LIMIT, -LIMIT, ALU.min, ALU.max)\
                      .then_inc(ll_ready, 1)

            experts(pool, body)

        @block.scalar
        def _(act):
            norm.scalar(act)
            act.wait_ge(exp_asked, 1)
            nc.scalar.activation(probs[:, :, :], probs[:, :, :], ACT.Exp).then_inc(exp_done, 1)
            for j in range(NBLK):
                act.wait_ge(cwT_ps, j + 1)
                nc.scalar.copy(cwT[:, j * BLK:(j + 1) * BLK], pm[2 + j % 2][0:NALL, :]).then_inc(cwT_ready, 1)
            for j in range(NBLK):
                act.wait_ge(seed_ps, j + 1)
                nc.scalar.copy(acc[:, j * TPB:(j + 1) * TPB, :].rearrange("p k e -> p (k e)"),
                               pm[4 + j % 2][:, :]).then_inc(seeded, 1)

            def tanh(n, p, j):
                act.wait_ge(gg_ready, n + 1)
                nc.scalar.activation(th[:, j % 2, :], gg[:, j % 2, :], ACT.Tanh, scale=ALPHA / 2)\
                  .then_inc(th_ready, 1)

            def body(e, p):
                act.wait_ge(we_in[p], weights_in(e, p))
                for j in range(NBLK):
                    n, q = e * NBLK + j, j % 2
                    act.wait_ge(gate_ps, n + 1)
                    nc.scalar.activation(g1[:, q, :], G1[:, :], ACT.Identity, bias=B[p][:, 0:1])\
                      .then_inc(first_g, 1)
                    if back(e, p, j, 1):
                        tanh(*back(e, p, j, 1))
                    act.wait_ge(lin_ps, n + 1)
                    nc.scalar.activation(l1[:, q, :], L1[:, :], ACT.Identity, bias=B[p][:, 1:2])\
                      .then_inc(first_l, 1)

            experts(act, body)
            tanh(*back(NE1, 0, NBLK, 1))

        @block.vector
        def _(dve):
            v = nc.vector
            chain = Chain(dve, v_chain)
            norm.vector(dve, chain)
            dve.wait_ge(w_in, 16 * 3)
            dve.wait_ge(ranks, 2)
            dve.wait_ge(logits_ready, 1)
            softmax_probs(dve, nc, chain, probs[:, :, :], pm[4][:, 0:NT * NE1].rearrange("p (k e) -> p k e", e=NE1),
                          None, top[:, :], NE1, exp_asked, exp_done)
            chain(v.tensor_tensor(keys[:, :, :], probs[:, :, :], gb[:, :].unsqueeze(1).to_broadcast([P, NT, NE1]),
                                  ALU.add))
            first_of_max(nc, chain, keys[:, :, :], rank[:, :], hot[:, :, :], top[:, :], NE1)
            chain(v.tensor_tensor(cw[:, :, 0:NE1], hot[:, :, :], probs[:, :, :], ALU.mult))
            chain(v.scalar_tensor_tensor(keys[:, :, :], hot[:, :, :], -3e38, keys[:, :, :], ALU.mult, ALU.add))
            first_of_max(nc, chain, keys[:, :, :], rank[:, :], hot[:, :, :], top[:, :], NE1)
            chain(v.tensor_tensor(hot[:, :, :], hot[:, :, :], probs[:, :, :], ALU.mult))
            chain(v.tensor_tensor(cw[:, :, 0:NE1], cw[:, :, 0:NE1], hot[:, :, :], ALU.add))
            chain(v.memset(cw[:, :, NE1:NALL], 1.0))
            v.sem_inc(cw_ready, 1)
            dve.wait_ge(seeded, NBLK)

            def add_up(n, p, j):
                dve.wait_ge(y_ready, n + 1)
                for t in range(TPB):
                    k = j * TPB + t
                    last = v.scalar_tensor_tensor(acc[:, k, :], Y[j % 2][:, t * P:(t + 1) * P],
                                                  cwe[:, p, k:k + 1], acc[:, k, :], ALU.mult, ALU.add)
                last.then_inc(y_summed, 1)

            def join(n, p, j):
                q = j % 2
                dve.wait_ge(gg_ready, n + 1)
                dve.wait_ge(ll_ready, n + 1)
                v.scalar_tensor_tensor(ll[:, q, :], ll[:, q, :], 1.0, gg[:, q, :], ALU.add, ALU.mult)\
                 .then_inc(gl_ready, 1)
                dve.wait_ge(gl_ready, n + 1)
                dve.wait_ge(th_ready, n + 1)
                v.scalar_tensor_tensor(a[:, q, :], th[:, q, :], 1.0, ll[:, q, :], ALU.add, ALU.mult)\
                 .then_inc(a_ready, 1)

            def body(e, p):
                src = cw[:, :, bass.ds(e, 1)] if not isinstance(e, int) else cw[:, :, e:e + 1]
                v.tensor_copy(cwe[:, p, :].unsqueeze(2), src).then_inc(cwe_ready, 1)
                dve.wait_ge(cwe_ready, e + 1)
                dve.wait_ge(we_in[p], weights_in(e, p))
                v.tensor_scalar(W[p][:, 4 * P:5 * P], W[p][:, 4 * P:5 * P], 0.5, None, ALU.mult).then_inc(w2_half, 1)
                dve.wait_ge(w2_half, e + 1)
                for j in range(NBLK):
                    n, q = e * NBLK + j, j % 2
                    if back(e, p, j, 2):
                        dve.wait_ge(a_ready, n - 1)
                    dve.wait_ge(first_g, n + 1)
                    v.scalar_tensor_tensor(gg[:, q, :], G3[q][:, :], B[p][:, 2:3], g1[:, q, :],
                                           ALU.add, ALU.mult).then_inc(gg_raw, 1)
                    dve.wait_ge(first_l, n + 1)
                    v.scalar_tensor_tensor(ll[:, q, :], L3[q][:, :], B[p][:, 3:4], l1[:, q, :],
                                           ALU.add, ALU.mult).then_inc(ll_raw, 1)
                    if back(e, p, j, 1):
                        join(*back(e, p, j, 1))
                    if back(e, p, j, 2):
                        add_up(*back(e, p, j, 2))

            experts(dve, body)
            join(*back(NE1, 0, NBLK, 1))
            add_up(*back(NE1, 0, NBLK, 2))
            add_up(*back(NE1, 0, NBLK, 1))
            dve.wait_ge(y_summed, NBLK * NALL)
            for j in range(NBLK):
                ts = slice(j * TPB, (j + 1) * TPB)
                chain(v.tensor_tensor(acc[:, ts, :], acc[:, ts, :],
                                      mod[:, 1, 5 * P:6 * P].unsqueeze(1).to_broadcast([P, TPB, P]), ALU.mult))
                chain(v.tensor_tensor(x[:, ts, :], x[:, ts, :], acc[:, ts, :], ALU.add))

        @block.tensor
        def _(pe):
            mm = nc.tensor.matmul
            norm.tensor(pe)
            pe.wait_ge(w_in, 16 * 3)
            pe.wait_ge(norm.hT_ready, NBLK)
            for k in range(NT):
                last = mm(pm[4][:, k * NE1:(k + 1) * NE1], hT[:, k * P:(k + 1) * P], gw[:, :], start=True, stop=True)
            last.then_inc(logits_ready, 1)
            pe.wait_ge(cw_ready, 1)
            for j in range(NBLK):
                if j >= 2:
                    pe.wait_ge(cwT_ready, j - 1)
                for t in range(TPB):
                    last = nc.tensor.transpose(pm[2 + j % 2][0:NALL, t * P:(t + 1) * P], cw[:, j * TPB + t, :],
                                               ident[:, :])
                last.then_inc(cwT_ps, 1)
            for j in range(NBLK):
                pe.wait_ge(cwT_ready, j + 1)
                if j >= 2:
                    pe.wait_ge(seeded, j - 1)
                for t in range(TPB):
                    last = mm(pm[4 + j % 2][:, t * P:(t + 1) * P], cwT[:, (j * TPB + t) * P:(j * TPB + t + 1) * P],
                              b2[:, :], start=True, stop=True)
                last.then_inc(seed_ps, 1)
            pe.wait_ge(seeded, NBLK)

            def second(n, p, j):
                pe.wait_ge(a_ready, n + 1)
                if not (isinstance(n, int) and n < 2):
                    pe.wait_ge(y_summed, n - 1)
                for t in range(TPB):
                    last = mm(Y[j % 2][:, t * P:(t + 1) * P], a[:, j % 2, t * P:(t + 1) * P],
                              W[p][:, 4 * P:5 * P], start=True, stop=True)
                last.then_inc(y_ready, 1)

            def body(e, p):
                pe.wait_ge(we_in[p], weights_in(e, p))
                for j in range(NBLK):
                    n, q = e * NBLK + j, j % 2
                    src = hT[:, j * BLK:(j + 1) * BLK]
                    first = isinstance(e, int) and e == 0
                    if not (first and j == 0):
                        pe.wait_ge(first_g, n)
                    mm(G1[:, :], W[p][:, 0:P], src, start=True, stop=True)
                    if not (first and j < 2):
                        pe.wait_ge(gg_raw, n - 1)
                    mm(G3[q][:, :], W[p][:, 2 * P:3 * P], src, start=True, stop=True).then_inc(gate_ps, 1)
                    if not (first and j == 0):
                        pe.wait_ge(first_l, n)
                    mm(L1[:, :], W[p][:, P:2 * P], src, start=True, stop=True)
                    if not (first and j < 2):
                        pe.wait_ge(ll_raw, n - 1)
                    mm(L3[q][:, :], W[p][:, 3 * P:4 * P], src, start=True, stop=True).then_inc(lin_ps, 1)
                    if back(e, p, j, 2):
                        second(*back(e, p, j, 2))

            experts(pe, body)
            second(*back(NE1, 0, NBLK, 2))
            second(*back(NE1, 0, NBLK, 1))


def store(nc, d, keep, out):
    with nc.semaphore("stored") as stored, nc.Block() as block:
        @block.sync
        def _(sp):
            sp.dma_start(out, keep["x"][:, :, :]).then_inc(stored, 16)
            sp.wait_ge(stored, 16)


def program(nc, d, out, stop):
    with ExitStack() as ctx:
        sb = lambda name, shape, dt=F32: ctx.enter_context(nc.sbuf_tensor(name, shape, dt))
        keep = {"x": sb("x", [P, NT, P]), "mod": sb("mod", [P, 2, MODS * P]),
                "ident": sb("ident", [P, P]), "ones": sb("ones", [P, P])}
        with ExitStack() as inner:
            sb1 = lambda name, shape, dt=F32: inner.enter_context(nc.sbuf_tensor(name, shape, dt))
            scan = {"A": sb1("A", [P, NS * NB]), "Bm": sb1("Bm", [P, NS]), "Dv": sb1("Dv", [P, 1]),
                    "xp": sb1("xp", [P, NC * P]), "gate": sb1("gate2", [P, NC * P]),
                    "hist": sb1("hist", [P, 2, U, NS * NB]), "diagC": sb1("diagC", [P, NS, P]),
                    "woT": sb1("woT", [P, P]), "bo": sb1("bo", [1, P])}
            prologue(nc, d, keep, scan)
            scan_phase(nc, d, keep, scan)
        experts0(nc, d, keep)
        scratch = {n: nc.dram_tensor(f"parts_{n}", shape, BF16, kind="Internal").ap()
                   for n, shape in (("q", (PARTS, P, TOK)), ("k", (HEADS, len(KEY_SLOTS), HD, TOK)),
                                    ("t", (HEADS, len(TABLE_SLOTS), HD, TROW)))}
        with ExitStack() as inner:
            vals = inner.enter_context(nc.sbuf_tensor("vals", [P, JT * NB, P], F32))
            attention_inputs(nc, d, keep, vals, scratch)
            ctxt = inner.enter_context(nc.sbuf_tensor("ctxt", [P, NT, P], F32))
            attention(nc, d, keep, vals, scratch, ctxt)
            attention_output(nc, d, keep, ctxt)
        experts1(nc, d, keep)
        store(nc, d, keep, out)


def layouts(inputs, np):
    g = lambda n: np.asarray(inputs[n])
    a = {}
    a["x"] = g("L0_attn_x").reshape(NB, NC, U, 2, P).transpose(2, 0, 1, 3, 4).reshape(P, NT, P)
    a["cT"] = np.stack([g("L0_c").T, g("L1_c").T], 1)
    a["wmod"] = np.stack([g("L0_wmod"), g("L1_wmod")], 1)
    a["w_inT"] = g("L0_attn_w_in").T
    a["b_in"] = g("L0_attn_b_in").reshape(2, P).T
    a["g_norm"] = g("L0_attn_g_norm").reshape(P, 1)
    a["A"], a["Bm"], a["Cm"] = g("L0_attn_A"), g("L0_attn_Bm"), g("L0_attn_Cm")
    a["Dv"] = g("L0_attn_Dv").reshape(P, 1)
    a["w_outT"] = g("L0_attn_w_out").T
    a["b_out"] = g("L0_attn_b_out").reshape(1, P)
    a["gw0"] = g("L0_ffn_gate_w").T
    a["gb0"] = g("L0_ffn_gate_b").reshape(1, NX0)
    a["ew0"] = g("L0_ffn_expert_w").transpose(1, 0, 2).reshape(P, NE0 * P)
    a["eb0"] = g("L0_ffn_expert_b")
    a["table"] = g("L1_attn_rpe_table")[:, TLEN - 1::-1, :].transpose(0, 2, 1).reshape(P, TLEN)
    for n in "qkvo":
        a[f"w{n}T"] = g(f"L1_attn_w{n}").T
    a["bq"], a["bk"] = g("L1_attn_bq").reshape(P, 1), g("L1_attn_bk").reshape(P, 1)
    a["bv"], a["bo"] = g("L1_attn_bv").reshape(1, P), g("L1_attn_bo").reshape(1, P)
    a["gw1"] = g("L1_ffn_gate_w").T
    a["gb1"] = g("L1_ffn_gate_b").reshape(1, NE1)
    w = [np.concatenate([g(f"L1_ffn_{n}"), g(f"L1_ffn_s{n}")[None]]) for n in ("w1", "w3", "w2")]
    b = [np.concatenate([g(f"L1_ffn_{n}"), g(f"L1_ffn_s{n}")[None]]) for n in ("b1", "b3", "b2")]
    a["ew1"] = np.concatenate([m.transpose(0, 2, 1) for m in (w[0][:, ::2], w[0][:, 1::2], w[1][:, ::2],
                                                            w[1][:, 1::2], w[2])], axis=2)
    a["eb1"] = np.stack([b[0][:, ::2], b[0][:, 1::2], b[1][:, ::2], b[1][:, 1::2]], axis=2)
    a["b2"] = b[2]
    return {k: np.ascontiguousarray(v) for k, v in a.items()}


def kernel(**inputs):
    import numpy as np
    import concourse.bacc as bacc
    from concourse.bass_utils import run_bass_kernel_spmd

    arrays = layouts(inputs, np)
    nc = bacc.Bacc("TRN2", target_bir_lowering=False, num_devices=1)
    d = {k: nc.dram_tensor(f"in_{k}", v.shape, F32, kind="ExternalInput").ap() for k, v in arrays.items()}
    out = nc.dram_tensor("out_x", (P, NT, P), F32, kind="ExternalOutput").ap()
    program(nc, d, out, 99)
    r = run_bass_kernel_spmd(nc, [{f"in_{k}": v for k, v in arrays.items()}], core_ids=[0])
    y = r.results[0]["out_x"]
    return y.reshape(U, NB, NC, 2, P).transpose(1, 2, 0, 3, 4).reshape(NB, SEQ, P)
```

```python
import concourse.bass as bass
from concourse import mybir
from contextlib import ExitStack

F32 = mybir.dt.float32
BF16 = mybir.dt.bfloat16
ALU = mybir.AluOpType
ACT = mybir.ActivationFunctionType
AX = mybir.AxisListType

P = 128
NB = 8
SEQ = 512
U = P // NB
NT = NB * SEQ // P
NC = NT // 2
BLK = 512
NBLK = NB * SEQ // BLK
TPB = BLK // P
NS = 64
PARTED = [(NS * j // 3 * NB, NS * (j + 1) // 3 * NB) for j in range(3)]
NPT = len(PARTED)
HEADS = 16
HD = P // HEADS
NE0, NX0 = 8, 10
NE1 = 8
MODS = 6
LN_EPS, RMS_EPS = 1e-5, 1e-6
TLEN = 2 * SEQ - 1
LIMIT = 7.0
LOWEST = -3.4028234e38
ALPHA = 1.702


class Chain:

    def __init__(self, eng, sem):
        self.eng, self.sem, self.n = eng, sem, 0

    def add(self, ins):
        self.n += 1
        ins.then_inc(self.sem, 1)

    def wait(self):
        self.eng.wait_ge(self.sem, self.n)

    def __call__(self, ins):
        self.add(ins)
        self.wait()


class Roots:

    def __init__(self, asked, answered):
        self.asked, self.answered, self.n, self.served = asked, answered, 0, 0

    def rsqrt(self, dve, v, chain, val, root, tmp):
        self.n += 1
        v.tensor_scalar(tmp, val, 1.0, None, ALU.mult).then_inc(self.asked, 1)
        dve.wait_ge(self.answered, self.n)
        chain(v.reciprocal(root, root))
        chain(v.tensor_tensor(tmp, root, root, ALU.mult))
        chain(v.tensor_tensor(tmp, tmp, val, ALU.mult))
        chain(v.tensor_scalar(tmp, tmp, -0.5, 1.5, ALU.mult, ALU.add))
        chain(v.tensor_tensor(root, root, tmp, ALU.mult))

    def serve(self, act, nc, root, tmp):
        self.served += 1
        act.wait_ge(self.asked, self.served)
        nc.scalar.activation(root, tmp, ACT.Sqrt).then_inc(self.answered, 1)


def moments(v, chain, src, n, stats, mv):
    for k in range(n):
        chain.add(v.bn_stats(stats[:, k, :], src[:, k, :]))
    chain.wait()
    for k in range(n):
        chain.add(v.bn_aggr(mv[:, k, :], stats[:, k, :]))
    chain.wait()
    chain(v.tensor_scalar(mv[:, 0:n, 1], mv[:, 0:n, 1], LN_EPS, None, ALU.add))


def layer_norm(dve, v, chain, roots, src, out, n, stats, mv, rstd, tmp, scale, shift):
    moments(v, chain, src, n, stats, mv)
    roots.rsqrt(dve, v, chain, mv[:, 0:n, 1], rstd[:, 0:n], tmp[:, 0:n])
    for k in range(n):
        chain.add(v.tensor_scalar(out[:, k, :], src[:, k, :], mv[:, k, 0:1], rstd[:, k:k + 1],
                                  ALU.subtract, ALU.mult))
    chain.wait()
    chain(v.tensor_tensor(out[:, 0:n, :], out[:, 0:n, :], scale.unsqueeze(1).to_broadcast([P, n, P]), ALU.mult))
    chain(v.tensor_tensor(out[:, 0:n, :], out[:, 0:n, :], shift.unsqueeze(1).to_broadcast([P, n, P]), ALU.add))


def prologue(nc, d, keep, scan):
    x, mod, ident, ones = keep["x"], keep["mod"], keep["ident"], keep["ones"]
    with ExitStack() as ctx:
        sb = lambda name, shape, dt=F32: ctx.enter_context(nc.sbuf_tensor(name, shape, dt))
        sem = lambda name: ctx.enter_context(nc.semaphore(name))
        cT = sb("cT", [P, 2, NB])
        cth = sb("cth", [P, 2, NB])
        crep = sb("crep", [P, 2, U, NB])
        wmod = sb("wmod", [P, 2, MODS * P])
        guard = sb("guard", [P, 2, P])
        winT = sb("winT", [P, 2 * P])
        binc = sb("binc", [P, 2])
        binh = sb("binh", [P, 1])
        gn = sb("gn", [P, 1])
        cm = sb("cm", [P, NS])
        am = sb("am", [P, NS])
        csum = sb("csum", [P, NS])
        h = sb("h0", [P, NC, P])
        hT = sb("h0T", [P, NC * P])
        sq = sb("sq", [P, NC, P])
        stats = sb("stats0", [P, NC, 6])
        mv = sb("mv0", [P, NC, 2])
        rstd = sb("rstd0", [P, NC])
        rtmp = sb("rtmp0", [P, NC])
        ms = sb("ms", [P, NC])
        gate = sb("gate", [P, 2, BLK])
        gth = sb("gth", [P, 2, BLK])
        pm = [ctx.enter_context(nc.psum_tensor(f"pm{i}", [P, 512], F32)) for i in range(8)]
        x_in, w_in, zero, id_ready, v_chain = sem("x_in"), sem("w_in"), sem("zero"), sem("id_ready"), sem("v_chain0")
        c_tanh, c_rep, mod_ps, mod_sb = sem("c_tanh"), sem("c_rep"), sem("mod_ps"), sem("mod_sb")
        h_ready, hT_ps, hT_sb, proj_ps = sem("h_ready"), sem("hT_ps"), sem("hT_sb"), sem("proj_ps")
        proj_sb, gate_sb, gate_used, csum_ps = sem("proj_sb"), sem("gate_sb"), sem("gate_used"), sem("csum_ps")
        w_scaled, csum_sb, scan_set = sem("w_scaled"), sem("csum_sb"), sem("scan_set")
        roots = Roots(sem("var_ready0"), sem("root_ready0"))
        NBK = NC * P // BLK
        block = ctx.enter_context(nc.Block())

        @block.sync
        def _(sp):
            sp.dma_start(cT[:, :, :], d["cT"]).then_inc(w_in, 16)
            sp.dma_start(wmod[:, :, :], d["wmod"]).then_inc(w_in, 16)
            sp.dma_start(x[:, :, :], d["x"]).then_inc(x_in, 16)
            for dst, src in ((winT[:, :], d["w_inT"]), (binc[:, :], d["b_in"]), (gn[:, :], d["g_norm"]),
                             (cm[:, :], d["Cm"]), (am[:, :], d["A"]), (scan["Bm"][:, :], d["Bm"]),
                             (scan["Dv"][:, :], d["Dv"]), (scan["woT"][:, :], d["w_outT"]),
                             (scan["bo"][:, :], d["b_out"])):
                sp.dma_start(dst, src).then_inc(w_in, 16)

        ALL_W = 16 * 11

        @block.gpsimd
        def _(pool):
            nc.gpsimd.memset(ident[:, :], 0.0).then_inc(zero, 1)
            nc.gpsimd.memset(ones[:, :], 1.0).then_inc(id_ready, 1)
            pool.wait_ge(zero, 1)
            nc.gpsimd.affine_select(out=ident[:, :], in_=ident[:, :], compare_op=ALU.not_equal, fill=1.0,
                                    base=0, pattern=[[-1, P]], channel_multiplier=1).then_inc(id_ready, 1)
            nc.gpsimd.memset(scan["hist"][:, 1, U - 1, :], 0.0).then_inc(scan_set, 1)
            pool.wait_ge(id_ready, 2)
            pool.wait_ge(csum_sb, 1)
            nc.gpsimd.tensor_tensor(scan["diagC"][:, 0:NS, :], ident[:, :].unsqueeze(1).to_broadcast([P, NS, P]),
                                    csum[:, :].unsqueeze(2).to_broadcast([P, NS, P]), ALU.mult).then_inc(scan_set, 1)
            nc.gpsimd.tensor_tensor(scan["diagC"][:, NS, :], ident[:, :], scan["Dv"][:, 0:1].to_broadcast([P, P]),
                                    ALU.mult).then_inc(scan_set, 1)
            pool.wait_ge(scan_set, 3)

        @block.scalar
        def _(act):
            act.wait_ge(w_in, ALL_W)
            nc.scalar.activation(cth[:, :, :], cT[:, :, :], ACT.Tanh, scale=0.5).then_inc(c_tanh, 1)
            for n, (lo, hi) in enumerate(((0, 512), (512, 768)) * 2):
                act.wait_ge(mod_ps, n + 1)
                nc.scalar.copy(mod[:, n // 2, lo:hi], pm[n][:, 0:hi - lo]).then_inc(mod_sb, 1)
            roots.serve(act, nc, rstd[:, :], rtmp[:, :])
            roots.serve(act, nc, rstd[:, :], rtmp[:, :])
            for j in range(NBK):
                act.wait_ge(hT_ps, j + 1)
                nc.scalar.copy(hT[:, j * BLK:(j + 1) * BLK], pm[4 + j % 2][:, :]).then_inc(hT_sb, 1)
            for j in range(NBK):
                act.wait_ge(proj_ps, 2 * j + 1)
                nc.scalar.activation(scan["xp"][:, j * BLK:(j + 1) * BLK], pm[2 * (j % 2)][:, :], ACT.Identity,
                                     bias=binc[:, 0:1]).then_inc(proj_sb, 1)
                act.wait_ge(proj_ps, 2 * j + 2)
                if j >= 2:
                    act.wait_ge(gate_used, j - 1)
                nc.scalar.activation(gate[:, j % 2, :], pm[2 * (j % 2) + 1][:, :], ACT.Identity,
                                     bias=binc[:, 1:2]).then_inc(proj_sb, 1)
                act.wait_ge(w_scaled, 1)
                nc.scalar.activation(gth[:, j % 2, :], pm[2 * (j % 2) + 1][:, :], ACT.Tanh,
                                     bias=binh[:, 0:1], scale=0.5).then_inc(gate_sb, 1)

        @block.vector
        def _(dve):
            v = nc.vector
            chain = Chain(dve, v_chain)
            dve.wait_ge(c_tanh, 1)
            chain(v.scalar_tensor_tensor(cth[:, :, :], cth[:, :, :], 1.0, cT[:, :, :], ALU.add, ALU.mult))
            for l in range(2):
                v.tensor_scalar(crep[:, l, :, :], cth[:, l, :].unsqueeze(1).to_broadcast([P, U, NB]), 0.5, None,
                                ALU.mult).then_inc(c_rep, 1)
            chain(v.tensor_scalar(winT[:, :], winT[:, :], gn[:, 0:1], None, ALU.mult))
            chain(v.tensor_scalar(scan["woT"][:, :], scan["woT"][:, :], 0.5, None, ALU.mult))
            v.tensor_scalar(binh[:, :], binc[:, 1:2], 0.5, None, ALU.mult).then_inc(w_scaled, 1)
            chain(v.tensor_copy(scan["A"][:, :].rearrange("p (s b) -> p s b", b=NB),
                                am[:, :].unsqueeze(2).to_broadcast([P, NS, NB])))
            dve.wait_ge(csum_ps, 1)
            v.tensor_copy(csum[:, :], pm[7][:, 0:NS]).then_inc(csum_sb, 1)
            dve.wait_ge(mod_sb, 4)
            for l in range(2):
                for m in (1, 4):
                    chain(v.tensor_scalar(mod[:, l, m * P:(m + 1) * P], mod[:, l, m * P:(m + 1) * P], 1.0, None,
                                          ALU.add))
                for m in (2, 5):
                    g = mod[:, l, m * P:(m + 1) * P]
                    chain(v.tensor_scalar(guard[:, 0, :], g, 0.0, 2.0, ALU.is_ge, ALU.mult))
                    chain(v.scalar_tensor_tensor(guard[:, 1, :], g, -1.0, g, ALU.mult, ALU.max))
                    chain(v.tensor_scalar(guard[:, 1, :], guard[:, 1, :], 0.25, None, ALU.max))
                    chain(v.scalar_tensor_tensor(g, guard[:, 0, :], -1.0, guard[:, 1, :], ALU.add, ALU.mult))
            dve.wait_ge(x_in, 16)
            layer_norm(dve, v, chain, roots, x[:, :, :].rearrange("p (c o) e -> p c o e", o=2)[:, :, 0, :], h, NC,
                       stats, mv, rstd, rtmp, mod[:, 0, P:2 * P], mod[:, 0, 0:P])
            chain(v.tensor_tensor(sq[:, :, :], h[:, :, :], h[:, :, :], ALU.mult))
            chain(v.tensor_reduce(ms[:, :], sq[:, :, :], AX.X, ALU.add))
            chain(v.tensor_scalar(ms[:, :], ms[:, :], 1.0 / P, RMS_EPS, ALU.mult, ALU.add))
            roots.rsqrt(dve, v, chain, ms[:, :], rstd[:, :], rtmp[:, :])
            v.tensor_tensor(h[:, :, :], h[:, :, :], rstd[:, :].unsqueeze(2).to_broadcast([P, NC, P]),
                            ALU.mult).then_inc(h_ready, 1)
            for j in range(NBK):
                dve.wait_ge(gate_sb, j + 1)
                v.scalar_tensor_tensor(scan["gate"][:, j * BLK:(j + 1) * BLK], gth[:, j % 2, :], 1.0,
                                       gate[:, j % 2, :], ALU.add, ALU.mult).then_inc(gate_used, 1)

        @block.tensor
        def _(pe):
            mm = nc.tensor.matmul
            pe.wait_ge(w_in, ALL_W)
            pe.wait_ge(id_ready, 2)
            mm(pm[7][:, 0:NS], ones[:, :], cm[:, :], start=True, stop=True).then_inc(csum_ps, 1)
            pe.wait_ge(c_rep, 2)
            for n, (lo, hi) in enumerate(((0, 512), (512, 768)) * 2):
                mm(pm[n][:, 0:hi - lo], crep[:, n // 2, :, :].rearrange("p u b -> p (u b)"),
                   wmod[:, n // 2, lo:hi], start=True, stop=True).then_inc(mod_ps, 1)
            pe.wait_ge(h_ready, 1)
            for j in range(NBK):
                if j >= 2:
                    pe.wait_ge(hT_sb, j - 1)
                for q in range(TPB):
                    last = nc.tensor.transpose(pm[4 + j % 2][:, q * P:(q + 1) * P], h[:, j * TPB + q, :], ident[:, :])
                last.then_inc(hT_ps, 1)
            for j in range(NBK):
                pe.wait_ge(hT_sb, j + 1)
                for half in range(2):
                    if j == 0:
                        pe.wait_ge(mod_sb, 4)
                    if j >= 2:
                        pe.wait_ge(proj_sb, 2 * (j - 2) + half + 1)
                        pe.wait_ge(gate_sb, j - 1)
                    mm(pm[2 * (j % 2) + half][:, :], winT[:, half * P:(half + 1) * P], hT[:, j * BLK:(j + 1) * BLK],
                       start=True, stop=True).then_inc(proj_ps, 1)


def scan_phase(nc, d, keep, scan):
    x, mod, ones = keep["x"], keep["mod"], keep["ones"]
    A, Bm, Dv, xp, gate = scan["A"], scan["Bm"], scan["Dv"], scan["xp"], scan["gate"]
    hist, diagC, woT, bo = scan["hist"], scan["diagC"], scan["woT"], scan["bo"]
    S_ACT = 22
    with ExitStack() as ctx:
        sb = lambda name, shape, dt=F32: ctx.enter_context(nc.sbuf_tensor(name, shape, dt))
        sem = lambda name: ctx.enter_context(nc.semaphore(name))
        xb = sb("xb", [P, 2, U, NS * NB])
        xc = sb("xc", [P, 2, P])
        g = sb("g", [P, NS * NB])
        yg = sb("yg", [P, P])
        upd = sb("upd", [P, 2, P])
        zp = [ctx.enter_context(nc.psum_tensor(f"zp{i}", [P, 512], F32)) for i in range(len(PARTED))]
        py = [ctx.enter_context(nc.psum_tensor(f"py{i}", [P, 512], F32)) for i in range(2)]
        po = ctx.enter_context(nc.psum_tensor("po", [P, 512], F32))
        decayed, z_ready, h_done = sem("decayed"), sem("z_ready"), sem("h_done")
        xb_act, xb_pool, xb_dve = sem("xb_act"), sem("xb_pool"), sem("xb_dve")
        xc_ready = sem("xc_ready")
        y_ready, yg_ready, out_ready, upd_ready, x_updated = (
            sem("y_ready"), sem("yg_ready"), sem("out_ready"), sem("upd_ready"), sem("x_updated"))
        block = ctx.enter_context(nc.Block())
        OUT_AT = 13
        N_POOL = NS - S_ACT
        N_DVE = 24

        def chunks(eng, body, peeled):
            for c in range(peeled):
                body(c, c % 2, c == 0)
            with eng.Fori(peeled // 2, NC // 2) as i:
                body(2 * i, 0, False)
                body(2 * i + 1, 1, False)

        def xb_slot(s, par):
            return xb[:, par, :, s * NB:(s + 1) * NB]

        def xp_chunk(c):
            return xp[:, bass.ds(c * P, P)] if not isinstance(c, int) else xp[:, c * P:(c + 1) * P]

        @block.vector
        def _(dve):
            v = nc.vector

            def output(c, par):
                dve.wait_ge(y_ready, c + 1)
                gs = gate[:, bass.ds(c * P, P)] if not isinstance(c, int) else gate[:, c * P:(c + 1) * P]
                v.tensor_tensor(yg[:, :], py[par][:, 0:P], gs, ALU.mult).then_inc(yg_ready, 1)

            def gate_output(c, par):
                dve.wait_ge(out_ready, c + 1)
                if not (isinstance(c, int) and c < 2):
                    dve.wait_ge(x_updated, c - 1)
                v.tensor_tensor(upd[:, par, :], po[:, 0:P], mod[:, 0, 2 * P:3 * P], ALU.mult).then_inc(upd_ready, 1)

            def body(c, par, first):
                dve.wait_ge(xb_act, S_ACT * (c + 1))
                dve.wait_ge(xb_pool, N_POOL * (c + 1) - N_DVE)
                for u in range(U):
                    prev = hist[:, par, u - 1, :] if u else hist[:, 1 - par, U - 1, :]
                    step = c * U + u

                    def decay(j):
                        lo, hi = PARTED[j]
                        if not (first and u == 0):
                            dve.wait_ge(h_done, NPT * step + j + 1 - NPT)
                        v.tensor_tensor(g[:, lo:hi], prev[:, lo:hi], A[:, lo:hi], ALU.mult).then_inc(decayed, 1)

                    def feed(j):
                        lo, hi = PARTED[j]
                        dve.wait_ge(decayed, NPT * step + j + 1)
                        v.tensor_tensor(zp[j][:, 0:hi - lo], g[:, lo:hi], xb[:, par, u, lo:hi], ALU.add)\
                         .then_inc(z_ready, 1)

                    decay(0)
                    decay(1)
                    feed(0)
                    decay(2)
                    feed(1)
                    feed(2)
                    if not first and u == OUT_AT:
                        output(c - 1, 1 - par)
                    if not first and u == U - 1:
                        gate_output(c - 1, 1 - par)

            for s in range(NS - N_DVE, NS):
                v.tensor_scalar(xb_slot(s, 0), xp_chunk(0).rearrange("p (u b) -> p u b", b=NB), Bm[:, s:s + 1], None,
                                ALU.mult).then_inc(xb_dve, 1)
            dve.wait_ge(xb_dve, N_DVE)
            chunks(dve, body, 4)
            output(NC - 1, 1)
            gate_output(NC - 1, 1)

        def make_xb(eng, op, states, c, par, ready):
            for s in states:
                op(xb_slot(s, par), xp_chunk(c).rearrange("p (u b) -> p u b", b=NB), Bm[:, s:s + 1]).then_inc(ready, 1)

        @block.scalar
        def _(act):
            def op(out, in_, scale):
                return nc.scalar.activation(out, in_, ACT.Copy, scale=scale)

            make_xb(act, op, range(S_ACT), 0, 0, xb_act)
            make_xb(act, op, range(S_ACT), 1, 1, xb_act)

            def body(c, par, first):
                made = 0
                for u in range(U):
                    step = c * U + u
                    for j, (lo, hi) in enumerate(PARTED):
                        act.wait_ge(z_ready, NPT * step + j + 1)
                        if u == 0 and j == 0 and not (isinstance(c, int) and c < 2):
                            act.wait_ge(y_ready, c - 1)
                        nc.scalar.activation(hist[:, par, u, lo:hi], zp[j][:, 0:hi - lo], ACT.Tanh)\
                          .then_inc(h_done, 1)
                    if not (isinstance(c, int) and c == 0):
                        upto = S_ACT * (u + 1) // U
                        make_next(c, par, range(made, upto), u)
                        made = upto

            def make_next(c, par, states, u):
                if u == 0:
                    act.wait_ge(z_ready, NPT * U * c)
                make_xb(act, op, states, c + 1, 1 - par, xb_act)

            body(0, 0, True)
            body(1, 1, False)
            with act.Fori(1, NC // 2 - 1) as i:
                body(2 * i, 0, False)
                body(2 * i + 1, 1, False)
            body(NC - 2, 0, False)
            for u in range(U):
                for j, (lo, hi) in enumerate(PARTED):
                    step = (NC - 1) * U + u
                    act.wait_ge(z_ready, NPT * step + j + 1)
                    if u == 0 and j == 0:
                        act.wait_ge(y_ready, NC - 2)
                    nc.scalar.activation(hist[:, 1, u, lo:hi], zp[j][:, 0:hi - lo], ACT.Tanh)\
                      .then_inc(h_done, 1)

        @block.gpsimd
        def _(pool):
            def update(c, par):
                pool.wait_ge(upd_ready, c + 1)
                xs = x[:, bass.ds(2 * c, 2), :] if not isinstance(c, int) else x[:, 2 * c:2 * c + 2, :]
                nc.gpsimd.tensor_tensor(xs, xs, upd[:, par, :].unsqueeze(1).to_broadcast([P, 2, P]), ALU.add)\
                  .then_inc(x_updated, 1)

            def chunk(c, par, slot_used):
                if slot_used:
                    pool.wait_ge(z_ready, NPT * U * (c - 1))
                nc.gpsimd.tensor_copy(xc[:, par, :], xp_chunk(c)).then_inc(xc_ready, 1)
                pool.wait_ge(xc_ready, c + 1)
                nc.gpsimd.tensor_tensor(xb_slot(S_ACT, par), xc[:, par, :].rearrange("p (u b) -> p u b", b=NB),
                                        Bm[:, S_ACT:S_ACT + 1].unsqueeze(1).to_broadcast([P, U, NB]), ALU.mult)\
                  .then_inc(xb_pool, 1)
                for s in range(S_ACT + 1, NS if slot_used or par else NS - N_DVE):
                    nc.gpsimd.tensor_scalar(xb_slot(s, par), xc[:, par, :].rearrange("p (u b) -> p u b", b=NB),
                                            Bm[:, s:s + 1], 1.0, ALU.mult, ALU.mult).then_inc(xb_pool, 1)

            chunk(0, 0, False)
            chunk(1, 1, False)
            chunk(2, 0, True)
            chunk(3, 1, True)
            update(0, 0)
            with pool.Fori(2, NC // 2) as i:
                chunk(2 * i, 0, True)
                update(2 * i - 3, 1)
                chunk(2 * i + 1, 1, True)
                update(2 * i - 2, 0)
            for c in range(NC - 3, NC):
                update(c, c % 2)
            pool.wait_ge(x_updated, NC)

        @block.tensor
        def _(pe):
            mm = nc.tensor.matmul

            def body(c, par, first):
                pe.wait_ge(h_done, NPT * U * (c + 1))
                mm(py[par][:, 0:P], diagC[:, NS, :], xp_chunk(c), start=True, stop=False)
                for s in range(NS):
                    last = mm(py[par][:, 0:P], diagC[:, s, :], hist[:, par, :, s * NB:(s + 1) * NB],
                              start=False, stop=(s == NS - 1))
                last.then_inc(y_ready, 1)
                pe.wait_ge(yg_ready, c + 1)
                if not first:
                    pe.wait_ge(upd_ready, c)
                mm(po[:, 0:P], yg[:, :], woT[:, :], start=True, stop=False)
                mm(po[:, 0:P], ones[0:1, :], bo[:, :], start=False, stop=True).then_inc(out_ready, 1)

            chunks(pe, body, 2)


class Normed:

    POOL_SHIFTS = (2, 5)
    ACT_BLOCKS = (6, 7)

    def __init__(self, nc, sb, sem, keep, layer, half, hT, banks, tag):
        self.nc, self.keep, self.hT, self.banks = nc, keep, hT, banks
        self.shift = keep["mod"][:, layer, (3 * half) * P:(3 * half + 1) * P]
        self.scale = keep["mod"][:, layer, (3 * half + 1) * P:(3 * half + 2) * P]
        self.h = sb(f"h{tag}", [P, NT, P])
        self.stats = sb(f"stats{tag}", [P, NT, 6])
        self.mv = sb(f"mv{tag}", [P, NT, 2])
        self.rstd = sb(f"rstd{tag}", [P, NT])
        self.tmp = sb(f"rtmp{tag}", [P, NT])
        self.offset = sb(f"offset{tag}", [P, NT])
        self.moments_ready, self.centred, self.scaled = sem(f"moments{tag}"), sem(f"centred{tag}"), sem(f"scaled{tag}")
        self.centred_act = sem(f"centred_act{tag}")
        self.h_pool = sem(f"h_pool{tag}")
        self.h_ready, self.t_ready, self.hT_ready = sem(f"h_ready{tag}"), sem(f"t_ready{tag}"), sem(f"hT_ready{tag}")
        self.roots = Roots(sem(f"var_ready{tag}"), sem(f"root_ready{tag}"))

    def block(self, t, j):
        return t[:, j * TPB:(j + 1) * TPB, :]

    def wide(self, row):
        return row.unsqueeze(1).to_broadcast([P, TPB, P])

    def vector(self, dve, chain):
        v = self.nc.vector
        moments(v, chain, self.keep["x"], NT, self.stats, self.mv)
        self.roots.rsqrt(dve, v, chain, self.mv[:, :, 1], self.rstd[:, :], self.tmp[:, :])
        v.scalar_tensor_tensor(self.offset[:, :], self.mv[:, :, 0], -1.0, self.rstd[:, :], ALU.mult, ALU.mult)\
         .then_inc(self.moments_ready, 1)
        dve.wait_ge(self.moments_ready, 1)
        for step in range(NBLK + 2):
            if step < NBLK and step not in self.ACT_BLOCKS:
                for k in range(step * TPB, (step + 1) * TPB):
                    last = v.tensor_scalar(self.h[:, k, :], self.keep["x"][:, k, :], self.mv[:, k, 0:1],
                                           self.rstd[:, k:k + 1], ALU.subtract, ALU.mult)
                last.then_inc(self.centred, 1)
            j = step - 1
            if 0 <= j < NBLK:
                by_act = sum(i <= j for i in self.ACT_BLOCKS)
                if j in self.ACT_BLOCKS:
                    dve.wait_ge(self.centred_act, by_act)
                else:
                    dve.wait_ge(self.centred, j + 1 - by_act)
                v.tensor_tensor(self.block(self.h, j), self.block(self.h, j), self.wide(self.scale), ALU.mult)\
                 .then_inc(self.scaled, 1)
            j = step - 2
            if j >= 0 and j not in self.POOL_SHIFTS:
                dve.wait_ge(self.scaled, j + 1)
                v.tensor_tensor(self.block(self.h, j), self.block(self.h, j), self.wide(self.shift), ALU.add)\
                 .then_inc(self.h_ready, 1)

    def gpsimd(self, pool):
        for j in self.POOL_SHIFTS:
            pool.wait_ge(self.scaled, j + 1)
            self.nc.gpsimd.tensor_tensor(self.block(self.h, j), self.block(self.h, j), self.wide(self.shift), ALU.add)\
                .then_inc(self.h_pool, 1)

    def scalar(self, act):
        self.roots.serve(act, self.nc, self.rstd[:, :], self.tmp[:, :])
        act.wait_ge(self.moments_ready, 1)
        for j in self.ACT_BLOCKS:
            for k in range(j * TPB, (j + 1) * TPB):
                last = self.nc.scalar.activation(self.h[:, k, :], self.keep["x"][:, k, :], ACT.Identity,
                                                 bias=self.offset[:, k:k + 1], scale=self.rstd[:, k:k + 1])
            last.then_inc(self.centred_act, 1)
        for j in range(NBLK):
            act.wait_ge(self.t_ready, j + 1)
            self.nc.scalar.copy(self.hT[:, j * BLK:(j + 1) * BLK], self.banks[j % 2][:, :]).then_inc(self.hT_ready, 1)

    def tensor(self, pe):
        for j in range(NBLK):
            from_pool = sum(i <= j for i in self.POOL_SHIFTS)
            if j in self.POOL_SHIFTS:
                pe.wait_ge(self.h_pool, from_pool)
            else:
                pe.wait_ge(self.h_ready, j + 1 - from_pool)
            if j >= 2:
                pe.wait_ge(self.hT_ready, j - 1)
            for q in range(TPB):
                last = self.nc.tensor.transpose(self.banks[j % 2][:, q * P:(q + 1) * P],
                                                self.h[:, j * TPB + q, :], self.keep["ident"][:, :])
            last.then_inc(self.t_ready, 1)


def softmax_probs(dve, nc, chain, probs, logits_ps, bias, top, n, asked, answered):
    v = nc.vector
    wide = lambda t: t.unsqueeze(2).to_broadcast([P, NT, n])
    if bias is None:
        chain(v.tensor_copy(probs, logits_ps))
    else:
        chain(v.tensor_tensor(probs, logits_ps, bias.unsqueeze(1).to_broadcast([P, NT, n]), ALU.add))
    chain(v.tensor_reduce(top, probs, AX.X, ALU.max))
    v.tensor_tensor(probs, probs, wide(top), ALU.subtract).then_inc(asked, 1)
    dve.wait_ge(answered, 1)
    chain(v.tensor_reduce(top, probs, AX.X, ALU.add))
    chain(v.reciprocal(top, top))
    chain(v.tensor_tensor(probs, probs, wide(top), ALU.mult))


def first_of_max(nc, chain, keys, rank, hot, top, n):
    v = nc.vector
    wide = lambda t: t.unsqueeze(2).to_broadcast([P, NT, n])
    chain(v.tensor_reduce(top, keys, AX.X, ALU.max))
    chain(v.tensor_tensor(hot, keys, wide(top), ALU.is_equal))
    chain(v.tensor_tensor(hot, hot, rank.unsqueeze(1).to_broadcast([P, NT, n]), ALU.mult))
    chain(v.tensor_reduce(top, hot, AX.X, ALU.max))
    chain(v.tensor_tensor(hot, hot, wide(top), ALU.is_equal))


def experts0(nc, d, keep):
    x, mod, ident = keep["x"], keep["mod"], keep["ident"]
    with ExitStack() as ctx:
        sb = lambda name, shape, dt=F32: ctx.enter_context(nc.sbuf_tensor(name, shape, dt))
        sem = lambda name: ctx.enter_context(nc.semaphore(name))
        pm = [ctx.enter_context(nc.psum_tensor(f"px{i}", [P, 512], F32)) for i in range(8)]
        hT = sb("hTx", [P, NT * P])
        W = sb("W0", [P, NE0 * P])
        gw = sb("gw0", [P, NX0])
        gb = sb("gb0", [P, NX0])
        eb = sb("eb0", [NE0, P])
        rank = sb("rank0", [P, NX0])
        ranki = sb("ranki0", [P, NX0], mybir.dt.int32)
        probs = sb("probs0", [P, NT, NX0])
        hot = sb("hot0", [P, 2, NT, NX0])
        top = sb("top0", [P, NT])
        den = sb("den0", [P, NT])
        cw = sb("cw0", [P, NT, NE0])
        cwT = sb("cwT0", [NE0, NT * P])
        acc = sb("acc0", [P, 2, 2, P])
        w_in, v_chain, ranks = sem("w_inx"), sem("v_chainx"), sem("ranks0")
        logits_ready, exp_asked, exp_done = sem("logits_ready0"), sem("exp_asked0"), sem("exp_done0")
        cw_ready, cwT_ps, cwT_ready = sem("cw_ready0"), sem("cwT_ps0"), sem("cwT_ready0")
        y_ready, y_used, seeded, x_added = sem("y_readyx"), sem("y_usedx"), sem("seeded0"), sem("x_added0")
        bias_ps, scaled = sem("bias_ps"), sem("scaled0")
        EH = NE0 // 2
        UNITS = 3
        norm = Normed(nc, sb, sem, keep, 0, 1, hT, pm[0:2], "x")
        block = ctx.enter_context(nc.Block())

        @block.sync
        def _(sp):
            for dst, src in ((gw[:, :], d["gw0"]), (gb[:, :], d["gb0"].to_broadcast([P, NX0])),
                             (W[:, :], d["ew0"]), (eb[:, :], d["eb0"])):
                sp.dma_start(dst, src).then_inc(w_in, 16)

        @block.gpsimd
        def _(pool):
            norm.gpsimd(pool)
            nc.gpsimd.iota(ranki[:, :], pattern=[[-1, NX0]], base=NX0, channel_multiplier=0).then_inc(ranks, 1)
            pool.wait_ge(ranks, 1)
            nc.gpsimd.tensor_copy(rank[:, :], ranki[:, :]).then_inc(ranks, 1)
            for k2 in range(0, NT, 2):
                par = (k2 // 2) % 2
                pool.wait_ge(y_used, (k2 + 2) * NE0)
                nc.gpsimd.tensor_tensor(acc[:, par, :, :], acc[:, par, :, :],
                                        mod[:, 0, 5 * P:6 * P].unsqueeze(1).to_broadcast([P, 2, P]), ALU.mult)\
                  .then_inc(scaled, 1)
                pool.wait_ge(scaled, k2 // 2 + 1)
                nc.gpsimd.tensor_tensor(x[:, k2:k2 + 2, :], x[:, k2:k2 + 2, :], acc[:, par, :, :], ALU.add)\
                  .then_inc(x_added, 1)
            pool.wait_ge(x_added, NT // 2)

        @block.scalar
        def _(act):
            norm.scalar(act)
            act.wait_ge(exp_asked, 1)
            nc.scalar.activation(probs[:, :, :], probs[:, :, :], ACT.Exp).then_inc(exp_done, 1)
            for j in range(NBLK):
                act.wait_ge(cwT_ps, j + 1)
                nc.scalar.copy(cwT[:, j * BLK:(j + 1) * BLK], pm[2 + j % 2][0:NE0, :]).then_inc(cwT_ready, 1)
            for k2 in range(0, NT, 2):
                act.wait_ge(bias_ps, k2 // 2 + 1)
                if k2 >= 4:
                    act.wait_ge(x_added, k2 // 2 - 1)
                for a in range(2):
                    nc.scalar.copy(acc[:, (k2 // 2) % 2, a, :], pm[6 + a][:, 0:P]).then_inc(seeded, 1)

        @block.vector
        def _(dve):
            v = nc.vector
            chain = Chain(dve, v_chain)
            norm.vector(dve, chain)
            dve.wait_ge(w_in, 16 * 4)
            dve.wait_ge(ranks, 2)
            dve.wait_ge(logits_ready, 1)
            softmax_probs(dve, nc, chain, probs[:, :, :], pm[4][:, 0:NT * NX0].rearrange("p (k e) -> p k e", e=NX0),
                          gb[:, :], top[:, :], NX0, exp_asked, exp_done)
            wide = lambda t: t.unsqueeze(2).to_broadcast([P, NT, NX0])
            chain(v.tensor_copy(hot[:, 1, :, :], probs[:, :, :]))
            first_of_max(nc, chain, hot[:, 1, :, :], rank[:, :], hot[:, 0, :, :], top[:, :], NX0)
            chain(v.scalar_tensor_tensor(hot[:, 1, :, :], hot[:, 0, :, :], -4.0, probs[:, :, :], ALU.mult, ALU.add))
            chain(v.tensor_tensor(hot[:, 0, :, :], hot[:, 0, :, :], probs[:, :, :], ALU.mult))
            chain(v.tensor_copy(cw[:, :, :], hot[:, 0, :, 0:NE0]))
            first_of_max(nc, chain, hot[:, 1, :, :], rank[:, :], hot[:, 0, :, :], top[:, :], NX0)
            chain(v.tensor_tensor(hot[:, 0, :, :], hot[:, 0, :, :], probs[:, :, :], ALU.mult))
            chain(v.tensor_tensor(cw[:, :, :], cw[:, :, :], hot[:, 0, :, 0:NE0], ALU.add))
            chain(v.tensor_reduce(den[:, :], cw[:, :, :], AX.X, ALU.add))
            chain(v.tensor_scalar(top[:, :], den[:, :], 0.0, None, ALU.is_le))
            chain(v.tensor_tensor(den[:, :], den[:, :], top[:, :], ALU.add))
            chain(v.reciprocal(den[:, :], den[:, :]))
            chain(v.tensor_tensor(cw[:, :, :], cw[:, :, :], den[:, :].unsqueeze(2).to_broadcast([P, NT, NE0]),
                                  ALU.mult))
            v.sem_inc(cw_ready, 1)
            for k2 in range(0, NT, 2):
                dve.wait_ge(seeded, k2 + 2)
                for half in range(2):
                    unit = k2 + half
                    dve.wait_ge(y_ready, unit + 1)
                    for e in range(EH):
                        for a in range(2):
                            before = unit * NE0 + 2 * e + a
                            if half or e:
                                dve.wait_ge(y_used, before - 1)
                            v.scalar_tensor_tensor(acc[:, (k2 // 2) % 2, a, :],
                                                   pm[unit % UNITS * 2 + a][:, e * P:(e + 1) * P],
                                                   cw[:, k2 + a, half * EH + e:half * EH + e + 1],
                                                   acc[:, (k2 // 2) % 2, a, :], ALU.mult, ALU.add).then_inc(y_used, 1)

        @block.tensor
        def _(pe):
            mm = nc.tensor.matmul
            norm.tensor(pe)
            pe.wait_ge(w_in, 16 * 4)
            for k in range(NT):
                if k % TPB == 0:
                    pe.wait_ge(norm.hT_ready, k // TPB + 1)
                last = mm(pm[4][:, k * NX0:(k + 1) * NX0], hT[:, k * P:(k + 1) * P], gw[:, :], start=True, stop=True)
            last.then_inc(logits_ready, 1)
            pe.wait_ge(cw_ready, 1)
            for j in range(NBLK):
                if j >= 2:
                    pe.wait_ge(cwT_ready, j - 1)
                for q in range(TPB):
                    last = nc.tensor.transpose(pm[2 + j % 2][0:NE0, q * P:(q + 1) * P], cw[:, j * TPB + q, :],
                                               ident[:, :])
                last.then_inc(cwT_ps, 1)
            pe.wait_ge(cwT_ready, NBLK)
            for k2 in range(0, NT, 2):
                if k2 >= 2:
                    pe.wait_ge(seeded, k2)
                for a in range(2):
                    last = mm(pm[6 + a][:, 0:P], cwT[:, (k2 + a) * P:(k2 + a + 1) * P], eb[:, :], start=True, stop=True)
                last.then_inc(bias_ps, 1)
                for half in range(2):
                    unit = k2 + half
                    if unit >= UNITS:
                        pe.wait_ge(y_used, (unit - UNITS + 1) * NE0)
                    for a in range(2):
                        last = mm(pm[unit % UNITS * 2 + a][:, :], hT[:, (k2 + a) * P:(k2 + a + 1) * P],
                                  W[:, half * EH * P:(half + 1) * EH * P], start=True, stop=True)
                    last.then_inc(y_ready, 1)


QK_TERMS = (((0, 0), (0, 1)), ((1, 1), (0, 1)), ((0, 2), (2, 0)))
REL_TERMS = (((0, 0, 1, 1), (0, 1, 0, 1)), ((0, 1, 2, 2), (2, 2, 0, 1)))
PARTS = 3
TOK = NB * SEQ
V4 = 4
W4 = U // V4
KEY_SLOTS = QK_TERMS[0][1] + QK_TERMS[2][1]
TABLE_SLOTS = REL_TERMS[0][1] + REL_TERMS[1][1]
TWIN = TLEN - 2 * (V4 - 1)
TROW = TLEN + 1
JT = SEQ // P


def attention_inputs(nc, d, keep, vals, scratch):
    with ExitStack() as ctx:
        sb = lambda name, shape, dt=F32: ctx.enter_context(nc.sbuf_tensor(name, shape, dt))
        sem = lambda name: ctx.enter_context(nc.semaphore(name))
        pm = [ctx.enter_context(nc.psum_tensor(f"pi{i}", [P, 512], F32)) for i in range(8)]
        hT = sb("hTi", [P, TOK])
        wq, wk, wv = sb("wq", [P, P]), sb("wk", [P, P]), sb("wv", [P, P])
        bq, bk, bks, bv = sb("bq", [P, 1]), sb("bk", [P, 1]), sb("bks", [P, 1]), sb("bv", [P, P])
        table = sb("table", [P, TROW])
        tparts = sb("tparts", [P, PARTS, TROW], BF16)
        rest = sb("rest", [P, 2, BLK])
        nat = sb("nat", [P, 2, PARTS, BLK], BF16)
        qparts = sb("qparts", [P, PARTS, W4, V4, NB, NT], BF16)
        kparts = sb("kparts", [P, PARTS, TOK], BF16)
        hTb = sb("hTb", [P, TOK])
        w_in, t_in, v_chain, bias_ready = sem("w_ini"), sem("t_in"), sem("v_chaini"), sem("bias_ready")
        proj_ready, value_ready, cut_ready = sem("proj_readyi"), sem("value_ready"), sem("cut_ready")
        q_placed, by_seq = sem("q_placed"), sem("by_seq")
        v_ready, v_done, t_cut, stored = sem("v_ready"), sem("v_done"), sem("t_cut"), sem("stored_parts")
        norm = Normed(nc, sb, sem, keep, 1, 0, hT, pm[0:2], "i")
        block = ctx.enter_context(nc.Block())
        NPROJ = 2 * NBLK

        @block.sync
        def _(sp):
            sp.dma_start(table[:, 0:TLEN], d["table"]).then_inc(t_in, 16)
            for dst, src in ((wq[:, :], d["wqT"]), (wk[:, :], d["wkT"]), (wv[:, :], d["wvT"]), (bq[:, :], d["bq"]),
                             (bk[:, :], d["bk"]), (bv[:, :], d["bv"].to_broadcast([P, P]))):
                sp.dma_start(dst, src).then_inc(w_in, 16)
            sp.wait_ge(t_cut, 1)
            for slot, t in enumerate(TABLE_SLOTS):
                sp.dma_start(scratch["t"][:, slot, :, 0:TLEN], tparts[:, t, 0:TLEN]).then_inc(stored, 16)
            sp.wait_ge(q_placed, NBLK)
            for t in range(PARTS):
                sp.dma_start(scratch["q"][t, :, :], qparts[:, t, :, :, :, :].rearrange("p w v b k -> p (w v b k)"))\
                  .then_inc(stored, 16)
            sp.wait_ge(cut_ready, NPROJ)
            for slot, t in enumerate(KEY_SLOTS):
                sp.dma_start(scratch["k"][:, slot, :, :], kparts[:, t, :]).then_inc(stored, 16)
            sp.wait_ge(stored, 16 * (len(TABLE_SLOTS) + PARTS + len(KEY_SLOTS)))

        @block.scalar
        def _(act):
            norm.scalar(act)
            act.wait_ge(w_in, 16 * 6)
            act.wait_ge(bias_ready, 1)
            for n in range(NPROJ):
                par, j = n % 2, n % NBLK
                is_q = n < NBLK
                act.wait_ge(proj_ready, n + 1)
                if n >= 2:
                    act.wait_ge(cut_ready, n - 1)
                nc.scalar.activation(rest[:, par, :], pm[2 + par][:, :], ACT.Identity,
                                     bias=bq[:, 0:1] if is_q else bks[:, 0:1],
                                     scale=1.0 if is_q else HD ** -0.5).then_inc(value_ready, 1)
                if is_q:
                    act.wait_ge(cut_ready, n + 1)
                    for t in range(PARTS):
                        last = nc.scalar.copy(
                            qparts[:, t, :, :, :, j * TPB:(j + 1) * TPB].rearrange("p w v b k -> p k (w v b)"),
                            nat[:, par, t, :].rearrange("p (k c) -> p k c", c=P))
                    last.then_inc(q_placed, 1)

        @block.vector
        def _(dve):
            v = nc.vector
            chain = Chain(dve, v_chain)
            dve.wait_ge(w_in, 16 * 6)
            v.tensor_scalar(bks[:, :], bk[:, :], HD ** -0.5, None, ALU.mult).then_inc(bias_ready, 1)
            dve.wait_ge(t_in, 16)
            T = slice(0, TLEN)
            chain(v.tensor_copy(tparts[:, 0, T], table[:, T]))
            chain(v.tensor_tensor(table[:, T], table[:, T], tparts[:, 0, T], ALU.subtract))
            chain(v.tensor_copy(tparts[:, 1, T], table[:, T]))
            v.tensor_tensor(tparts[:, 2, T], table[:, T], tparts[:, 1, T], ALU.subtract).then_inc(t_cut, 1)
            norm.vector(dve, chain)
            for n in range(NPROJ):
                par = n % 2
                dve.wait_ge(value_ready, n + 1)
                j = n % NBLK
                p0, p1, p2 = (nat[:, par, t, :] if n < NBLK else kparts[:, t, j * BLK:(j + 1) * BLK]
                              for t in range(PARTS))
                if 2 <= n < NBLK:
                    dve.wait_ge(q_placed, n - 1)
                chain(v.tensor_copy(p0, rest[:, par, :]))
                chain(v.tensor_tensor(rest[:, par, :], rest[:, par, :], p0, ALU.subtract))
                chain(v.tensor_copy(p1, rest[:, par, :]))
                v.tensor_tensor(p2, rest[:, par, :], p1, ALU.subtract).then_inc(cut_ready, 1)
            for m in range(JT * NB // TPB):
                dve.wait_ge(v_ready, m + 1)
                v.tensor_tensor(vals[:, m * TPB:(m + 1) * TPB, :], pm[4 + m % 2][:, :].rearrange("p (q e) -> p q e", q=TPB),
                                bv[:, :].unsqueeze(1).to_broadcast([P, TPB, P]), ALU.add).then_inc(v_done, 1)

        @block.gpsimd
        def _(pool):
            norm.gpsimd(pool)
            for j in range(NBLK):
                pool.wait_ge(norm.hT_ready, j + 1)
                for c in range(2):
                    src = hT[:, (2 * j + c) * 2 * P:(2 * j + c + 1) * 2 * P].rearrange("p (o u b) -> p o u b", o=2, u=U)
                    dst = hTb[:, :].rearrange("p (b c u o) -> p c o u b", b=NB, u=U, o=2)[:, 2 * j + c, :, :, :]
                    nc.gpsimd.tensor_copy(dst, src).then_inc(by_seq, 1)

        @block.tensor
        def _(pe):
            mm = nc.tensor.matmul
            norm.tensor(pe)
            pe.wait_ge(w_in, 16 * 6)
            for n in range(NPROJ):
                j = n % NBLK
                if n < NBLK:
                    pe.wait_ge(norm.hT_ready, j + 1)
                if n >= 2:
                    pe.wait_ge(value_ready, n - 1)
                if n == NBLK:
                    pe.wait_ge(by_seq, 2 * NBLK)
                w, src = (wq, hT) if n < NBLK else (wk, hTb)
                mm(pm[2 + n % 2][:, :], w[:, :], src[:, j * BLK:(j + 1) * BLK], start=True, stop=True)\
                  .then_inc(proj_ready, 1)
            for m in range(JT * NB // TPB):
                if m >= 2:
                    pe.wait_ge(v_done, m - 1)
                for q in range(TPB):
                    jt, b = divmod(m * TPB + q, NB)
                    last = mm(pm[4 + m % 2][:, q * P:(q + 1) * P], hTb[:, b * SEQ + jt * P:b * SEQ + (jt + 1) * P],
                              wv[:, :], start=True, stop=True)
                last.then_inc(v_ready, 1)


def attention(nc, d, keep, vals, scratch, ctxt):
    ident = keep["ident"]
    GRP = 4
    BG = NB // 2
    RING = 2
    MIXED = GRP * U * BG
    STEPS = 2 * NT
    with ExitStack() as ctx:
        sb = lambda name, shape, dt=F32: ctx.enter_context(nc.sbuf_tensor(name, shape, dt))
        sem = lambda name: ctx.enter_context(nc.semaphore(name))
        qs = [[sb(f"qs{p}{m}", [P, U, NB, NT], BF16) for m in range(len(QK_TERMS))] for p in range(2)]
        qr = [[sb(f"qr{p}{m}", [P, W4, V4, NB, NT], BF16) for m in range(len(REL_TERMS))] for p in range(2)]
        ks = [[sb(f"ks{p}{m}", [P, SEQ], BF16) for m in range(2)] for p in range(2)]
        tb = [[sb(f"tb{p}{m}", [P, TWIN], BF16) for m in range(len(REL_TERMS))] for p in range(2)]
        vh = sb("vh", [P, 2, JT, NB, HD])
        own2 = sb("own2", [P, 4 * BG])
        own = sb("own", [P, BG])
        part = sb("part", [P, 2, GRP, HD])
        masked = sb("masked", [P, 2, GRP * U, NB])
        prob = [sb(f"prob{i}", [P, SEQ]) for i in range(2)]
        probT = [sb(f"probT{i}", [P, JT, GRP * P]) for i in range(2)]
        ntop = sb("ntop", [P, NT])
        rsum = sb("rsum", [P, 2, NT])
        score_ps = [ctx.enter_context(nc.psum_tensor(f"score{i}", [P, 512], F32)) for i in range(RING)]
        turned_ps = [ctx.enter_context(nc.psum_tensor(f"turned{i}", [P, 512], F32)) for i in range(2)]
        mixed_ps = [ctx.enter_context(nc.psum_tensor(f"mixed{i}", [P, 512], F32)) for i in range(2)]
        untangled_ps = ctx.enter_context(nc.psum_tensor("untangled", [P, 512], F32))
        zeroed, head_in = [sem("zeroed0"), sem("zeroed1")], [sem("head_in0"), sem("head_in1")]
        mask_zeroed, mask_ready, v_head = sem("mask_zeroed"), sem("mask_ready"), sem("v_head")
        scores, top_ready, prob_ready, turned, turned_sb = (sem("scores"), sem("top_ready"), sem("prob_ready"),
                                                            sem("turned"), sem("turned_sb"))
        mixed, masked_ready, untangled, rinv_ready, part_ready, ctx_ready = (
            sem("mixed"), sem("masked_ready"), sem("untangled"), sem("rinv_ready"), sem("part_ready"), sem("ctx_ready"))
        block = ctx.enter_context(nc.Block())
        PS = P * TOK
        TRANSFERS = len(REL_TERMS) * (1 + 2 * V4) + 2 + len(QK_TERMS) * NB
        ARRIVED = 16 * TRANSFERS

        def load_head(eng, p, h, first=False):

            def start(dst, base, dims):
                src = bass.AP(base.tensor, base.offset + dims[0], dims[1])
                eng.dma_start(dst, src).then_inc(head_in[p], 16)

            for m in range(len(REL_TERMS)):
                start(tb[p][m][:, :], scratch["t"],
                      (h * (len(TABLE_SLOTS) * HD * TROW) + m * 4 * HD * TROW,
                       [[2, V4], [TROW, 4 * HD], [1, TWIN]]))
            for m in range(2):
                start(ks[p][m][:, :], scratch["k"],
                      (h * (len(KEY_SLOTS) * HD * TOK) + m * 2 * HD * TOK, [[SEQ, NB], [TOK, 2 * HD], [1, SEQ]]))
            if first:
                eng.wait_ge(zeroed[p], len(QK_TERMS) + len(REL_TERMS))
            for m, ((t0, t1), _) in enumerate(QK_TERMS):
                for b in range(NB):
                    start(qs[p][m][16 * b:16 * b + 16, :, b, :], scratch["q"],
                          (h * (HD * TOK) + t0 * PS + b * NT,
                           [[(t1 - t0) * PS, 2], [TOK, HD], [NB * NT, U], [1, NT]]))
            for m, (ts, _) in enumerate(REL_TERMS):
                for v in range(V4):
                    for a in range(2):
                        at = 32 * (V4 - 1 - v) + 16 * a
                        start(qr[p][m][at:at + 16, :, v, :, :].rearrange("p w b k -> p w (b k)"), scratch["q"],
                              (h * (HD * TOK) + ts[2 * a] * PS + v * NB * NT,
                               [[(ts[2 * a + 1] - ts[2 * a]) * PS, 2], [TOK, HD], [V4 * NB * NT, W4], [1, NB * NT]]))

        @block.sync
        def _(sp):
            load_head(sp, 0, 0, True)
            load_head(sp, 1, 1, True)
            with sp.Fori(1, HEADS // 2) as i:
                for p in range(2):
                    sp.wait_ge(scores, (2 * i - 1 + p) * NT)
                    load_head(sp, p, 2 * i + p)

        def before(i, K):
            return K >= 0 or not (isinstance(i, int) and i == 0)

        @block.gpsimd
        def _(pool):
            for p in range(2):
                for t in qr[p]:
                    nc.gpsimd.memset(t[:, :, :, :, :], 0.0).then_inc(zeroed[p], 1)
            nc.gpsimd.memset(masked[:, :, :, :], 0.0).then_inc(mask_zeroed, 1)

            def head(p, h, used):
                if used:
                    pool.wait_ge(mixed, (h - 1) * (NT // GRP))
                src = vals[:, :, bass.ds(h * HD, HD)] if not isinstance(h, int) else vals[:, :, h * HD:(h + 1) * HD]
                nc.gpsimd.tensor_copy(vh[:, p, :, :, :].rearrange("p j b d -> p (j b) d"), src).then_inc(v_head, 1)

            head(0, 0, False)
            head(1, 1, False)
            with pool.Fori(1, HEADS // 2) as i:
                head(0, 2 * i, True)
                head(1, 2 * i + 1, True)

        @block.tensor
        def _(pe):
            mm = nc.tensor.matmul

            def score(i, K):
                p, k = divmod(K, NT)
                if k == 0:
                    pe.wait_ge(head_in[p], ARRIVED * (i + 1))
                out = score_ps[K % RING]
                if before(i, K - RING):
                    pe.wait_ge(prob_ready, i * STEPS + K + 1 - RING)
                c, o = divmod(k, 2)
                for m in range(len(REL_TERMS)):
                    for w in range(W4):
                        s = SEQ - 1 - 2 * U * c - o - 2 * V4 * w - 2 * (V4 - 1)
                        mm(out[32 * w:32 * w + 32, :],
                           qr[p][m][:, w, :, :, k].rearrange("p v b -> p (v b)"), tb[p][m][:, s:s + SEQ],
                           start=(m == 0), stop=False)
                for m in range(len(QK_TERMS)):
                    last = mm(out[:, :], qs[p][m][:, :, :, k].rearrange("p u b -> p (u b)"), ks[p][m // 2][:, :],
                              start=False, stop=(m == len(QK_TERMS) - 1))
                last.then_inc(scores, 1)

            def turn(i, K):
                pe.wait_ge(prob_ready, i * STEPS + K + 1)
                if before(i, K - 2):
                    pe.wait_ge(turned_sb, i * STEPS + K - 1)
                for j in range(JT):
                    last = nc.tensor.transpose(turned_ps[K % 2][:, j * P:(j + 1) * P],
                                               prob[K % 2][:, j * P:(j + 1) * P], ident[:, :])
                last.then_inc(turned, 1)

            def mix(i, g):
                n = i * (STEPS // GRP) + g
                pe.wait_ge(turned_sb, (n + 1) * GRP)
                h, p = 2 * i + g // (NT // GRP), g // (NT // GRP) % 2
                if g % (NT // GRP) == 0:
                    pe.wait_ge(v_head, h + 1)
                if before(i, g - 2):
                    pe.wait_ge(masked_ready, 2 * (n - 1))
                for jj in range(JT // 2):
                    for half in range(2):
                        for bg in range(2):
                            c, j = 2 * bg + half, JT // 2 * half + jj
                            last = mm(mixed_ps[g % 2][32 * c:32 * c + 32, 0:MIXED],
                                      vh[:, p, j, BG * bg:BG * (bg + 1), :].rearrange("p b d -> p (b d)"),
                                      probT[g % 2][:, j, :].rearrange("p (u b) -> p u b", b=NB)[:, :, BG * bg:BG * (bg + 1)],
                                      start=(jj == 0), stop=(jj == JT // 2 - 1))
                last.then_inc(mixed, 1)

            def untangle(i, g):
                n = i * (STEPS // GRP) + g
                pe.wait_ge(masked_ready, 2 * (n + 1))
                if before(i, g - 1):
                    pe.wait_ge(part_ready, n)
                for t in range(GRP):
                    last = nc.tensor.transpose(
                        untangled_ps[:, t * P:(t + 1) * P],
                        masked[:, g % 2, t * U:(t + 1) * U, :].rearrange("p u b -> p (u b)"), ident[:, :])
                last.then_inc(untangled, 1)

            def rest(i, K):
                if K % GRP == 0 and before(i, K - 2 * GRP):
                    untangle(i, K // GRP - 2)
                if before(i, K - 2):
                    turn(i, K - 2)
                if K % GRP == 2 and before(i, K - 6):
                    mix(i, (K - 6) // GRP)

            def pair(i):
                for K in range(STEPS):
                    score(i, K)
                    rest(i, K)

            pair(0)
            with pe.Fori(1, HEADS // 2) as i:
                pair(i)
            last_pair = HEADS // 2
            untangle(last_pair, -2)
            turn(last_pair, -2)
            turn(last_pair, -1)
            mix(last_pair, -1)
            untangle(last_pair, -1)

        @block.scalar
        def _(act):
            def copy_turned(i, K):
                act.wait_ge(turned, i * STEPS + K + 1)
                if K % GRP == 0 and before(i, K - 2 * GRP):
                    act.wait_ge(mixed, i * (STEPS // GRP) + K // GRP - 1)
                nc.scalar.copy(probT[K // GRP % 2][:, :, K % GRP * P:(K % GRP + 1) * P],
                               turned_ps[K % 2][:, :].rearrange("p (j t) -> p j t", j=JT)).then_inc(turned_sb, 1)

            def pair(i):
                for K in range(STEPS):
                    p, k = divmod(K, NT)
                    act.wait_ge(top_ready, i * STEPS + K + 1)
                    if before(i, K - 2):
                        act.wait_ge(turned, i * STEPS + K - 1)
                    nc.scalar.activation(prob[K % 2][:, :], score_ps[K % RING][:, :], ACT.Exp, bias=ntop[:, k:k + 1],
                                         accum_out=rsum[:, p, k:k + 1]).then_inc(prob_ready, 1)
                    if before(i, K - 1):
                        copy_turned(i, K - 1)

            pair(0)
            with act.Fori(1, HEADS // 2) as i:
                pair(i)
            copy_turned(HEADS // 2, -1)

        @block.vector
        def _(dve):
            v = nc.vector
            for p in range(2):
                for t in qs[p]:
                    v.memset(t[:, :, :, :], 0.0).then_inc(zeroed[p], 1)
            v.tensor_reduce(own2[:, :], ident[:, :].rearrange("p (e d) -> p e d", d=HD), AX.X, ALU.add)\
             .then_inc(mask_ready, 1)
            dve.wait_ge(mask_ready, 1)
            v.tensor_reduce(own[:, :], own2[:, :].rearrange("p (c b) -> p b c", b=BG), AX.X, ALU.add)\
             .then_inc(mask_ready, 1)
            dve.wait_ge(mask_ready, 2)
            dve.wait_ge(mask_zeroed, 1)

            def pick(i, g):
                n = i * (STEPS // GRP) + g
                dve.wait_ge(mixed, n + 1)
                if before(i, g - 2):
                    dve.wait_ge(untangled, n - 1)
                for bg in range(2):
                    rows = slice(P // 2 * bg, P // 2 * (bg + 1))
                    v.tensor_tensor(masked[rows, g % 2, :, BG * bg:BG * (bg + 1)],
                                    mixed_ps[g % 2][rows, 0:MIXED].rearrange("p (u b) -> p u b", b=BG),
                                    own[rows, :].unsqueeze(1).to_broadcast([P // 2, GRP * U, BG]), ALU.mult)\
                     .then_inc(masked_ready, 1)

            def finish(i, g):
                n = i * (STEPS // GRP) + g
                p, q = g // (NT // GRP) % 2, g % 2
                tiles = slice(g % (NT // GRP) * GRP, (g % (NT // GRP) + 1) * GRP)
                h = 2 * i + g // (NT // GRP)
                dve.wait_ge(untangled, n + 1)
                v.tensor_reduce(part[:, q, :, :], untangled_ps[:, :].rearrange("p (k e d) -> p k d e", k=GRP, d=HD),
                                AX.X, ALU.add).then_inc(part_ready, 1)
                v.reciprocal(rsum[:, p, tiles], rsum[:, p, tiles]).then_inc(rinv_ready, 1)
                dve.wait_ge(part_ready, n + 1)
                dve.wait_ge(rinv_ready, n + 1)
                v.tensor_tensor(ctxt[:, tiles, bass.ds(h * HD, HD)], part[:, q, :, :],
                                rsum[:, p, tiles].unsqueeze(2).to_broadcast([P, GRP, HD]), ALU.mult)\
                 .then_inc(ctx_ready, 1)

            def pair(i):
                for K in range(STEPS):
                    p, k = divmod(K, NT)
                    dve.wait_ge(scores, i * STEPS + K + 1)
                    v.tensor_reduce(ntop[:, k:k + 1], score_ps[K % RING][:, :], AX.X, ALU.max, negate=True)\
                     .then_inc(top_ready, 1)
                    if K % GRP == 3 and before(i, K - 7):
                        pick(i, (K - 7) // GRP)
                    if K % GRP == 1 and before(i, K - 9):
                        finish(i, (K - 9) // GRP)

            pair(0)
            with dve.Fori(1, HEADS // 2) as i:
                pair(i)
            finish(HEADS // 2, -2)
            pick(HEADS // 2, -1)
            finish(HEADS // 2, -1)

def attention_output(nc, d, keep, ctxt):
    x, mod, ident, ones = keep["x"], keep["mod"], keep["ident"], keep["ones"]
    with ExitStack() as ctx:
        sb = lambda name, shape, dt=F32: ctx.enter_context(nc.sbuf_tensor(name, shape, dt))
        sem = lambda name: ctx.enter_context(nc.semaphore(name))
        pt = [ctx.enter_context(nc.psum_tensor(f"pt{i}", [P, 512], F32)) for i in range(2)]
        po = [ctx.enter_context(nc.psum_tensor(f"pp{i}", [P, 512], F32)) for i in range(2)]
        wo, bo = sb("wo1", [P, P]), sb("bo1", [1, P])
        cT = sb("ctxT", [P, 2, BLK])
        upd = sb("upd1", [P, 2, TPB, P])
        w_in, turned, cT_ready, out_ready, upd_ready, x_added = (
            sem("w_ino"), sem("turnedo"), sem("cT_ready"), sem("out_readyo"), sem("upd_readyo"), sem("x_addedo"))
        block = ctx.enter_context(nc.Block())

        @block.sync
        def _(sp):
            sp.dma_start(wo[:, :], d["woT"]).then_inc(w_in, 16)
            sp.dma_start(bo[:, :], d["bo"]).then_inc(w_in, 16)

        @block.scalar
        def _(act):
            for j in range(NBLK):
                act.wait_ge(turned, j + 1)
                if j >= 2:
                    act.wait_ge(out_ready, j - 1)
                nc.scalar.copy(cT[:, j % 2, :], pt[j % 2][:, :]).then_inc(cT_ready, 1)

        @block.tensor
        def _(pe):
            pe.wait_ge(w_in, 32)
            for j in range(NBLK + 1):
                if j < NBLK:
                    if j >= 2:
                        pe.wait_ge(cT_ready, j - 1)
                    for q in range(TPB):
                        last = nc.tensor.transpose(pt[j % 2][:, q * P:(q + 1) * P], ctxt[:, j * TPB + q, :], ident[:, :])
                    last.then_inc(turned, 1)
                if j >= 1:
                    i = j - 1
                    pe.wait_ge(cT_ready, i + 1)
                    if i >= 2:
                        pe.wait_ge(upd_ready, i - 1)
                    for q in range(TPB):
                        to = po[i % 2][:, q * P:(q + 1) * P]
                        nc.tensor.matmul(to, cT[:, i % 2, q * P:(q + 1) * P], wo[:, :], start=True, stop=False)
                        last = nc.tensor.matmul(to, ones[0:1, :], bo[:, :], start=False, stop=True)
                    last.then_inc(out_ready, 1)

        @block.vector
        def _(dve):
            v = nc.vector
            for j in range(NBLK):
                dve.wait_ge(out_ready, j + 1)
                if j >= 2:
                    dve.wait_ge(x_added, j - 1)
                v.tensor_tensor(upd[:, j % 2, :, :], po[j % 2][:, :].rearrange("p (q e) -> p q e", q=TPB),
                                mod[:, 1, 2 * P:3 * P].unsqueeze(1).to_broadcast([P, TPB, P]), ALU.mult)\
                 .then_inc(upd_ready, 1)
                dve.wait_ge(upd_ready, j + 1)
                xs = x[:, j * TPB:(j + 1) * TPB, :]
                v.tensor_tensor(xs, xs, upd[:, j % 2, :, :], ALU.add).then_inc(x_added, 1)
            dve.wait_ge(x_added, NBLK)


def experts1(nc, d, keep, out):
    x, mod, ident = keep["x"], keep["mod"], keep["ident"]
    NALL = NE1 + 1
    WCOLS = 5 * P
    with ExitStack() as ctx:
        sb = lambda name, shape, dt=F32: ctx.enter_context(nc.sbuf_tensor(name, shape, dt))
        sem = lambda name: ctx.enter_context(nc.semaphore(name))
        pm = [ctx.enter_context(nc.psum_tensor(f"pz{i}", [P, 512], F32)) for i in range(8)]
        hT = sb("hTz", [P, TOK])
        W = [sb(f"w1_{p}", [P, WCOLS]) for p in range(2)]
        B = [sb(f"b1_{p}", [P, 4]) for p in range(2)]
        gw = sb("gw1", [P, NE1])
        gb = sb("gb1", [P, NE1])
        b2 = sb("b2", [NALL, P])
        rank = sb("rank1", [P, NE1])
        ranki = sb("ranki1", [P, NE1], mybir.dt.int32)
        probs = sb("probs1", [P, NT, NE1])
        keys = sb("keys1", [P, NT, NE1])
        hot = sb("hot1", [P, NT, NE1])
        top = sb("top1", [P, NT])
        cw = sb("cw1", [P, NT, NALL])
        cwe = sb("cwe", [P, 2, NT])
        cwT = sb("cwT1", [NALL, TOK])
        acc = sb("acc1", [P, NT, P])
        g1, l1 = sb("g1", [P, 2, BLK]), sb("l1", [P, 2, BLK])
        gg, ll = sb("gg", [P, 2, BLK]), sb("ll", [P, 2, BLK])
        th, a = sb("th", [P, 2, BLK]), sb("a", [P, 2, BLK])
        w_in, v_chain, ranks = sem("w_inz"), sem("v_chainz"), sem("ranks1")
        logits_ready, exp_asked, exp_done = sem("logits_ready1"), sem("exp_asked1"), sem("exp_done1")
        cw_ready, cwT_ps, cwT_ready = sem("cw_ready1"), sem("cwT_ps1"), sem("cwT_ready1")
        seed_ps, seeded = sem("seed_ps"), sem("seeded1")
        we_in, w2_half = [sem("we_in0"), sem("we_in1")], sem("w2_half")
        gate_ps, lin_ps, first_g, first_l = sem("gate_ps"), sem("lin_ps"), sem("first_g"), sem("first_l")
        pool_steps = sem("pool_steps")
        gg_raw, gg_ready, th_ready = sem("gg_raw"), sem("gg_ready"), sem("th_ready")
        ll_raw, ll_ready, gl_ready, a_ready = sem("ll_raw"), sem("ll_ready"), sem("gl_ready"), sem("a_ready")
        x_final, stored = sem("x_final"), sem("stored")
        y_ready, y_summed, cwe_ready = sem("y_ready1"), sem("y_summed"), sem("cwe_ready")
        norm = Normed(nc, sb, sem, keep, 1, 1, hT, pm[0:2], "z")
        G1, L1, G3, L3, Y = pm[0], pm[1], pm[2:4], pm[4:6], pm[6:8]
        block = ctx.enter_context(nc.Block())

        def experts(eng, body):
            body(0, 0)
            body(1, 1)
            with eng.Fori(1, NE1 // 2) as i:
                body(2 * i, 0)
                body(2 * i + 1, 1)
            body(NE1, 0)

        def back(e, p, j, steps):
            if j >= steps:
                return e * NBLK + j - steps, p, j - steps
            if isinstance(e, int) and e == 0:
                return None
            return e * NBLK + j - steps, 1 - p, j - steps + NBLK

        def weights_in(e, p):
            return 32 * (e // 2 + 1) if isinstance(e, int) else 16 * e + 32 - 16 * p

        @block.sync
        def _(sp):
            for dst, src in ((gw[:, :], d["gw1"]), (gb[:, :], d["gb1"].to_broadcast([P, NE1])),
                             (b2[:, :], d["b2"])):
                sp.dma_start(dst, src).then_inc(w_in, 16)

            def load(e, p):
                w, b = ((d["ew1"][bass.ds(e, 1), :, :], d["eb1"][bass.ds(e, 1), :, :]) if not isinstance(e, int)
                        else (d["ew1"][e:e + 1, :, :], d["eb1"][e:e + 1, :, :]))
                sp.dma_start(W[p][:, :], w.rearrange("o p n -> p (o n)")).then_inc(we_in[p], 16)
                sp.dma_start(B[p][:, :], b.rearrange("o p n -> p (o n)")).then_inc(we_in[p], 16)

            load(0, 0)
            load(1, 1)
            with sp.Fori(1, NE1 // 2) as i:
                for p in range(2):
                    sp.wait_ge(y_ready, (2 * i - 1 + p) * NBLK)
                    load(2 * i + p, p)
            sp.wait_ge(y_ready, (NE1 - 1) * NBLK)
            load(NE1, 0)
            for j in range(NBLK):
                ts = slice(j * TPB, (j + 1) * TPB)
                sp.wait_ge(x_final, j + 1)
                sp.dma_start(out[:, ts, :], x[:, ts, :]).then_inc(stored, 16)
            sp.wait_ge(stored, 16 * NBLK)

        @block.gpsimd
        def _(pool):
            norm.gpsimd(pool)
            nc.gpsimd.iota(ranki[:, :], pattern=[[-1, NE1]], base=NE1, channel_multiplier=0).then_inc(ranks, 1)
            pool.wait_ge(ranks, 1)
            nc.gpsimd.tensor_copy(rank[:, :], ranki[:, :]).then_inc(ranks, 1)

            def body(e, p):
                for j in range(NBLK):
                    n, q = e * NBLK + j, j % 2
                    pool.wait_ge(gg_raw, n + 1)
                    pool.sem_inc(pool_steps, 1)
                    nc.gpsimd.tensor_scalar(gg[:, q, :], gg[:, q, :], LIMIT, LOWEST, ALU.min, ALU.max)\
                      .then_inc(gg_ready, 1)
                    pool.wait_ge(ll_raw, n + 1)
                    pool.sem_inc(pool_steps, 1)
                    nc.gpsimd.tensor_scalar(ll[:, q, :], ll[:, q, :], LIMIT, -LIMIT, ALU.min, ALU.max)\
                      .then_inc(ll_ready, 1)

            experts(pool, body)

        @block.scalar
        def _(act):
            norm.scalar(act)
            act.wait_ge(exp_asked, 1)
            nc.scalar.activation(probs[:, :, :], probs[:, :, :], ACT.Exp).then_inc(exp_done, 1)
            for j in range(NBLK):
                act.wait_ge(cwT_ps, j + 1)
                nc.scalar.copy(cwT[:, j * BLK:(j + 1) * BLK], pm[2 + j % 2][0:NALL, :]).then_inc(cwT_ready, 1)
            for j in range(NBLK):
                act.wait_ge(seed_ps, j + 1)
                nc.scalar.copy(acc[:, j * TPB:(j + 1) * TPB, :].rearrange("p k e -> p (k e)"),
                               pm[4 + j % 2][:, :]).then_inc(seeded, 1)

            def tanh(n, p, j):
                act.wait_ge(gg_ready, n + 1)
                nc.scalar.activation(th[:, j % 2, :], gg[:, j % 2, :], ACT.Tanh, scale=ALPHA / 2)\
                  .then_inc(th_ready, 1)

            def body(e, p):
                act.wait_ge(we_in[p], weights_in(e, p))
                for j in range(NBLK):
                    n, q = e * NBLK + j, j % 2
                    act.wait_ge(gate_ps, n + 1)
                    nc.scalar.activation(g1[:, q, :], G1[:, :], ACT.Identity, bias=B[p][:, 0:1])\
                      .then_inc(first_g, 1)
                    if back(e, p, j, 1):
                        tanh(*back(e, p, j, 1))
                    act.wait_ge(lin_ps, n + 1)
                    nc.scalar.activation(l1[:, q, :], L1[:, :], ACT.Identity, bias=B[p][:, 1:2])\
                      .then_inc(first_l, 1)

            experts(act, body)
            tanh(*back(NE1, 0, NBLK, 1))

        @block.vector
        def _(dve):
            v = nc.vector
            chain = Chain(dve, v_chain)
            norm.vector(dve, chain)
            dve.wait_ge(w_in, 16 * 3)
            dve.wait_ge(ranks, 2)
            dve.wait_ge(logits_ready, 1)
            softmax_probs(dve, nc, chain, probs[:, :, :], pm[4][:, 0:NT * NE1].rearrange("p (k e) -> p k e", e=NE1),
                          None, top[:, :], NE1, exp_asked, exp_done)
            chain(v.tensor_tensor(keys[:, :, :], probs[:, :, :], gb[:, :].unsqueeze(1).to_broadcast([P, NT, NE1]),
                                  ALU.add))
            first_of_max(nc, chain, keys[:, :, :], rank[:, :], hot[:, :, :], top[:, :], NE1)
            chain(v.tensor_tensor(cw[:, :, 0:NE1], hot[:, :, :], probs[:, :, :], ALU.mult))
            chain(v.scalar_tensor_tensor(keys[:, :, :], hot[:, :, :], -3e38, keys[:, :, :], ALU.mult, ALU.add))
            first_of_max(nc, chain, keys[:, :, :], rank[:, :], hot[:, :, :], top[:, :], NE1)
            chain(v.tensor_tensor(hot[:, :, :], hot[:, :, :], probs[:, :, :], ALU.mult))
            chain(v.tensor_tensor(cw[:, :, 0:NE1], cw[:, :, 0:NE1], hot[:, :, :], ALU.add))
            chain(v.memset(cw[:, :, NE1:NALL], 1.0))
            v.sem_inc(cw_ready, 1)
            dve.wait_ge(seeded, NBLK)

            def add_up(n, p, j):
                dve.wait_ge(y_ready, n + 1)
                for t in range(TPB):
                    k = j * TPB + t
                    last = v.scalar_tensor_tensor(acc[:, k, :], Y[j % 2][:, t * P:(t + 1) * P],
                                                  cwe[:, p, k:k + 1], acc[:, k, :], ALU.mult, ALU.add)
                last.then_inc(y_summed, 1)

            def finish(j):
                ts = slice(j * TPB, (j + 1) * TPB)
                dve.wait_ge(y_summed, NE1 * NBLK + j + 1)
                chain(v.tensor_tensor(acc[:, ts, :], acc[:, ts, :],
                                      mod[:, 1, 5 * P:6 * P].unsqueeze(1).to_broadcast([P, TPB, P]), ALU.mult))
                v.tensor_tensor(x[:, ts, :], x[:, ts, :], acc[:, ts, :], ALU.add).then_inc(x_final, 1)

            def join(n, p, j):
                q = j % 2
                dve.wait_ge(gg_ready, n + 1)
                dve.wait_ge(ll_ready, n + 1)
                v.scalar_tensor_tensor(ll[:, q, :], ll[:, q, :], 1.0, gg[:, q, :], ALU.add, ALU.mult)\
                 .then_inc(gl_ready, 1)
                dve.wait_ge(gl_ready, n + 1)
                dve.wait_ge(th_ready, n + 1)
                v.scalar_tensor_tensor(a[:, q, :], th[:, q, :], 1.0, ll[:, q, :], ALU.add, ALU.mult)\
                 .then_inc(a_ready, 1)

            def body(e, p):
                src = cw[:, :, bass.ds(e, 1)] if not isinstance(e, int) else cw[:, :, e:e + 1]
                v.tensor_copy(cwe[:, p, :].unsqueeze(2), src).then_inc(cwe_ready, 1)
                dve.wait_ge(cwe_ready, e + 1)
                dve.wait_ge(we_in[p], weights_in(e, p))
                v.tensor_scalar(W[p][:, 4 * P:5 * P], W[p][:, 4 * P:5 * P], 0.5, None, ALU.mult).then_inc(w2_half, 1)
                dve.wait_ge(w2_half, e + 1)
                for j in range(NBLK):
                    n, q = e * NBLK + j, j % 2
                    if back(e, p, j, 2):
                        dve.wait_ge(a_ready, n - 1)
                    dve.wait_ge(first_g, n + 1)
                    v.scalar_tensor_tensor(gg[:, q, :], G3[q][:, :], B[p][:, 2:3], g1[:, q, :],
                                           ALU.add, ALU.mult).then_inc(gg_raw, 1)
                    dve.wait_ge(first_l, n + 1)
                    v.scalar_tensor_tensor(ll[:, q, :], L3[q][:, :], B[p][:, 3:4], l1[:, q, :],
                                           ALU.add, ALU.mult).then_inc(ll_raw, 1)
                    if back(e, p, j, 1):
                        join(*back(e, p, j, 1))
                    if back(e, p, j, 2):
                        add_up(*back(e, p, j, 2))
                    if isinstance(e, int) and e == NE1 and j >= 2:
                        finish(j - 2)

            experts(dve, body)
            join(*back(NE1, 0, NBLK, 1))
            for j in range(NBLK - 2, NBLK):
                add_up(*back(NE1, 0, NBLK, NBLK - j))
                finish(j)

        @block.tensor
        def _(pe):
            mm = nc.tensor.matmul
            norm.tensor(pe)
            pe.wait_ge(w_in, 16 * 3)
            for k in range(NT):
                if k % TPB == 0:
                    pe.wait_ge(norm.hT_ready, k // TPB + 1)
                last = mm(pm[4][:, k * NE1:(k + 1) * NE1], hT[:, k * P:(k + 1) * P], gw[:, :], start=True, stop=True)
            last.then_inc(logits_ready, 1)
            pe.wait_ge(cw_ready, 1)
            for j in range(NBLK):
                if j >= 2:
                    pe.wait_ge(cwT_ready, j - 1)
                for t in range(TPB):
                    last = nc.tensor.transpose(pm[2 + j % 2][0:NALL, t * P:(t + 1) * P], cw[:, j * TPB + t, :],
                                               ident[:, :])
                last.then_inc(cwT_ps, 1)
            for j in range(NBLK):
                pe.wait_ge(cwT_ready, j + 1)
                if j >= 2:
                    pe.wait_ge(seeded, j - 1)
                for t in range(TPB):
                    last = mm(pm[4 + j % 2][:, t * P:(t + 1) * P], cwT[:, (j * TPB + t) * P:(j * TPB + t + 1) * P],
                              b2[:, :], start=True, stop=True)
                last.then_inc(seed_ps, 1)
            pe.wait_ge(seeded, NBLK)

            def second(n, p, j):
                pe.wait_ge(a_ready, n + 1)
                if not (isinstance(n, int) and n < 2):
                    pe.wait_ge(y_summed, n - 1)
                for t in range(TPB):
                    last = mm(Y[j % 2][:, t * P:(t + 1) * P], a[:, j % 2, t * P:(t + 1) * P],
                              W[p][:, 4 * P:5 * P], start=True, stop=True)
                last.then_inc(y_ready, 1)

            def body(e, p):
                pe.wait_ge(we_in[p], weights_in(e, p))
                for j in range(NBLK):
                    n, q = e * NBLK + j, j % 2
                    src = hT[:, j * BLK:(j + 1) * BLK]
                    first = isinstance(e, int) and e == 0
                    if not (first and j == 0):
                        pe.wait_ge(first_g, n)
                    mm(G1[:, :], W[p][:, 0:P], src, start=True, stop=True)
                    if not (first and j < 2):
                        pe.wait_ge(gg_raw, n - 1)
                    mm(G3[q][:, :], W[p][:, 2 * P:3 * P], src, start=True, stop=True).then_inc(gate_ps, 1)
                    if not (first and j == 0):
                        pe.wait_ge(first_l, n)
                    mm(L1[:, :], W[p][:, P:2 * P], src, start=True, stop=True)
                    if not (first and j < 2):
                        pe.wait_ge(ll_raw, n - 1)
                    mm(L3[q][:, :], W[p][:, 3 * P:4 * P], src, start=True, stop=True).then_inc(lin_ps, 1)
                    if back(e, p, j, 2):
                        second(*back(e, p, j, 2))

            experts(pe, body)
            second(*back(NE1, 0, NBLK, 2))
            second(*back(NE1, 0, NBLK, 1))


def program(nc, d, out):
    with ExitStack() as ctx:
        sb = lambda name, shape, dt=F32: ctx.enter_context(nc.sbuf_tensor(name, shape, dt))
        keep = {"x": sb("x", [P, NT, P]), "mod": sb("mod", [P, 2, MODS * P]),
                "ident": sb("ident", [P, P]), "ones": sb("ones", [P, P])}
        with ExitStack() as inner:
            sb1 = lambda name, shape, dt=F32: inner.enter_context(nc.sbuf_tensor(name, shape, dt))
            scan = {"A": sb1("A", [P, NS * NB]), "Bm": sb1("Bm", [P, NS]), "Dv": sb1("Dv", [P, 1]),
                    "xp": sb1("xp", [P, NC * P]), "gate": sb1("gate2", [P, NC * P]),
                    "hist": sb1("hist", [P, 2, U, NS * NB]), "diagC": sb1("diagC", [P, NS + 1, P]),
                    "woT": sb1("woT", [P, P]), "bo": sb1("bo", [1, P])}
            prologue(nc, d, keep, scan)
            scan_phase(nc, d, keep, scan)
        experts0(nc, d, keep)
        scratch = {n: nc.dram_tensor(f"parts_{n}", shape, BF16, kind="Internal").ap()
                   for n, shape in (("q", (PARTS, P, TOK)), ("k", (HEADS, len(KEY_SLOTS), HD, TOK)),
                                    ("t", (HEADS, len(TABLE_SLOTS), HD, TROW)))}
        with ExitStack() as inner:
            vals = inner.enter_context(nc.sbuf_tensor("vals", [P, JT * NB, P], F32))
            attention_inputs(nc, d, keep, vals, scratch)
            ctxt = inner.enter_context(nc.sbuf_tensor("ctxt", [P, NT, P], F32))
            attention(nc, d, keep, vals, scratch, ctxt)
            attention_output(nc, d, keep, ctxt)
        experts1(nc, d, keep, out)


def layouts(inputs, np):
    g = lambda n: np.asarray(inputs[n])
    a = {}
    a["x"] = g("L0_attn_x").reshape(NB, NC, U, 2, P).transpose(2, 0, 1, 3, 4).reshape(P, NT, P)
    a["cT"] = np.stack([g("L0_c").T, g("L1_c").T], 1)
    a["wmod"] = np.stack([g("L0_wmod"), g("L1_wmod")], 1)
    a["w_inT"] = g("L0_attn_w_in").T
    a["b_in"] = g("L0_attn_b_in").reshape(2, P).T
    a["g_norm"] = g("L0_attn_g_norm").reshape(P, 1)
    a["A"], a["Bm"], a["Cm"] = g("L0_attn_A"), g("L0_attn_Bm"), g("L0_attn_Cm")
    a["Dv"] = g("L0_attn_Dv").reshape(P, 1)
    a["w_outT"] = g("L0_attn_w_out").T
    a["b_out"] = g("L0_attn_b_out").reshape(1, P)
    a["gw0"] = g("L0_ffn_gate_w").T
    a["gb0"] = g("L0_ffn_gate_b").reshape(1, NX0)
    a["ew0"] = g("L0_ffn_expert_w").transpose(1, 0, 2).reshape(P, NE0 * P)
    a["eb0"] = g("L0_ffn_expert_b")
    a["table"] = g("L1_attn_rpe_table")[:, TLEN - 1::-1, :].transpose(0, 2, 1).reshape(P, TLEN)
    for n in "qkvo":
        a[f"w{n}T"] = g(f"L1_attn_w{n}").T
    a["bq"], a["bk"] = g("L1_attn_bq").reshape(P, 1), g("L1_attn_bk").reshape(P, 1)
    a["bv"], a["bo"] = g("L1_attn_bv").reshape(1, P), g("L1_attn_bo").reshape(1, P)
    a["gw1"] = g("L1_ffn_gate_w").T
    a["gb1"] = g("L1_ffn_gate_b").reshape(1, NE1)
    w = [np.concatenate([g(f"L1_ffn_{n}"), g(f"L1_ffn_s{n}")[None]]) for n in ("w1", "w3", "w2")]
    b = [np.concatenate([g(f"L1_ffn_{n}"), g(f"L1_ffn_s{n}")[None]]) for n in ("b1", "b3", "b2")]
    a["ew1"] = np.concatenate([m.transpose(0, 2, 1) for m in (w[0][:, ::2], w[0][:, 1::2], w[1][:, ::2],
                                                            w[1][:, 1::2], w[2])], axis=2)
    a["eb1"] = np.stack([b[0][:, ::2], b[0][:, 1::2], b[1][:, ::2], b[1][:, 1::2]], axis=2)
    a["b2"] = b[2]
    return {k: np.ascontiguousarray(v) for k, v in a.items()}


def kernel(**inputs):
    import numpy as np
    import concourse.bacc as bacc
    from concourse.bass_utils import run_bass_kernel_spmd

    arrays = layouts(inputs, np)
    nc = bacc.Bacc("TRN2", target_bir_lowering=False, num_devices=1)
    d = {k: nc.dram_tensor(f"in_{k}", v.shape, F32, kind="ExternalInput").ap() for k, v in arrays.items()}
    out = nc.dram_tensor("out_x", (P, NT, P), F32, kind="ExternalOutput").ap()
    program(nc, d, out)
    r = run_bass_kernel_spmd(nc, [{f"in_{k}": v for k, v in arrays.items()}], core_ids=[0])
    y = r.results[0]["out_x"]
    return y.reshape(U, NB, NC, 2, P).transpose(1, 2, 0, 3, 4).reshape(NB, SEQ, P)
```
